# Optimizing a Trainium2 kernel written in Bass

```python
import numpy as np
import jax
import jax.numpy as jnp

def _softmax(x, axis=-1):
    return jax.nn.softmax(x, axis=axis)

def _gelu(x):
    return jax.nn.gelu(x, approximate=True)

def _silu(x):
    return jax.nn.silu(x)

def _sigmoid(x):
    return jax.nn.sigmoid(x)

def _layernorm(x, axis=-1, eps=1e-05):
    m = jnp.mean(x, axis=axis, keepdims=True)
    v = jnp.var(x, axis=axis, keepdims=True)
    return (x - m) / jnp.sqrt(v + eps)

def _scatter_add(tgt, idx, src, axis=0):
    return tgt.at[idx].add(src)

def _segment_sum(src, seg, n):
    return jax.ops.segment_sum(src, seg, n)
kernel_name = 'mk_recurrent_d2_jaxref_r8_24ec3d'

def setup_inputs(seed: int=0):
    np.random.seed(seed)
    _w = jnp.asarray

    def _L0_attn_setup():
        import jax, jax.numpy as jnp
        import numpy as np
        B, T, C = (4, 128, 128)
        HEAD_SIZE = 64
        H = C // HEAD_SIZE
        N_LAYER, LAYER_ID = (24, 12)
        D_MIX_LORA, D_DECAY_LORA = (32, 64)
        HEAD_SIZE_DIVISOR = 8
        LN_EPS = 1e-05 * HEAD_SIZE_DIVISOR ** 2

        def _wkv6(r, k, v, w, u):

            def step(S, inp):
                r_t, k_t, v_t, w_t = inp
                y = jnp.einsum('bhj,bhji->bhi', r_t, S) + jnp.sum(r_t * u * k_t, axis=-1, keepdims=True) * v_t
                decay = jnp.exp(-jnp.exp(w_t))
                S = decay[..., None] * S + k_t[..., None] * v_t[..., None, :]
                return (S, y)
            to_t = lambda a: jnp.transpose(a, (1, 0, 2, 3))
            S0 = jnp.zeros(r.shape[:1] + (r.shape[2], r.shape[3], r.shape[3]), r.dtype)
            _, ys = jax.lax.scan(step, S0, (to_t(r), to_t(k), to_t(v), to_t(w)))
            return jnp.transpose(ys, (1, 0, 2, 3))
        key = jax.random.key(seed)
        ks = jax.random.split(key, 16)
        x = jax.random.normal(ks[0], (B, T, C), jnp.float32)
        r01 = LAYER_ID / (N_LAYER - 1)
        r10 = 1.0 - LAYER_ID / N_LAYER
        ddd = np.arange(C, dtype=np.float64) / C
        time_maa_x = jnp.asarray((1.0 - ddd ** r10).astype(np.float32))
        time_maa_w = jnp.asarray((1.0 - ddd ** r10).astype(np.float32))
        time_maa_k = jnp.asarray((1.0 - ddd ** r10).astype(np.float32))
        time_maa_v = jnp.asarray((1.0 - (ddd ** r10 + 0.3 * r01)).astype(np.float32))
        time_maa_r = jnp.asarray((1.0 - ddd ** (0.5 * r10)).astype(np.float32))
        time_maa_g = jnp.asarray((1.0 - ddd ** (0.5 * r10)).astype(np.float32))
        n = np.arange(C, dtype=np.float64)
        time_decay = jnp.asarray((-6.0 + 5.0 * (n / (C - 1)) ** (0.7 + 1.3 * r01)).astype(np.float32))
        zigzag = ((n + 1) % 3 - 1) * 0.1
        time_faaaa = jnp.asarray((r01 * (1.0 - n / (C - 1)) + zigzag).astype(np.float32)).reshape(H, HEAD_SIZE)
        u = lambda k, shp: jax.random.uniform(k, shp, jnp.float32, -0.01, 0.01)
        time_maa_w1 = u(ks[1], (C, D_MIX_LORA * 5))
        time_maa_w2 = u(ks[2], (5, D_MIX_LORA, C))
        time_decay_w1 = u(ks[3], (C, D_DECAY_LORA))
        time_decay_w2 = u(ks[4], (D_DECAY_LORA, C))
        s = 1.0 / np.sqrt(C)
        Wr = jax.random.normal(ks[5], (C, C), jnp.float32) * s
        Wk = jax.random.normal(ks[6], (C, C), jnp.float32) * s
        Wv = jax.random.normal(ks[7], (C, C), jnp.float32) * s
        Wg = jax.random.normal(ks[8], (C, C), jnp.float32) * s
        Wo = jax.random.normal(ks[9], (C, C), jnp.float32) * s
        ln_w = jnp.ones((C,), jnp.float32)
        ln_b = jnp.zeros((C,), jnp.float32)
        return dict(x=x, time_maa_x=time_maa_x, time_maa_w=time_maa_w, time_maa_k=time_maa_k, time_maa_v=time_maa_v, time_maa_r=time_maa_r, time_maa_g=time_maa_g, time_maa_w1=time_maa_w1, time_maa_w2=time_maa_w2, time_decay=time_decay, time_decay_w1=time_decay_w1, time_decay_w2=time_decay_w2, time_faaaa=time_faaaa, Wr=Wr, Wk=Wk, Wv=Wv, Wg=Wg, Wo=Wo, ln_w=ln_w, ln_b=ln_b)
    _L0_attn_in = _L0_attn_setup()

    def _L0_ffn_setup():
        import jax, jax.numpy as jnp
        import numpy as np
        B, S, D = (4, 128, 128)
        E, K = (8, 2)
        H = 2 * D
        key = jax.random.key(seed)
        ks = jax.random.split(key, 5)
        x = jax.random.normal(ks[0], (B, S, D), dtype=jnp.float32)
        Wg = jax.random.normal(ks[1], (E, D), dtype=jnp.float32) * 0.02
        W1 = jax.random.normal(ks[2], (E, H, D), dtype=jnp.float32) * 0.02
        W2 = jax.random.normal(ks[3], (E, H, D), dtype=jnp.float32) * 0.02
        W3 = jax.random.normal(ks[4], (E, D, H), dtype=jnp.float32) * 0.02
        return {'x': x, 'Wg': Wg, 'W1': W1, 'W2': W2, 'W3': W3}
    _L0_ffn_in = _L0_ffn_setup()

    def _L1_attn_setup():
        import jax, jax.numpy as jnp
        import numpy as np
        N_HEADS = 16
        INPUT_DIM = 128
        EMBED_DIM = 128
        KEY_DIM = EMBED_DIM // N_HEADS
        BATCH = 4
        SEQ = 256

        def _uniform(key, shape, bound):
            return jax.random.uniform(key, shape, jnp.float32, -bound, bound)
        key = jax.random.key(seed)
        kq, k1, k2, k3, k4 = jax.random.split(key, 5)
        stdv_k = 1.0 / np.sqrt(KEY_DIM)
        stdv_e = 1.0 / np.sqrt(EMBED_DIM)
        return {'q': jax.random.normal(kq, (BATCH, SEQ, INPUT_DIM), jnp.float32), 'W_query': _uniform(k1, (N_HEADS, INPUT_DIM, KEY_DIM), stdv_k), 'W_key': _uniform(k2, (N_HEADS, INPUT_DIM, KEY_DIM), stdv_k), 'W_val': _uniform(k3, (N_HEADS, INPUT_DIM, KEY_DIM), stdv_k), 'W_out': _uniform(k4, (N_HEADS, KEY_DIM, EMBED_DIM), stdv_e)}
    _L1_attn_in = _L1_attn_setup()

    def _L1_ffn_setup():
        import jax, jax.numpy as jnp
        import numpy as np
        TOP_K = 2
        E = 8
        D = 128
        F = 256
        B, S = (2, 128)
        key = jax.random.key(seed)
        ks = jax.random.split(key, 8)
        sc = 0.02
        return {'x_bsD': jax.random.normal(ks[0], (B, S, D), dtype=jnp.float32), 'router_DE': jax.random.normal(ks[1], (D, E), dtype=jnp.float32) * sc, 'w_in_shared_FD': jax.random.normal(ks[2], (F, D), dtype=jnp.float32) * sc, 'w_out_shared_DF': jax.random.normal(ks[3], (D, F), dtype=jnp.float32) * sc, 'w_swiglu_FD': jax.random.normal(ks[4], (F, D), dtype=jnp.float32) * sc, 'w_in_eDF': jax.random.normal(ks[5], (E, D, F), dtype=jnp.float32) * sc, 'w_swiglu_eDF': jax.random.normal(ks[6], (E, D, F), dtype=jnp.float32) * sc, 'w_out_eFD': jax.random.normal(ks[7], (E, F, D), dtype=jnp.float32) * sc}
    _L1_ffn_in = _L1_ffn_setup()
    _d = {'L0_attn_x': _L0_attn_in['x'], 'L0_attn_time_maa_x': _L0_attn_in['time_maa_x'], 'L0_attn_time_maa_w': _L0_attn_in['time_maa_w'], 'L0_attn_time_maa_k': _L0_attn_in['time_maa_k'], 'L0_attn_time_maa_v': _L0_attn_in['time_maa_v'], 'L0_attn_time_maa_r': _L0_attn_in['time_maa_r'], 'L0_attn_time_maa_g': _L0_attn_in['time_maa_g'], 'L0_attn_time_maa_w1': _L0_attn_in['time_maa_w1'], 'L0_attn_time_maa_w2': _L0_attn_in['time_maa_w2'], 'L0_attn_time_decay': _L0_attn_in['time_decay'], 'L0_attn_time_decay_w1': _L0_attn_in['time_decay_w1'], 'L0_attn_time_decay_w2': _L0_attn_in['time_decay_w2'], 'L0_attn_time_faaaa': _L0_attn_in['time_faaaa'], 'L0_attn_Wr': _L0_attn_in['Wr'], 'L0_attn_Wk': _L0_attn_in['Wk'], 'L0_attn_Wv': _L0_attn_in['Wv'], 'L0_attn_Wg': _L0_attn_in['Wg'], 'L0_attn_Wo': _L0_attn_in['Wo'], 'L0_attn_ln_w': _L0_attn_in['ln_w'], 'L0_attn_ln_b': _L0_attn_in['ln_b'], 'L0_ffn_Wg': _L0_ffn_in['Wg'], 'L0_ffn_W1': _L0_ffn_in['W1'], 'L0_ffn_W2': _L0_ffn_in['W2'], 'L0_ffn_W3': _L0_ffn_in['W3'], 'L1_attn_W_query': _L1_attn_in['W_query'], 'L1_attn_W_key': _L1_attn_in['W_key'], 'L1_attn_W_val': _L1_attn_in['W_val'], 'L1_attn_W_out': _L1_attn_in['W_out'], 'L1_ffn_router_DE': _L1_ffn_in['router_DE'], 'L1_ffn_w_in_shared_FD': _L1_ffn_in['w_in_shared_FD'], 'L1_ffn_w_out_shared_DF': _L1_ffn_in['w_out_shared_DF'], 'L1_ffn_w_swiglu_FD': _L1_ffn_in['w_swiglu_FD'], 'L1_ffn_w_in_eDF': _L1_ffn_in['w_in_eDF'], 'L1_ffn_w_swiglu_eDF': _L1_ffn_in['w_swiglu_eDF'], 'L1_ffn_w_out_eFD': _L1_ffn_in['w_out_eFD']}
    _x0 = _d['L0_attn_x']
    _d['L0_attn_x'] = jax.random.normal(jax.random.fold_in(jax.random.key(seed), 1), (16, 512, 128), dtype=_x0.dtype)
    del _x0
    return _d

def reference(L0_attn_x, L0_attn_time_maa_x, L0_attn_time_maa_w, L0_attn_time_maa_k, L0_attn_time_maa_v, L0_attn_time_maa_r, L0_attn_time_maa_g, L0_attn_time_maa_w1, L0_attn_time_maa_w2, L0_attn_time_decay, L0_attn_time_decay_w1, L0_attn_time_decay_w2, L0_attn_time_faaaa, L0_attn_Wr, L0_attn_Wk, L0_attn_Wv, L0_attn_Wg, L0_attn_Wo, L0_attn_ln_w, L0_attn_ln_b, L0_ffn_Wg, L0_ffn_W1, L0_ffn_W2, L0_ffn_W3, L1_attn_W_query, L1_attn_W_key, L1_attn_W_val, L1_attn_W_out, L1_ffn_router_DE, L1_ffn_w_in_shared_FD, L1_ffn_w_out_shared_DF, L1_ffn_w_swiglu_FD, L1_ffn_w_in_eDF, L1_ffn_w_swiglu_eDF, L1_ffn_w_out_eFD):

    def _L0_attn_ref(x, time_maa_x, time_maa_w, time_maa_k, time_maa_v, time_maa_r, time_maa_g, time_maa_w1, time_maa_w2, time_decay, time_decay_w1, time_decay_w2, time_faaaa, Wr, Wk, Wv, Wg, Wo, ln_w, ln_b):
        import jax, jax.numpy as jnp
        import numpy as np
        B, T, C = (4, 128, 128)
        HEAD_SIZE = 64
        H = C // HEAD_SIZE
        N_LAYER, LAYER_ID = (24, 12)
        D_MIX_LORA, D_DECAY_LORA = (32, 64)
        HEAD_SIZE_DIVISOR = 8
        LN_EPS = 1e-05 * HEAD_SIZE_DIVISOR ** 2

        def _wkv6(r, k, v, w, u):

            def step(S, inp):
                r_t, k_t, v_t, w_t = inp
                y = jnp.einsum('bhj,bhji->bhi', r_t, S) + jnp.sum(r_t * u * k_t, axis=-1, keepdims=True) * v_t
                decay = jnp.exp(-jnp.exp(w_t))
                S = decay[..., None] * S + k_t[..., None] * v_t[..., None, :]
                return (S, y)
            to_t = lambda a: jnp.transpose(a, (1, 0, 2, 3))
            S0 = jnp.zeros(r.shape[:1] + (r.shape[2], r.shape[3], r.shape[3]), r.dtype)
            _, ys = jax.lax.scan(step, S0, (to_t(r), to_t(k), to_t(v), to_t(w)))
            return jnp.transpose(ys, (1, 0, 2, 3))
        b, t, c = x.shape
        h, n = (H, HEAD_SIZE)
        xx = jnp.concatenate([jnp.zeros_like(x[:, :1]), x[:, :-1]], axis=1) - x
        xxx = x + xx * time_maa_x
        mix = jnp.tanh(xxx @ time_maa_w1).reshape(b, t, 5, D_MIX_LORA)
        m = jnp.einsum('btsd,sdc->sbtc', mix, time_maa_w2)
        xw = x + xx * (time_maa_w + m[0])
        xk = x + xx * (time_maa_k + m[1])
        xv = x + xx * (time_maa_v + m[2])
        xr = x + xx * (time_maa_r + m[3])
        xg = x + xx * (time_maa_g + m[4])
        r = xr @ Wr
        k = xk @ Wk
        v = xv @ Wv
        g = jax.nn.silu(xg @ Wg)
        w = time_decay + jnp.tanh(xw @ time_decay_w1) @ time_decay_w2
        y = _wkv6(r.reshape(b, t, h, n), k.reshape(b, t, h, n), v.reshape(b, t, h, n), w.reshape(b, t, h, n), time_faaaa)
        mu = y.mean(-1, keepdims=True)
        var = y.var(-1, keepdims=True)
        yn = ((y - mu) / jnp.sqrt(var + LN_EPS)).reshape(b, t, c) * ln_w + ln_b
        return yn * g @ Wo

    def _L0_ffn_ref(x, Wg, W1, W2, W3):
        import jax, jax.numpy as jnp
        import numpy as np
        B, S, D = (4, 128, 128)
        E, K = (8, 2)
        H = 2 * D
        gate_out = jnp.einsum('bsd,ed->bse', x, Wg)
        top_v, top_i = jax.lax.top_k(gate_out, K)
        probs = jax.nn.softmax(top_v, axis=-1)
        out = jnp.zeros_like(x)
        for e in range(E):
            w_e = jnp.sum(probs * (top_i == e), axis=-1)
            h1 = jnp.einsum('bsd,hd->bsh', x, W1[e])
            h2 = jnp.einsum('bsd,hd->bsh', x, W2[e])
            g = h1 * jax.nn.sigmoid(h1) * h2
            y = jnp.einsum('bsh,dh->bsd', g, W3[e])
            out = out + y * w_e[..., None]
        return out

    def _L1_attn_ref(q, W_query, W_key, W_val, W_out):
        import jax, jax.numpy as jnp
        import numpy as np
        N_HEADS = 16
        INPUT_DIM = 128
        EMBED_DIM = 128
        KEY_DIM = EMBED_DIM // N_HEADS
        BATCH = 4
        SEQ = 256

        def _uniform(key, shape, bound):
            return jax.random.uniform(key, shape, jnp.float32, -bound, bound)
        norm = 1.0 / np.sqrt(KEY_DIM)
        Q = jnp.einsum('bsd,hdk->hbsk', q, W_query)
        K = jnp.einsum('bsd,hdk->hbsk', q, W_key)
        V = jnp.einsum('bsd,hdv->hbsv', q, W_val)
        scores = norm * jnp.einsum('hbqk,hbnk->hbqn', Q, K)
        attn = jax.nn.softmax(scores, axis=-1)
        heads = jnp.einsum('hbqn,hbnv->hbqv', attn, V)
        out = jnp.einsum('hbqv,hve->bqe', heads, W_out)
        return out

    def _L1_ffn_ref(x_bsD, router_DE, w_in_shared_FD, w_out_shared_DF, w_swiglu_FD, w_in_eDF, w_swiglu_eDF, w_out_eFD):
        import jax, jax.numpy as jnp
        import numpy as np
        TOP_K = 2
        E = 8
        D = 128
        F = 256
        B, S = (2, 128)
        b, s, d = x_bsD.shape
        x_aD = x_bsD.reshape(-1, d)
        a = x_aD.shape[0]
        scores_aE = x_aD @ router_DE
        topv_aK, topi_aK = jax.lax.top_k(scores_aE, TOP_K)
        masked_aE = jnp.full_like(scores_aE, -jnp.inf)
        masked_aE = masked_aE.at[jnp.arange(a)[:, None], topi_aK].set(topv_aK)
        gates_Ea = jax.nn.sigmoid(masked_aE.astype(jnp.float32)).astype(x_aD.dtype).T
        routed_in_EaD = x_aD[None, :, :] * gates_Ea[:, :, None]
        routed_in_EaD = jax.lax.stop_gradient(routed_in_EaD)
        mid_EaF = jnp.einsum('ead,edf->eaf', routed_in_EaD, w_in_eDF)
        sw_EaF = jnp.einsum('ead,edf->eaf', routed_in_EaD, w_swiglu_eDF)
        h_EaF = jax.nn.silu(mid_EaF) * sw_EaF
        out_EaD = jnp.einsum('eaf,efd->ead', h_EaF, w_out_eFD)
        shared_aF = jax.nn.silu(x_aD @ w_in_shared_FD.T) * (x_aD @ w_swiglu_FD.T)
        shared_out_aD = jax.lax.stop_gradient(shared_aF @ w_out_shared_DF.T)
        out_aD = shared_out_aD + jnp.sum(out_EaD, axis=0)
        return out_aD.reshape(b, s, d)
    x = L0_attn_x
    xn = _layernorm(x, axis=-1)
    s = _L0_attn_ref(xn, L0_attn_time_maa_x, L0_attn_time_maa_w, L0_attn_time_maa_k, L0_attn_time_maa_v, L0_attn_time_maa_r, L0_attn_time_maa_g, L0_attn_time_maa_w1, L0_attn_time_maa_w2, L0_attn_time_decay, L0_attn_time_decay_w1, L0_attn_time_decay_w2, L0_attn_time_faaaa, L0_attn_Wr, L0_attn_Wk, L0_attn_Wv, L0_attn_Wg, L0_attn_Wo, L0_attn_ln_w, L0_attn_ln_b)
    g = _silu(_L0_ffn_ref(xn, L0_ffn_Wg, L0_ffn_W1, L0_ffn_W2, L0_ffn_W3))
    x = x + s * g
    xn = _layernorm(x, axis=-1)
    s = _L1_attn_ref(xn, L1_attn_W_query, L1_attn_W_key, L1_attn_W_val, L1_attn_W_out)
    g = _silu(_L1_ffn_ref(xn, L1_ffn_router_DE, L1_ffn_w_in_shared_FD, L1_ffn_w_out_shared_DF, L1_ffn_w_swiglu_FD, L1_ffn_w_in_eDF, L1_ffn_w_swiglu_eDF, L1_ffn_w_out_eFD))
    x = x + s * g
    return x

_drawn_inputs = setup_inputs


def setup_inputs(seed=0):
    import zlib

    import numpy as np

    out = dict(_drawn_inputs(seed))
    spreads = {'L0_attn_ln_w': (1.0, 0.6), 'L0_attn_ln_b': (0.0, 0.8)}
    factors = {'L0_attn_time_maa_x': 8.0,
     'L0_attn_time_maa_w': 64.0,
     'L0_attn_time_maa_k': 8.0,
     'L0_attn_time_maa_v': 8.0,
     'L0_attn_time_maa_r': 8.0,
     'L0_attn_time_maa_g': 8.0,
     'L0_attn_time_maa_w1': 8.0,
     'L0_attn_time_maa_w2': 8.0,
     'L0_attn_time_decay': 8.0,
     'L0_attn_time_decay_w1': 64.0,
     'L0_attn_time_decay_w2': 64.0,
     'L0_attn_time_faaaa': 8.0,
     'L0_attn_Wr': 8.0,
     'L0_attn_Wk': 8.0,
     'L0_attn_Wv': 8.0,
     'L0_attn_Wg': 8.0,
     'L0_attn_Wo': 8.0,
     'L0_ffn_Wg': 8.0,
     'L0_ffn_W1': 8.0,
     'L0_ffn_W2': 8.0,
     'L0_ffn_W3': 8.0,
     'L1_attn_W_query': 8.0,
     'L1_attn_W_key': 8.0,
     'L1_attn_W_val': 8.0,
     'L1_attn_W_out': 8.0,
     'L1_ffn_router_DE': 8.0,
     'L1_ffn_w_in_shared_FD': 8.0,
     'L1_ffn_w_out_shared_DF': 8.0,
     'L1_ffn_w_swiglu_FD': 8.0,
     'L1_ffn_w_in_eDF': 8.0,
     'L1_ffn_w_swiglu_eDF': 8.0,
     'L1_ffn_w_out_eFD': 8.0}
    for name, (base, spread) in spreads.items():
        noise = np.random.default_rng([zlib.crc32(name.encode()), seed]).standard_normal(out[name].shape)
        drawn = base * np.exp(spread * noise) if base else spread * noise
        out[name] = jnp.asarray(drawn.astype(out[name].dtype))
    for name, factor in factors.items():
        out[name] = (out[name] * factor).astype(out[name].dtype)
    return out
```

```python
from contextlib import ExitStack

import concourse.bass as bass
import numpy as np
from concourse import mybir

F32 = mybir.dt.float32
F32R = mybir.dt.float32r
I32 = mybir.dt.int32
U32 = mybir.dt.uint32
ALU = mybir.AluOpType
ACT = mybir.ActivationFunctionType
AX = mybir.AxisListType.X

P = 128
B, T, C = 16, 512, 128
NT = T // P
NH0, HS = 2, 64
E = 8
FT = 2
E1 = E + 1
NH, DK = 16, 8
HG = 4
NG = NH // HG
LN_EPS = 1e-5
GN_EPS = 64e-5
DECAY_MAX = 110.0
HALVES = (2, 4, 8, 16, 32)
VCOLS = 32

MIX_W, MIX_K, MIX_V, MIX_R, MIX_G = range(5)
COL_X, COL_MIX, COL_DECAY, COL_U, COL_LNW, COL_LNB, COL_KONE = 0, 1, 6, 7, 8, 9, 10
WR, WK, WV, WG, WO, AQ, AK, AV, AO = range(9)
QSCALE = (DK ** -0.5, 1.0)
LEVEL = {"cross128": len(HALVES), "cross256": len(HALVES) + 1, "cross512": len(HALVES) + 2}


def plan():
    experts0 = [(0, "up", e, f) for e in range(E) for f in range(FT)]
    mix = [(0, "mixin"), (0, "lora", MIX_W), (0, "lora", MIX_K), (0, "decay"), (0, "lora", MIX_R),
           (0, "proj", WK), (0, "lora", MIX_V), (0, "proj", WR), (0, "lora", MIX_G), (0, "value"),
           (0, "proj", WG), (0, "diag"), (0, "pair")]
    mix += [(0, "level", n) for n in range(len(HALVES))]
    mix += [(0, "cross128"), (0, "cross256"), (0, "cross512", 0), (0, "cross512", 1), (0, "wkv"), (0, "wkvT")]
    attn = [(1, "qk", AQ), (1, "qk", AK), (1, "attnv")]
    maxes = [(1, "smax", h, t) for h in range(NH) for t in range(NT)]
    return experts0, mix, attn, maxes


def with_downs(ups, lag):
    out, due = [], []
    for i, s in enumerate(ups):
        out.append(s)
        due = [(n - 1, d) for n, d in due]
        while due and due[0][0] <= 0:
            out.append(due.pop(0)[1])
        if s[3] == FT - 1:
            due.append((lag, (s[0], "down", s[2])))
    return out + [d for _, d in due]


def merge(*streams):
    tagged = []
    for k, stream in enumerate(streams):
        tagged += [((i + 0.5) / len(stream), k, i, s) for i, s in enumerate(stream)]
    return [s for *_, s in sorted(tagged, key=lambda x: x[:3])]


def build_plan():
    ups0, mix, attn, _ = plan()
    ups1 = []
    for e in [E] + list(range(E)):
        if e < E:
            ups1.append((1, "gates", e))
        ups1 += [(1, "up", e, f) for f in range(FT)]
    moe1, moe0 = [], []
    for s in ups1:
        moe1.append(s)
        if s[1] == "up" and s[3] == 0 and s[2] != E:
            moe1.append((1, "down", s[2] - 1 if s[2] else E))
    moe1 += [(1, "down", E - 1), (1, "mixed")]
    for s in ups0:
        moe0.append(s)
        if s[3] == 0 and s[2] > 0:
            moe0.append((0, "down", s[2] - 1))
    moe0.append((0, "down", E - 1))
    steps = []
    for g in range(NG + 1):
        tiles = []
        for j in range(HG):
            for t in range(NT):
                if g < NG:
                    tiles.append((1, "smax", HG * g + j, t))
                if g > 0:
                    tiles.append((1, "soft", HG * (g - 1) + j, t))
        if g > 0:
            tiles.append((1, "pv", g - 1))
        if g < NG:
            tiles.append((1, "mrow", g))
        if g > 0:
            tiles.append((1, "headsT", g - 1))
        if g < NG:
            tiles = [(1, "stack", AQ, g), (1, "stack", AK, g)] + tiles
        steps += tiles
    head = [(1, "norm"), (0, "norm"), (1, "route"), (0, "route")] 
    nk = 3
    attention = attn + steps + [(1, "outT")]
    moe = moe1 + moe0
    body = merge(attention, moe, mix)
    tail = [(1, "finish"), (0, "finish")]
    return head + body + tail


PLAN = build_plan()
MISC, HA, GA, HB, GB, YB, SB, TB = "misc", "ha", "ga", "hb", "gb", "y", "s", "st"
BANKS = (MISC, HA, GA, HB, GB, YB, SB, TB)


def fills(step):
    layer, kind = step[:2]
    if kind == "up":
        return [HA, GA] if step[3] == 0 else [HB, GB]
    if kind == "down":
        return [YB] if layer == 0 or step[2] == E - 1 else []
    if kind == "smax":
        return [SB]
    if kind == "soft":
        return [TB]
    n = {"norm": 1, "route": 1, "mixin": 2, "lora": 1, "decay": 2, "proj": 1, "value": 1, "diag": 1, "pair": 1,
         "level": 1, "cross128": 1, "cross256": 1, "cross512": 1, "wkv": 1, "wkvT": 1, "finish": 1, "mixed": 0,
         "qk": 1, "attnv": 1, "stack": 1, "mrow": 1, "pv": 1, "headsT": 1, "outT": 1, "gates": 1}[kind]
    if kind == "route" and layer == 1:
        n = 2
    return [MISC] * n


def fills_of(layer, bank):
    return sum(fills(s).count(bank) for s in PLAN if s[0] == layer)


class Turn:

    def __init__(self, number, layers):
        self.seq = (number, number - 1)
        self.steps = [s for s in PLAN if s[0] in layers]
        self.ups = [s for s in self.steps if s[1] == "up"]
        self.before, count = {}, {b: 0 for b in BANKS}
        for s in self.steps:
            self.before[s] = dict(count)
            for b in fills(s):
                count[b] += 1

    def fill(self, step, bank, n=0):
        return self.before[step][bank] + n + 1


def two_layer_kernel(nc, x, cols, mix1, square, mix2, dec1, dec2, up0, gate0, down0, up1, gate1, down1,
                     routers, ident, masks, select, iota, out):
    with ExitStack() as ctx:
        def sb(name, shape, dt=F32):
            return ctx.enter_context(nc.sbuf_tensor(name, shape, dt))

        def sem(name):
            return ctx.enter_context(nc.semaphore(name))

        def tiles(tensor):
            return tensor[:].rearrange("p (q c) -> p q c", q=NT)

        cols_sb = sb("cols_sb", [P, 11])
        mix1_sb = sb("mix1_sb", [P, 160])
        sq = sb("sq", [P, 9, C])
        mix2_sb = sb("mix2_sb", [P, C])
        mix2g_sb = sb("mix2g_sb", [32, C])
        dec1_sb = sb("dec1_sb", [P, 64])
        dec2_sb = sb("dec2_sb", [64, C])
        up_sb = [sb("up0_sb", [P, E, 256]), sb("up1_sb", [P, E1, 256])]
        gate_sb = [sb("gate0_sb", [P, E, 256]), sb("gate1_sb", [P, E1, 256])]
        down_sb = [sb("down0_sb", [P, E, FT, C]), sb("down1_sb", [P, E1, FT, C])]
        router_sb = sb("router_sb", [P, 2, E])
        ident_sb = sb("ident_sb", [P, P])
        masks_sb = sb("masks_sb", [P, 7, HS])
        select_sb = sb("select_sb", [P, 4, P], F32R)
        iota_sb = sb("iota_sb", [P, E])
        ones_sb = sb("ones_sb", [P, P])
        power_sb = sb("power_sb", [P, 8])

        stats = [sb(f"stats{i}", [P, NT, 6]) for i in range(2)]
        moments = [sb(f"moments{i}", [P, NT, 2]) for i in range(2)]
        vareps = [sb(f"vareps{i}", [P, NT]) for i in range(2)]
        rstd = [sb(f"rstd{i}", [P, NT]) for i in range(2)]
        xn = [sb(f"xn{i}", [P, NT, C]) for i in range(2)]
        xnT0 = sb("xnT0", [P, 1 + T])
        xnT1 = sb("xnT1", [P, T])
        xnT = (xnT0[:, 1:], xnT1[:])
        top = [sb(f"top{i}", [P, NT, 8]) for i in range(2)]
        scores_sb = [sb(f"scores{i}", [P, NT, E]) for i in range(2)]
        topi = [sb(f"topi{i}", [P, NT, 8], U32) for i in range(2)]
        wtmp = [sb(f"wtmp{i}", [P, 6, NT]) for i in range(2)]
        gatew = [sb(f"gatew{i}", [P, NT, E]) for i in range(2)]
        pick_sb = [sb(f"pick{i}", [P, 2, NT, E]) for i in range(2)]
        th = sb("th", [P, 2, T])
        hid = sb("hid", [P, 4, T])

        x_sb = sb("x_sb", [P, NT, C])
        shiftT = sb("shiftT", [P, T])
        p128 = shiftT[0:HS, :].rearrange("p (q h c) -> p q h c", q=NT, h=NH0)
        xxxT = sb("xxxT", [P, T])
        elw, gth = xxxT, xxxT
        pdiag = xxxT[:].rearrange("p (q h c) -> p q h c", q=NT, h=NH0)
        mixa = sb("mixa", [P, T])
        zT = mixa
        gT = sb("gT", [P, T])
        mixb = gT[0:32, :]
        elwc = sb("elwc", [P, T])
        dec_h, ynT = elwc[0:64, :], elwc
        moved = sb("moved", [P, 2, T])
        diff = moved
        th_f0 = moved[:, 0, :].rearrange("p (q c) -> p q c", q=NT)
        xmixT = sb("xmixT", [P, 3, T])
        p512 = xmixT[:, 0:2, :].rearrange("p h (c n) -> p h c n", c=2)
        p256 = xmixT[:, 2, :].rearrange("p (m h c) -> p m h c", m=2, h=NH0)
        cum = sb("cum", [P, NT, P + 1])
        tot01 = sb("tot01", [P, 1])
        rT = sb("rT", [P, T])
        kT = sb("kT", [P, T])
        urT = sb("urT", [P, T])
        v0 = sb("v0", [P, NT, C])
        expd = sb("expd", [P, 2, T])
        q2_0 = expd[:, 0, :].rearrange("p (q c) -> p q c", q=NT)
        rk = sb("rk", [P, 2, T])
        gstats = sb("gstats", [P, NT * NH0, 6])
        gmom = sb("gmom", [P, NT * NH0, 2])
        gvar = sb("gvar", [P, NT * NH0])
        grstd = sb("grstd", [P, NT * NH0])
        yn = xn[0]
        acc0 = sb("acc0", [P, NT, C])
        ytmp = sb("ytmp", [P, 2, NT, C])
        x1 = sb("x1", [P, NT, C])

        x1b = sb("x1b", [P, NT, C])
        gwT = sb("gwT", [E, T])
        xg = sb("xg", [P, 2, T])
        qk_hi = sb("qk_hi", [P, 2, T], F32R)
        qk_lo = sb("qk_lo", [P, 2, T], F32R)
        qs = sb("qs", [P, 2, T], F32R)
        ks = sb("ks", [P, 2, T], F32R)
        v1 = sb("v1", [P, NT, NH, VCOLS])
        rowmax = sb("rowmax", [P, NG, NT, HG])
        m_hi = sb("m_hi", [HG, T], F32R)
        m_lo = sb("m_lo", [HG, T], F32R)
        probs = sb("probs", [P, HG, NT, T])
        oT = sb("oT", [P, T])
        headsT_sb = oT
        rden = sb("rden", [P, NT, HG])
        heads, out_sb = xn[1], xn[1]
        q1_1 = sb("q1_1", [P, NT, C])

        select_ld = probs[:, 0, 0, :].rearrange("p (n c) -> p n c", n=4)
        th_f = (th_f0, xg[:, 1, :].rearrange("p (q c) -> p q c", q=NT))
        q1 = (ytmp[:, 0], q1_1[:])
        q2 = (q2_0, xg[:, 0, :].rearrange("p (q c) -> p q c", q=NT))

        bank = {b: ctx.enter_context(nc.psum_tensor(f"bank_{b}", [P, T], F32)) for b in BANKS}
        s_load = sem("s_load")
        s_set = sem("s_set")
        s_select = sem("s_select")
        arrived = sem("arrived")
        clearing = sem("clearing")
        left = sem("left")
        first_turn_sem = left.num + 1
        filled = {b: sem(f"filled_{b}") for b in BANKS}
        emptied = {b: sem(f"emptied_{b}") for b in BANKS}

        x_in = sem("x_in")
        out_done = sem("out_done")
        mrow_in = sem("mrow_in")
        L = (0, 1)
        st_done = [sem(f"stats_done{i}") for i in L]
        rstd_done = [sem(f"rstd_done{i}") for i in L]
        xn_done = [sem(f"xn_done{i}") for i in L]
        x1_copied = sem("x1_copied")
        top_done = [sem(f"top_done{i}") for i in L]
        gate_pre = [sem(f"gate_pre{i}") for i in L]
        gate_exp = [sem(f"gate_exp{i}") for i in L]
        gate_math = [sem(f"gate_math{i}") for i in L]
        gatew_done = [sem(f"gatew_done{i}") for i in L]
        shift_done = sem("shift_done")
        xxx_done = sem("xxx_done")
        xmix_done = sem("xmix_done")
        elwc_done = sem("elwc_done")
        cum_done = sem("cum_done")
        tot_done = sem("tot_done")
        ur_done = sem("ur_done")
        gth_done = sem("gth_done")
        diff_done = sem("diff_done")
        expd_done = sem("expd_done")
        rows_done = sem("rows_done")
        rk_half = sem("rk_half")
        rk_done = sem("rk_done")
        gst_done = sem("gst_done")
        grstd_done = sem("grstd_done")
        yn_done = sem("yn_done")
        zT_done = sem("zT_done")
        acc_done = sem("acc_done")
        thf_done = [sem(f"thf_done{i}") for i in L]
        q1_done = sem("q1_done")
        x1_done = sem("x1_done")
        th_done = [sem(f"th_done{i}") for i in L]
        down_done = [sem(f"down_done{i}") for i in L]
        qkhi_done = sem("qkhi_done")
        mhi_done = sem("mhi_done")
        rden_done = sem("rden_done")
        out_ready = sem("out_ready")

        loads = [(cols_sb[:], cols), (mix1_sb[:], mix1), (sq[:], square), (mix2_sb[:], mix2[0:P, :]),
                 (mix2g_sb[:], mix2[P:160, :]), (dec1_sb[:], dec1), (dec2_sb[:], dec2),
                 (router_sb[:], routers), (ident_sb[:], ident), (masks_sb[:], masks), (select_ld, select),
                 (iota_sb[:], iota), (up_sb[0][:], up0), (gate_sb[0][:], gate0), (down_sb[0][:], down0),
                 (up_sb[1][:], up1), (gate_sb[1][:], gate1), (down_sb[1][:], down1)]
        NSET = 6
        ups = [s for s in PLAN if s[1] == "up"]
        downs = [[s for s in PLAN if s[:2] == (i, "down")] for i in L]
        loras = [s[2] for s in PLAN if s[1] == "lora"]

        def up_no(s):
            return [u for u in ups if u[0] == s[0]].index(s)

        def hid_slot(s):
            return ups.index(s) % 4

        def down_no(s):
            return downs[s[0]].index((s[0], "down", s[2]))

        def lora_no(m):
            return loras.index(m)

        fenced = [s for s in PLAN if s[1] in ("diag", "pair", "level", "cross128", "cross256", "wkv")]

        def level_step(n):
            names = [(0, "diag"), (0, "pair")] + [(0, "level", k) for k in range(len(HALVES))] + [(0, "cross128"), (0, "cross256")]
            return names[n + 2]

        last_turn_sem = out_ready.num

        def turns(eng, step):
            run(eng, step, Turn(0, (0,)), 0)
            with eng.Fori(1, B) as i:
                run(eng, step, Turn(i, (0, 1)), i)
            run(eng, step, Turn(B, (1,)), None)

        def run(eng, step, turn, number):
            for s in turn.steps:
                step(turn, s)
            if number is not None:
                eng.drain().then_inc(arrived, 1)
                if eng is nc.sync:
                    eng.wait_ge(arrived, number * 5 + 5)
                    eng.sem_inc(clearing, 1)
                    eng.sem_clear(range(first_turn_sem, last_turn_sem + 1))
                    eng.sem_inc(left, 1)
                else:
                    eng.wait_ge(left, number + 1)
                    eng.wait_ge(s_load, 16 * len(loads))

        block = ctx.enter_context(nc.Block())

        @block.sync
        def _(sp):
            for dst, src in loads:
                sp.dma_start(dst, src).then_inc(s_load, 16)

            def step(t, s):
                layer, kind = s[:2]
                if (layer, kind) == (0, "norm"):
                    sp.dma_start(x_sb[:], x[t.seq[0]].rearrange("(q p) c -> p q c", p=P)).then_inc(x_in, 16)
                elif kind == "mrow":
                    g = s[2]
                    sp.wait_ge(mhi_done, g + 1)
                    sp.dma_start(qs[24::32, g % 2, :].bitcast(F32), m_hi[:].bitcast(F32)).then_inc(mrow_in, 16)
                    sp.wait_ge(emptied[MISC], t.fill(s, MISC))
                    sp.dma_start(qs[25::32, g % 2, :].bitcast(F32), m_lo[:].bitcast(F32)).then_inc(mrow_in, 16)
                elif (layer, kind) == (1, "finish"):
                    sp.wait_ge(out_ready, 1)
                    sp.dma_start(out[t.seq[1]].rearrange("(q p) c -> p q c", p=P), out_sb[:]).then_inc(out_done, 16)
                    sp.wait_ge(out_done, 16)

            turns(sp, step)

        @block.tensor
        def _(pe):
            mm = nc.tensor.matmul

            def room(t, s, b, n=0):
                if t.fill(s, b, n) > 1:
                    pe.wait_ge(emptied[b], t.fill(s, b, n) - 1)
                return bank[b]

            def fence(s, last):
                last.then_inc(rows_done, 1)
                pe.wait_ge(rows_done, fenced.index(s) + 1)

            def transposes(dst, src):
                for q in range(NT):
                    last = nc.tensor.transpose(dst[:, q * P:(q + 1) * P], src[:, q, :], ident_sb[:])
                return last

            def step(t, s):
                layer, kind = s[:2]
                if kind == "norm":
                    pe.wait_ge(xn_done[layer], NT)
                    transposes(room(t, s, MISC), xn[layer]).then_inc(filled[MISC], 1)
                elif kind == "route":
                    pe.wait_ge(emptied[MISC], t.fill((layer, "norm"), MISC))
                    ps = room(t, s, MISC)
                    for q in range(NT):
                        last = mm(ps[:, q * E:(q + 1) * E], xnT[layer][:, q * P:(q + 1) * P], router_sb[:, layer, :],
                                  start=True, stop=True)
                    last.then_inc(filled[MISC], 1)
                    if layer == 1:
                        pe.wait_ge(gatew_done[1], 1)
                        ps = room(t, s, MISC, 1)
                        for q in range(NT):
                            last = nc.tensor.transpose(ps[0:E, q * P:(q + 1) * P], gatew[1][:, q, :], ident_sb[:])
                        last.then_inc(filled[MISC], 1)
                elif kind == "gates":
                    pe.wait_ge(emptied[MISC], t.fill((1, "route"), MISC, 1))
                    mm(room(t, s, MISC)[:], ident_sb[0:E, s[2]:s[2] + 1].to_broadcast([E, P]), gwT[:], start=True, stop=True).then_inc(filled[MISC], 1)
                elif kind == "up":
                    e, f = s[2:]
                    if layer == 1 and e < E:
                        pe.wait_ge(emptied[MISC], t.fill((1, "gates", e), MISC))
                    rhs = xnT[layer] if layer == 0 or e == E else xg[:, e % 2, :]
                    for b, w in zip(fills(s), (up_sb[layer], gate_sb[layer])):
                        mm(room(t, s, b)[:], w[:, e, f * P:(f + 1) * P], rhs, start=True, stop=True).then_inc(filled[b], 1)
                elif kind == "down":
                    e, n = s[2], down_no(s)
                    for f in range(FT):
                        pe.wait_ge(emptied[(GA, GB)[f]], t.fill((layer, "up", e, f), (GA, GB)[f]))
                    if layer == 0 or n == 0:
                        room(t, s if layer == 0 else (1, "down", E - 1), YB)
                    for q in range(NT):
                        for f in range(FT):
                            start = f == 0 if layer == 0 else n == q == f == 0
                            last = mm(bank[YB][:, q * P:(q + 1) * P],
                                      hid[:, hid_slot((layer, "up", e, f)), q * P:(q + 1) * P], down_sb[layer][:, e, f, :],
                                      start=start, stop=f == FT - 1 and (layer == 0 or n == E), skip_group_check=True)
                    last.then_inc(down_done[layer], 1)
                elif kind == "mixin":
                    pe.wait_ge(xxx_done, 1)
                    mm(room(t, s, MISC)[:], mix1_sb[:, 0:P], xxxT[:], start=True, stop=True).then_inc(filled[MISC], 1)
                    mm(room(t, s, MISC, 1)[0:32, :], mix1_sb[:, P:160], xxxT[:], start=True, stop=True).then_inc(filled[MISC], 1)
                elif kind == "lora":
                    m = s[2]
                    pe.wait_ge(emptied[MISC], t.fill((0, "mixin"), MISC, 1))
                    lhsT, rhs = (mix2g_sb[:], mixb) if m == 4 else (mix2_sb[32 * m:32 * m + 32, :], mixa[32 * m:32 * m + 32, :])
                    mm(room(t, s, MISC)[:], lhsT, rhs, start=True, stop=True).then_inc(filled[MISC], 1)
                elif kind == "decay":
                    pe.wait_ge(xmix_done, lora_no(MIX_W) + 1)
                    mm(room(t, s, MISC)[0:64, :], dec1_sb[:], xmixT[:, lora_no(MIX_W) % 3, :], start=True, stop=True).then_inc(filled[MISC], 1)
                    pe.wait_ge(emptied[MISC], t.fill(s, MISC, 0))
                    mm(room(t, s, MISC, 1)[:], dec2_sb[:], dec_h, start=True, stop=True).then_inc(filled[MISC], 1)
                elif kind == "proj":
                    m = {WR: MIX_R, WK: MIX_K, WG: MIX_G}[s[2]]
                    pe.wait_ge(xmix_done, lora_no(m) + 1)
                    mm(room(t, s, MISC)[:], sq[:, s[2], :], xmixT[:, lora_no(m) % 3, :], start=True, stop=True).then_inc(filled[MISC], 1)
                elif kind == "value":
                    pe.wait_ge(xmix_done, lora_no(MIX_V) + 1)
                    ps = room(t, s, MISC)
                    for q in range(NT):
                        last = mm(ps[:, q * P:(q + 1) * P], xmixT[:, lora_no(MIX_V) % 3, q * P:(q + 1) * P], sq[:, WV, :], start=True, stop=True)
                    last.then_inc(filled[MISC], 1)
                elif kind == "attnv":
                    ps = room(t, s, MISC)
                    for q in range(NT):
                        last = mm(ps[:, q * P:(q + 1) * P], xnT[1][:, q * P:(q + 1) * P], sq[:, AV, :], start=True, stop=True)
                    last.then_inc(filled[MISC], 1)
                elif kind in ("diag", "pair", "level"):
                    if kind == "level":
                        pe.wait_ge(rk_done, s[2] + 1)
                        a = b = rk[:, s[2] % 2, :]
                    else:
                        pe.wait_ge(emptied[MISC], t.fill((0, "proj", WK), MISC))
                        pe.wait_ge(emptied[MISC], t.fill((0, "proj", WR), MISC))
                        if kind == "diag":
                            pe.wait_ge(ur_done, 1)
                        a, b = kT[:], (urT if kind == "diag" else rT)[:]
                    ps = room(t, s, MISC)
                    for h in range(NH0):
                        for q in range(NT):
                            ch, o = slice(HS * h, HS * h + HS), (q * NH0 + h) * HS
                            for half in range(2):
                                tok = slice(q * P + HS * half, q * P + HS * half + HS)
                                last = mm(ps[HS * half:HS * half + HS, o:o + HS], a[ch, tok], b[ch, tok], start=True, stop=True)
                        if h == 0:
                            fence(s, last)
                    last.then_inc(filled[MISC], 1)
                elif kind in ("cross128", "cross256", "cross512"):
                    n = LEVEL[kind]
                    pe.wait_ge(rk_done, n + 1)
                    ps, a = room(t, s, MISC), rk[:, n % 2, :]
                    for h in ([s[2]] if kind == "cross512" else range(NH0)):
                        ch = slice(HS * h, HS * h + HS)
                        if kind == "cross128":
                            for q in range(NT):
                                o = (q * NH0 + h) * HS
                                last = mm(ps[0:HS, o:o + HS], a[ch, q * P:q * P + HS], a[ch, q * P + HS:(q + 1) * P], start=True, stop=True)
                        elif kind == "cross256":
                            for p in range(2):
                                o = (p * NH0 + h) * P
                                last = mm(ps[:, o:o + P], a[ch, 2 * p * P:(2 * p + 1) * P], a[ch, (2 * p + 1) * P:(2 * p + 2) * P],
                                          start=True, stop=True)
                        else:
                            for c in range(2):
                                last = mm(ps[:, c * 2 * P:(c + 1) * 2 * P], a[ch, c * P:(c + 1) * P], a[ch, 2 * P:4 * P], start=True, stop=True)
                        if h == 0 and kind != "cross512":
                            fence(s, last)
                    last.then_inc(filled[MISC], 1)
                elif kind == "wkv":
                    pe.wait_ge(emptied[MISC], t.fill((0, "value"), MISC))
                    pe.wait_ge(emptied[MISC], t.fill((0, "level", len(HALVES) - 1), MISC))
                    pe.wait_ge(emptied[MISC], t.fill((0, "cross512", 1), MISC))
                    ps = room(t, s, MISC)
                    for q in range(NT):
                        for h in range(NH0):
                            o, clear = ps[:, q * P + HS * h:q * P + HS * h + HS], q == h == 0
                            vv = v0[:, :, HS * h:HS * h + HS]
                            far = [(p256[:, q // 2, h, :], vv[:, q - 1, :])] if q % 2 else []
                            if q >= 2:
                                far += [(p512[:, h, c, (q - 2) * P:(q - 1) * P], vv[:, c, :]) for c in range(2)]
                            for a, b in far:
                                mm(o, a, b, start=False, stop=False, skip_group_check=True)
                            mm(o[0:HS], pdiag[0:HS, q, h, :], vv[0:HS, q, :], start=clear, stop=True, skip_group_check=True)
                            last = mm(o[HS:P], p128[:, q, h, :], vv[0:HS, q, :], start=clear, stop=False, skip_group_check=True)
                    fence(s, last)
                    for q in range(NT):
                        for h in range(NH0):
                            last = mm(ps[HS:P, q * P + HS * h:q * P + HS * h + HS], pdiag[HS:P, q, h, :],
                                      v0[HS:P, q, HS * h:HS * h + HS], start=False, stop=True, skip_group_check=True)
                    last.then_inc(filled[MISC], 1)
                elif kind == "wkvT":
                    pe.wait_ge(yn_done, 1)
                    transposes(room(t, s, MISC), yn).then_inc(filled[MISC], 1)
                elif kind == "finish":
                    if layer == 0:
                        pe.wait_ge(zT_done, 1)
                    else:
                        pe.wait_ge(emptied[MISC], t.fill((1, "outT"), MISC))
                    ps, src = room(t, s, MISC), (zT, headsT_sb)[layer]
                    for q in range(NT):
                        last = mm(ps[:, q * P:(q + 1) * P], src[:, q * P:(q + 1) * P], sq[:, (WO, AO)[layer], :], start=True, stop=True)
                    last.then_inc(filled[MISC], 1)
                elif kind == "qk":
                    mm(room(t, s, MISC)[:], sq[:, s[2], :], xnT[1], start=True, stop=True).then_inc(filled[MISC], 1)
                elif kind == "stack":
                    k = s[2] - AQ
                    pe.wait_ge(emptied[MISC], t.fill((1, "qk", s[2]), MISC))
                    ps = room(t, s, MISC)
                    r = slice(32 * s[3], 32 * s[3] + 32)
                    mm(ps[:], select_sb[r, 2 * k, :], qk_hi[r, k, :], start=True, stop=False)
                    mm(ps[:], select_sb[r, 2 * k + 1, :], qk_lo[r, k, :], start=False, stop=True).then_inc(filled[MISC], 1)
                elif kind == "smax":
                    h, q = s[2:]
                    g, r = h // HG, 32 * (h % HG)
                    if (h % HG, q) == (0, 0):
                        pe.wait_ge(emptied[MISC], t.fill((1, "stack", AK, g), MISC))
                    mm(room(t, s, SB)[:], qs[r:r + 32, g % 2, q * P:(q + 1) * P], ks[r:r + 32, g % 2, :],
                       start=True, stop=True).then_inc(filled[SB], 1)
                elif kind == "mrow":
                    g = s[2]
                    pe.wait_ge(emptied[SB], t.fill((1, "smax", HG * g + HG - 1, NT - 1), SB))
                    ps = room(t, s, MISC)
                    for q in range(NT):
                        last = nc.tensor.transpose(ps[0:HG, q * P:(q + 1) * P], rowmax[:, g, q, :], ident_sb[:])
                    last.then_inc(filled[MISC], 1)
                elif kind == "soft":
                    h, k = s[2:]
                    g, r = h // HG, 32 * (h % HG)
                    if (h % HG, k) == (0, 0):
                        pe.wait_ge(mrow_in, 32 * (g + 1))
                    mm(room(t, s, TB)[:], ks[r:r + 32, g % 2, k * P:(k + 1) * P], qs[r:r + 32, g % 2, :],
                       start=True, stop=True).then_inc(filled[TB], 1)
                elif kind == "pv":
                    g = s[2]
                    pe.wait_ge(emptied[MISC], t.fill((1, "attnv"), MISC))
                    pe.wait_ge(emptied[TB], t.fill((1, "soft", HG * g + HG - 1, NT - 1), TB))
                    ps = room(t, s, MISC)
                    for k in range(NT):
                        for j in range(HG):
                            last = mm(ps[32 * j:32 * j + 32, :], v1[:, k, HG * g + j, :], probs[:, j, k, :],
                                      start=k == 0, stop=k == NT - 1, skip_group_check=True)
                    last.then_inc(filled[MISC], 1)
                elif kind == "headsT":
                    pe.wait_ge(emptied[MISC], t.fill((1, "pv", s[2]), MISC))
                    ps = room(t, s, MISC)
                    for q in range(NT):
                        last = nc.tensor.transpose(ps[:, q * P:(q + 1) * P], oT[:, q * P:(q + 1) * P], ident_sb[:])
                    last.then_inc(filled[MISC], 1)
                elif kind == "outT":
                    pe.wait_ge(emptied[MISC], t.fill((1, "headsT", NG - 1), MISC))
                    transposes(room(t, s, MISC), heads).then_inc(filled[MISC], 1)

            pe.wait_ge(s_load, 16 * len(loads))
            pe.wait_ge(s_set, NSET)
            pe.wait_ge(s_select, 1)
            turns(pe, step)

        @block.scalar
        def _(act):
            A = nc.scalar.activation

            def content(t, s, b, n=0):
                act.wait_ge(filled[b], t.fill(s, b, n))
                return bank[b]

            def step(t, s):
                layer, kind = s[:2]
                if kind == "norm":
                    A(xnT[layer], content(t, s, MISC)[:], ACT.Copy).then_inc(emptied[MISC], 1)
                elif kind == "route":
                    w, n = wtmp[layer], layer + 1
                    act.wait_ge(gate_pre[layer], 1)
                    A(w[:, 2:2 + n, :], w[:, 0:n, :], ACT.Exp).then_inc(gate_exp[layer], 1)
                    if layer == 1:
                        A(gwT[:], content(t, s, MISC, 1)[0:E, :], ACT.Copy).then_inc(emptied[MISC], 1)
                elif kind == "up":
                    ba, bb = fills(s)
                    if t.fill(s, bb) > 1:
                        act.wait_ge(emptied[bb], t.fill(s, bb) - 1)
                    A(th[:, s[3], :], content(t, s, ba)[:], ACT.Tanh, scale=0.5).then_inc(th_done[layer], 1)
                elif kind == "mixed":
                    act.wait_ge(down_done[1], E + 1)
                    A(th_f[1], tiles(bank[YB]), ACT.Tanh, scale=0.25).then_inc(thf_done[1], 1)
                elif kind == "mixin":
                    A(mixa[:], content(t, s, MISC)[:], ACT.Tanh).then_inc(emptied[MISC], 1)
                    A(mixb, content(t, s, MISC, 1)[0:32, :], ACT.Tanh).then_inc(emptied[MISC], 1)
                elif kind == "decay":
                    A(dec_h, content(t, s, MISC)[0:64, :], ACT.Tanh).then_inc(emptied[MISC], 1)
                    A(elw[:], content(t, s, MISC, 1)[:], ACT.Exp, bias=cols_sb[:, COL_DECAY:COL_DECAY + 1]).then_inc(emptied[MISC], 1)
                elif kind == "proj":
                    if s[2] == WG:
                        A(gth[:], content(t, s, MISC)[:], ACT.Tanh, scale=0.5).then_inc(gth_done, 1)
                    else:
                        A((rT if s[2] == WR else kT)[:], content(t, s, MISC)[:], ACT.Copy).then_inc(emptied[MISC], 1)
                elif kind == "value":
                    A(v0[:], tiles(content(t, s, MISC)), ACT.Copy).then_inc(emptied[MISC], 1)
                elif kind == "attnv":
                    A(v1[:, :, :, 0:DK], content(t, s, MISC)[:].rearrange("p (q h k) -> p q h k", q=NT, h=NH),
                      ACT.Copy).then_inc(emptied[MISC], 1)
                elif kind == "level":
                    decays(t, s[2])
                elif kind == "cross128":
                    decays(t, LEVEL[kind])
                    A(p128, content(t, s, MISC)[0:HS, :].rearrange("p (q h c) -> p q h c", q=NT, h=NH0),
                      ACT.Copy).then_inc(emptied[MISC], 1)
                elif kind == "cross256":
                    e = expd[:, LEVEL[kind] % 2, :].rearrange("p (q c) -> p q c", q=NT)
                    act.wait_ge(cum_done, NT)
                    act.wait_ge(rk_done, LEVEL[kind] - 1)
                    A(e[:, 1::2, :], cum[:, 1::2, 0:P], ACT.Exp).then_inc(expd_done, 1)
                    for q in (0, 2):
                        A(e[:, q, :], cum[:, q, 1:P + 1], ACT.Exp, bias=cum[:, q, P:P + 1], scale=-1.0).then_inc(expd_done, 1)
                    A(p256, content(t, s, MISC)[:].rearrange("p (q h c) -> p q h c", q=2, h=NH0), ACT.Copy).then_inc(emptied[MISC], 1)
                elif kind == "cross512":
                    if s[2] == 0:
                        e = expd[:, LEVEL[kind] % 2, :].rearrange("p (q c) -> p q c", q=NT)
                        act.wait_ge(tot_done, 1)
                        act.wait_ge(rk_done, LEVEL[kind] - 1)
                        A(e[:, 2, :], cum[:, 2, 0:P], ACT.Exp).then_inc(expd_done, 1)
                        A(e[:, 3, :], cum[:, 3, 0:P], ACT.Exp, bias=cum[:, 2, P:P + 1]).then_inc(expd_done, 1)
                        A(e[:, 1, :], cum[:, 1, 1:P + 1], ACT.Exp, bias=cum[:, 1, P:P + 1], scale=-1.0).then_inc(expd_done, 1)
                        A(e[:, 0, :], cum[:, 0, 1:P + 1], ACT.Exp, bias=tot01[:], scale=-1.0).then_inc(expd_done, 1)
                    A(p512[:, s[2]], content(t, s, MISC)[:].rearrange("p (c n) -> p c n", c=2), ACT.Copy).then_inc(emptied[MISC], 1)
                elif (layer, kind) == (0, "finish"):
                    act.wait_ge(acc_done, E - 1)
                    A(th_f[0], acc0[:], ACT.Tanh, scale=0.5).then_inc(thf_done[0], 1)
                elif kind == "qk":
                    k = s[2] - AQ
                    A(qk_hi[:, k, :], content(t, s, MISC)[:], ACT.Copy, scale=QSCALE[k]).then_inc(qkhi_done, 1)
                elif kind == "stack":
                    ps = content(t, s, MISC)
                    if s[3] >= 2:
                        act.wait_ge(filled[TB], t.fill((1, "soft", HG * (s[3] - 1) - 1, NT - 1), TB))
                    if s[2] == AQ:
                        A(qs[:, s[3] % 2, :], ps[:], ACT.Copy).then_inc(emptied[MISC], 1)
                    else:
                        A(ks[:, s[3] % 2, :], ps[:], ACT.Identity, bias=cols_sb[:, COL_KONE:COL_KONE + 1]).then_inc(emptied[MISC], 1)
                elif kind == "mrow":
                    ps = content(t, s, MISC)
                    if s[2] > 0:
                        act.wait_ge(mrow_in, 32 * s[2])
                    A(m_hi[:], ps[0:HG, :], ACT.Copy, scale=-1.0).then_inc(mhi_done, 1)
                elif kind == "soft":
                    h, k = s[2:]
                    ps = content(t, s, TB)
                    if h >= HG and (h % HG, k) == (0, 0):
                        act.wait_ge(filled[MISC], t.fill((1, "pv", h // HG - 1), MISC))
                    A(probs[:, h % HG, k, :], ps[:], ACT.Exp).then_inc(emptied[TB], 1)
                elif kind == "pv":
                    A(oT[:], content(t, s, MISC)[:], ACT.Copy).then_inc(emptied[MISC], 1)
                elif kind == "outT":
                    A(headsT_sb[:], content(t, s, MISC)[:], ACT.Copy).then_inc(emptied[MISC], 1)

            def decays(t, n):
                act.wait_ge(diff_done, 2 * n + 2)
                if n >= 2:
                    act.wait_ge(rk_done, n - 1)
                A(expd[:, n % 2, :], diff[:, n % 2, :], ACT.Exp).then_inc(expd_done, 1)

            act.wait_ge(s_load, 16 * len(loads))
            A(select_sb[:], select_ld, ACT.Copy).then_inc(s_select, 1)
            act.wait_ge(s_set, NSET)
            turns(act, step)

        @block.gpsimd
        def _(pool):
            tt = nc.gpsimd.tensor_tensor

            def step(t, s):
                layer, kind = s[:2]
                if kind == "norm":
                    pool.wait_ge(st_done[layer], 2 * NT + 1)
                    tt(rstd[layer][:], vareps[layer][:], power_sb[:, 0:NT], ALU.pow).then_inc(rstd_done[layer], 1)
                elif kind == "mixin":
                    pool.wait_ge(emptied[MISC], t.fill((0, "norm"), MISC))
                    tt(shiftT[:], xnT0[:, 0:T], xnT[0], ALU.subtract).then_inc(shift_done, 1)
                elif kind == "lora":
                    m = s[2]
                    pool.wait_ge(emptied[MISC], t.fill(s, MISC))
                    n = lora_no(m)
                    if n >= 3:
                        user = {MIX_W: (0, "decay"), MIX_K: (0, "proj", WK)}[loras[n - 3]]
                        pool.wait_ge(filled[MISC], t.fill(user, MISC))
                    tt(xmixT[:, n % 3, :], moved[:, n % 2, :], xnT[0], ALU.add).then_inc(xmix_done, 1)
                elif kind == "diag":
                    differences(t, 0)
                elif kind == "level":
                    differences(t, s[2] + 1)
                    decayed(t, s[2])
                elif kind == "cross128":
                    decayed(t, LEVEL[kind])
                elif kind == "cross256":
                    n = LEVEL[kind]
                    pool.wait_ge(expd_done, n + 3)
                    pool.wait_ge(filled[MISC], t.fill(level_step(n - 2), MISC))
                    for k, src in ((0, kT), (1, rT)):
                        a, b, c = (v.rearrange("p (m k c) -> p m k c", m=2, k=2)[:, :, k, :] for v in (rk[:, n % 2, :], src[:], expd[:, n % 2, :]))
                        last = tt(a, b, c, ALU.mult)
                        if k == 0:
                            last.then_inc(rk_half, 1)
                    last.then_inc(rk_done, 1)
                elif kind == "cross512" and s[2] == 0:
                    n = LEVEL[kind]
                    pool.wait_ge(expd_done, n + 6)
                    pool.wait_ge(filled[MISC], t.fill(level_step(n - 2), MISC))
                    tt(rk[:, n % 2, 0:2 * P], kT[:, 0:2 * P], expd[:, n % 2, 0:2 * P], ALU.mult).then_inc(rk_half, 1)
                    tt(rk[:, n % 2, 2 * P:T], rT[:, 2 * P:T], expd[:, n % 2, 2 * P:T], ALU.mult).then_inc(rk_done, 1)
                elif kind == "wkv":
                    pool.wait_ge(gst_done, 2 * NT * NH0 + 1)
                    tt(grstd[:], gvar[:], power_sb[:], ALU.pow).then_inc(grstd_done, 1)
                elif (layer, kind) == (0, "down"):
                    n = down_no(s)
                    if n > 0:
                        pool.wait_ge(emptied[YB], t.fill(s, YB))
                        if n > 1:
                            pool.wait_ge(acc_done, n - 1)
                        tt(acc0[:], acc0[:], ytmp[:, n % 2], ALU.add).then_inc(acc_done, 1)
                elif kind == "finish":
                    pool.wait_ge(emptied[MISC], t.fill(s, MISC))
                    dst, src, done = ((x1, x_sb, x1_done), (out_sb, x1b, out_ready))[layer]
                    tt(dst[:], src[:], q2[layer], ALU.add).then_inc(done, 1)

            def differences(t, n):
                if n > len(HALVES):
                    return
                hs = (HALVES + (HS,))[n]
                if n == 0:
                    pool.wait_ge(cum_done, NT)
                    pool.wait_ge(xmix_done, 5)
                if n >= 2:
                    pool.wait_ge(expd_done, n - 1)
                shape = [P, NT, P // (2 * hs), hs]
                before, upto = (cum[:, :, o:o + P].rearrange("p q (n a s) -> p q n a s", a=2, s=hs) for o in (0, 1))
                d = diff[:, n % 2, :].rearrange("p (q n a s) -> p q n a s", q=NT, a=2, s=hs)
                middle = before[:, :, :, 1, 0:1].to_broadcast(shape)
                tt(d[:, :, :, 0, :], middle, upto[:, :, :, 0, :], ALU.subtract).then_inc(diff_done, 1)
                tt(d[:, :, :, 1, :], before[:, :, :, 1, :], middle, ALU.subtract).then_inc(diff_done, 1)

            def decayed(t, n):
                hs = (HALVES + (HS,))[n]
                pool.wait_ge(expd_done, n + 1)
                if n == 0:
                    pool.wait_ge(emptied[MISC], t.fill((0, "proj", WR), MISC))
                    pool.wait_ge(emptied[MISC], t.fill((0, "proj", WK), MISC))
                if n >= 2:
                    pool.wait_ge(filled[MISC], t.fill(level_step(n - 2), MISC))
                for k, src, done in ((0, kT, rk_half), (1, rT, rk_done)):
                    a, b, c = (v.rearrange("p (m a s) -> p m a s", a=2, s=hs)[:, :, k, :] for v in (rk[:, n % 2, :], src[:], expd[:, n % 2, :]))
                    tt(a, b, c, ALU.mult).then_inc(done, 1)

            pool.wait_ge(s_load, 16 * len(loads))
            pool.wait_ge(s_set, NSET)
            turns(pool, step)

        @block.vector
        def _(dve):
            v = nc.vector
            v.memset(ones_sb[:], 1.0).then_inc(s_set, 1)
            v.memset(power_sb[:], -0.5).then_inc(s_set, 1)
            v.memset(xnT0[:, 0:1], 0.0).then_inc(s_set, 1)
            v.memset(cum[:, :, 0:1], 0.0).then_inc(s_set, 1)
            v.memset(v1[:], 0.0).then_inc(s_set, 1)
            dve.wait_ge(s_set, 5)
            v.memset(v1[:, :, :, DK:DK + 1], 1.0).then_inc(s_set, 1)

            def content(t, s, b, n=0):
                dve.wait_ge(filled[b], t.fill(s, b, n))
                return bank[b]

            def col(n):
                return cols_sb[:, n:n + 1]

            def row_mean_var(t, src, layer):
                sig = st_done[layer]
                for q in range(NT):
                    v.bn_stats(stats[layer][:, q, :], src[:, q, :]).then_inc(sig, 1)
                for q in range(NT):
                    dve.wait_ge(sig, q + 1)
                    v.bn_aggr(moments[layer][:, q, :], stats[layer][:, q, :]).then_inc(sig, 1)
                dve.wait_ge(sig, 2 * NT)
                v.tensor_scalar(vareps[layer][:], moments[layer][:, :, 1], LN_EPS, None, ALU.add).then_inc(sig, 1)

            def step(t, s):
                layer, kind = s[:2]
                if kind == "norm":
                    if layer == 0:
                        dve.wait_ge(x_in, 16)
                        src = x_sb
                    else:
                        v.tensor_copy(x1b[:], x1[:]).then_inc(x1_copied, 1)
                        dve.wait_ge(x1_copied, 1)
                        src = x1b
                    row_mean_var(t, src, layer)
                    dve.wait_ge(rstd_done[layer], 1)
                    for q in range(NT):
                        v.tensor_scalar(xn[layer][:, q, :], src[:, q, :], moments[layer][:, q, 0:1], rstd[layer][:, q:q + 1],
                                        ALU.subtract, ALU.mult).then_inc(xn_done[layer], 1)
                elif kind == "route":
                    route(t, s)
                elif kind == "gates":
                    e = s[2]
                    ps = content(t, s, MISC)
                    if e >= 2:
                        dve.wait_ge(filled[GB], t.fill((1, "up", e - 2, 1), GB))
                    v.tensor_tensor(xg[:, e % 2, :], ps[:], xnT[1], ALU.mult).then_inc(emptied[MISC], 1)
                elif kind == "up":
                    ba, bb = fills(s)
                    no = t.ups.index(s)
                    dve.wait_ge(th_done[layer], up_no(s) + 1)
                    v.scalar_tensor_tensor(out=th[:, s[3], :], in0=th[:, s[3], :], scalar=1.0, in1=bank[ba][:],
                                           op0=ALU.add, op1=ALU.mult).then_inc(emptied[ba], 1)
                    ps = content(t, s, bb)
                    if no >= 4:
                        old = t.ups[no - 4]
                        dve.wait_ge(down_done[old[0]], down_no(old) + 1)
                    dve.wait_ge(emptied[ba], t.fill(s, ba))
                    v.tensor_tensor(hid[:, hid_slot(s), :], th[:, s[3], :], ps[:], ALU.mult).then_inc(emptied[bb], 1)
                elif (layer, kind) == (0, "down"):
                    e, n = s[2], down_no(s)
                    dve.wait_ge(down_done[0], n + 1)
                    if n >= 3:
                        dve.wait_ge(acc_done, n - 2)
                    v.tensor_tensor(acc0[:] if n == 0 else ytmp[:, n % 2], bank[YB][:].rearrange("p (q c) -> p q c", q=NT),
                                    gatew[0][:, :, e:e + 1].to_broadcast([P, NT, C]), ALU.mult).then_inc(emptied[YB], 1)
                elif kind == "mixed":
                    dve.wait_ge(thf_done[1], 1)
                    v.scalar_tensor_tensor(out=q1[1], in0=th_f[1], scalar=1.0, in1=bank[YB][:].rearrange("p (q c) -> p q c", q=NT),
                                           op0=ALU.add, op1=ALU.mult).then_inc(emptied[YB], 1)
                elif kind == "mixin":
                    dve.wait_ge(shift_done, 1)
                    v.scalar_tensor_tensor(out=xxxT[:], in0=shiftT[:], scalar=col(COL_X), in1=xnT[0],
                                           op0=ALU.mult, op1=ALU.add).then_inc(xxx_done, 1)
                elif kind == "lora":
                    m = s[2]
                    n = lora_no(m)
                    ps = content(t, s, MISC)
                    if n >= 2:
                        dve.wait_ge(xmix_done, n - 1)
                    v.scalar_tensor_tensor(out=moved[:, n % 2, :], in0=ps[:], scalar=col(COL_MIX + m), in1=shiftT[:],
                                           op0=ALU.add, op1=ALU.mult).then_inc(emptied[MISC], 1)
                elif kind == "decay":
                    dve.wait_ge(emptied[MISC], t.fill(s, MISC, 1))
                    v.tensor_scalar(elwc[:], elw[:], DECAY_MAX, None, ALU.min).then_inc(elwc_done, 1)
                    dve.wait_ge(elwc_done, 1)
                    for q in range(NT):
                        v.tensor_tensor_scan(cum[:, q, 1:P + 1], ones_sb[:], elwc[:, q * P:(q + 1) * P], 0.0,
                                             ALU.mult, ALU.subtract).then_inc(cum_done, 1)
                    dve.wait_ge(cum_done, NT)
                    v.tensor_tensor(tot01[:], cum[:, 0, P:P + 1], cum[:, 1, P:P + 1], ALU.add).then_inc(tot_done, 1)
                elif kind == "proj":
                    if s[2] == WR:
                        dve.wait_ge(emptied[MISC], t.fill(s, MISC))
                        v.tensor_scalar(urT[:], rT[:], col(COL_U), None, ALU.mult).then_inc(ur_done, 1)
                    elif s[2] == WG:
                        dve.wait_ge(gth_done, 1)
                        v.scalar_tensor_tensor(out=gT[:], in0=gth[:], scalar=1.0, in1=bank[MISC][:],
                                               op0=ALU.add, op1=ALU.mult).then_inc(emptied[MISC], 1)
                elif kind in ("diag", "pair", "level"):
                    n = {"diag": 0, "pair": 1}.get(kind, 2 + s[2] if kind == "level" else 0)
                    ps = content(t, s, MISC)[:].rearrange("p (m c) -> p m c", c=HS)
                    mask = masks_sb[:, n:n + 1, :].to_broadcast([P, NT * NH0, HS])
                    dst = pdiag.rearrange("p q h c -> p (q h) c")
                    if n == 0:
                        v.tensor_tensor(dst, ps, mask, ALU.mult).then_inc(emptied[MISC], 1)
                    else:
                        dve.wait_ge(emptied[MISC], t.fill(level_step(n - 3), MISC))
                        v.copy_predicated(dst, mask.bitcast(I32), ps).then_inc(emptied[MISC], 1)
                elif kind == "wkv":
                    ps = content(t, s, MISC)[:].rearrange("p (m c) -> p m c", c=HS)
                    n = NT * NH0
                    for m in range(n):
                        v.bn_stats(gstats[:, m, :], ps[:, m, :]).then_inc(gst_done, 1)
                    for m in range(n):
                        dve.wait_ge(gst_done, m + 1)
                        v.bn_aggr(gmom[:, m, :], gstats[:, m, :]).then_inc(gst_done, 1)
                    dve.wait_ge(gst_done, 2 * n)
                    v.tensor_scalar(gvar[:], gmom[:, :, 1], GN_EPS, None, ALU.add).then_inc(gst_done, 1)
                    v.tensor_tensor(yn[:].rearrange("p q (h c) -> p (q h) c", c=HS), ps, gmom[:, :, 0:1].to_broadcast([P, n, HS]),
                                    ALU.subtract).then_inc(emptied[MISC], 1)
                    dve.wait_ge(emptied[MISC], t.fill(s, MISC))
                    dve.wait_ge(grstd_done, 1)
                    v.tensor_tensor(yn[:].rearrange("p q (h c) -> p (q h) c", c=HS), yn[:].rearrange("p q (h c) -> p (q h) c", c=HS),
                                    grstd[:].unsqueeze(2).to_broadcast([P, n, HS]), ALU.mult).then_inc(yn_done, 1)
                elif kind == "wkvT":
                    v.tensor_scalar(ynT[:], content(t, s, MISC)[:], col(COL_LNW), col(COL_LNB), ALU.mult, ALU.add).then_inc(emptied[MISC], 1)
                    dve.wait_ge(emptied[MISC], t.fill(s, MISC))
                    v.scalar_tensor_tensor(out=zT[:], in0=gT[:], scalar=0.5, in1=ynT[:], op0=ALU.mult, op1=ALU.mult).then_inc(zT_done, 1)
                elif kind == "finish":
                    if layer == 0:
                        dve.wait_ge(thf_done[0], 1)
                        v.scalar_tensor_tensor(out=q1[0], in0=th_f[0], scalar=1.0, in1=acc0[:],
                                               op0=ALU.add, op1=ALU.mult).then_inc(q1_done, 1)
                        dve.wait_ge(q1_done, 1)
                    else:
                        dve.wait_ge(emptied[YB], t.fill((1, "down", E - 1), YB))
                    v.scalar_tensor_tensor(out=q2[layer], in0=q1[layer], scalar=(0.5, 0.25)[layer],
                                           in1=content(t, s, MISC)[:].rearrange("p (q c) -> p q c", q=NT),
                                           op0=ALU.mult, op1=ALU.mult).then_inc(emptied[MISC], 1)
                elif kind == "qk":
                    k = s[2] - AQ
                    dve.wait_ge(qkhi_done, k + 1)
                    v.scalar_tensor_tensor(out=qk_lo[:, k, :], in0=bank[MISC][:], scalar=QSCALE[k], in1=qk_hi[:, k, :].bitcast(F32),
                                           op0=ALU.mult, op1=ALU.subtract).then_inc(emptied[MISC], 1)
                elif kind == "smax":
                    h, q = s[2:]
                    v.reduce_max(rowmax[:, h // HG, q, h % HG:h % HG + 1], content(t, s, SB)[:], AX).then_inc(emptied[SB], 1)
                elif kind == "mrow":
                    dve.wait_ge(mhi_done, s[2] + 1)
                    v.scalar_tensor_tensor(out=m_lo[:], in0=bank[MISC][0:HG, :], scalar=-1.0, in1=m_hi[:].bitcast(F32),
                                           op0=ALU.mult, op1=ALU.subtract).then_inc(emptied[MISC], 1)
                elif kind == "headsT":
                    g = s[2]
                    ps = content(t, s, MISC)[:].rearrange("p (q j c) -> p q j c", q=NT, j=HG)
                    v.reciprocal(rden[:], ps[:, :, :, DK]).then_inc(rden_done, 1)
                    dve.wait_ge(rden_done, g + 1)
                    v.tensor_tensor(heads[:, :, 32 * g:32 * g + 32].rearrange("p q (j c) -> p q j c", j=HG), ps[:, :, :, 0:DK],
                                    rden[:].unsqueeze(3).to_broadcast([P, NT, HG, DK]), ALU.mult).then_inc(emptied[MISC], 1)

            def route(t, s):
                layer = s[0]
                sc, w, sig = scores_sb[layer], wtmp[layer], gate_math[layer]
                v.tensor_copy(sc[:], content(t, s, MISC)[:, 0:NT * E].rearrange("p (q e) -> p q e", q=NT)).then_inc(emptied[MISC], 1)
                dve.wait_ge(emptied[MISC], t.fill(s, MISC, 0))
                tops = top_done[layer]
                for q in range(NT):
                    v.max(top[layer][:, q, :], sc[:, q, :]).then_inc(tops, 1)
                for q in range(NT):
                    dve.wait_ge(tops, q + 1)
                    v.max_index(topi[layer][:, q, :], top[layer][:, q, :], sc[:, q, :]).then_inc(tops, 1)
                dve.wait_ge(tops, NT)
                if layer == 0:
                    v.tensor_tensor(w[:, 0, :], top[0][:, :, 1], top[0][:, :, 0], ALU.subtract).then_inc(gate_pre[0], 1)
                else:
                    v.tensor_scalar(w[:, 0:2, :], top[1][:, :, 0:2].rearrange("p q k -> p k q"), -1.0, None, ALU.mult).then_inc(gate_pre[1], 1)
                dve.wait_ge(gate_exp[layer], 1)
                if layer == 0:
                    v.tensor_scalar(w[:, 3, :], w[:, 2, :], 1.0, None, ALU.add).then_inc(sig, 1)
                    dve.wait_ge(sig, 1)
                    v.reciprocal(w[:, 4, :], w[:, 3, :]).then_inc(sig, 1)
                    dve.wait_ge(sig, 2)
                    v.tensor_scalar(w[:, 4, :], w[:, 4, :], 0.5, None, ALU.mult).then_inc(sig, 1)
                    dve.wait_ge(sig, 3)
                    v.tensor_tensor(w[:, 5, :], w[:, 2, :], w[:, 4, :], ALU.mult).then_inc(sig, 1)
                else:
                    v.tensor_scalar(w[:, 2:4, :], w[:, 2:4, :], 1.0, None, ALU.add).then_inc(sig, 1)
                    dve.wait_ge(sig, 1)
                    v.reciprocal(w[:, 4:6, :], w[:, 2:4, :]).then_inc(sig, 1)
                n = 4 if layer == 0 else 2
                dve.wait_ge(sig, n)
                dve.wait_ge(tops, 2 * NT)
                shape = [P, NT, E]
                experts = iota_sb[:].unsqueeze(1).to_broadcast(shape)
                for k in range(2):
                    pick = pick_sb[layer][:, k]
                    v.tensor_tensor(pick, experts, topi[layer][:, :, k:k + 1].to_broadcast(shape), ALU.is_equal).then_inc(sig, 1)
                    dve.wait_ge(sig, n + 2 * k + 1)
                    v.tensor_tensor(pick, pick, w[:, 4 + k, :].unsqueeze(2).to_broadcast(shape), ALU.mult).then_inc(sig, 1)
                dve.wait_ge(sig, n + 4)
                v.tensor_tensor(gatew[layer][:], pick_sb[layer][:, 0], pick_sb[layer][:, 1], ALU.add).then_inc(gatew_done[layer], 1)
                dve.wait_ge(gatew_done[layer], 1)

            turns(dve, step)


def _layout(a, np):
    f = lambda v: np.ascontiguousarray(v, dtype=np.float32)
    p = "L0_attn_"
    kone = np.zeros(P)
    for j in range(HG):
        kone[32 * j + 24:32 * j + 26] = 1.0
    cols = [a[p + f"time_maa_{n}"] for n in "xwkvrg"] + [a[p + "time_decay"], a[p + "time_faaaa"].reshape(C), a[p + "ln_w"], a[p + "ln_b"], kone]
    square = [a[p + n] for n in ("Wr", "Wk", "Wv", "Wg", "Wo")]
    square += [a[f"L1_attn_W_{n}"].transpose(1, 0, 2).reshape(C, C) for n in ("query", "key", "val")] + [a["L1_attn_W_out"].reshape(C, C)]
    w3 = a["L0_ffn_W3"].transpose(2, 0, 1).reshape(FT, P, E, C).transpose(1, 2, 0, 3)
    up1 = np.concatenate([a["L1_ffn_w_in_eDF"], a["L1_ffn_w_in_shared_FD"].T[None]]).transpose(1, 0, 2)
    gate1 = np.concatenate([a["L1_ffn_w_swiglu_eDF"], a["L1_ffn_w_swiglu_FD"].T[None]]).transpose(1, 0, 2)
    down1 = np.concatenate([a["L1_ffn_w_out_eFD"], a["L1_ffn_w_out_shared_DF"].T[None]]).reshape(E1, FT, P, C).transpose(2, 0, 1, 3)
    s, u = np.arange(HS)[:, None], np.arange(HS)[None, :]
    masks = [s == u]
    for hs in (1,) + HALVES:
        masks.append((s // (2 * hs) == u // (2 * hs)) & (s % (2 * hs) < hs) & (u % (2 * hs) >= hs))
    masks = np.tile(np.stack(masks, 1), (2, 1, 1))
    select = np.zeros((P, 4, P))
    for g in range(NG):
        for j in range(HG):
            for d in range(DK):
                row = (HG * g + j) * DK + d
                for n, parts in enumerate(((0, 2), (1,), (0, 1), (2,))):
                    for part in parts:
                        select[row, n, 32 * j + DK * part + d] = 1.0
    return {
        "x": f(a["L0_attn_x"]), "cols": f(np.stack(cols, 1)), "mix1": f(a[p + "time_maa_w1"]), "square": f(np.stack(square, 1)),
        "mix2": f(a[p + "time_maa_w2"].reshape(5 * 32, C)), "dec1": f(a[p + "time_decay_w1"]), "dec2": f(a[p + "time_decay_w2"]),
        "up0": f(a["L0_ffn_W1"].transpose(2, 0, 1)), "gate0": f(a["L0_ffn_W2"].transpose(2, 0, 1)), "down0": f(w3),
        "up1": f(up1), "gate1": f(gate1), "down1": f(down1),
        "routers": f(np.stack([a["L0_ffn_Wg"].T, a["L1_ffn_router_DE"]], 1)), "ident": f(np.eye(P)), "masks": f(masks),
        "select": f(select), "iota": f(np.tile(np.arange(E), (P, 1))),
    }


def kernel(**inputs):
    import numpy as np
    from concourse import bacc
    from concourse.bass_utils import run_bass_kernel_spmd

    nc = bacc.Bacc("TRN2", target_bir_lowering=False, num_devices=1)
    arrays = _layout({k: np.asarray(v) for k, v in inputs.items()}, np)
    args = [nc.dram_tensor(n, v.shape, F32, kind="ExternalInput").ap() for n, v in arrays.items()]
    out = nc.dram_tensor("out", (B, T, C), F32, kind="ExternalOutput").ap()
    two_layer_kernel(nc, *args, out)
    return run_bass_kernel_spmd(nc, [arrays], core_ids=[0]).results[0]["out"]
```

```python
from contextlib import ExitStack

import concourse.bass as bass
import numpy as np
from concourse import mybir

F32 = mybir.dt.float32
F32R = mybir.dt.float32r
I32 = mybir.dt.int32
U32 = mybir.dt.uint32
ALU = mybir.AluOpType
ACT = mybir.ActivationFunctionType
AX = mybir.AxisListType.X

P = 128
B, T, C = 16, 512, 128
NT = T // P
NH0, HS = 2, 64
E = 8
FT = 2
E1 = E + 1
NH, DK = 16, 8
HG = 4
NG = NH // HG
LN_EPS = 1e-5
GN_EPS = 64e-5
DECAY_MAX = 110.0
HALVES = (2, 4, 8, 16, 32)
VCOLS = 32
RING = 3

MIX_W, MIX_K, MIX_V, MIX_R, MIX_G = range(5)
COL_X, COL_MIX, COL_DECAY, COL_U, COL_LNW, COL_LNB, COL_KONE = 0, 1, 6, 7, 8, 9, 10
WR, WK, WV, WG, WO, AQ, AK, AV, AO = range(9)
QSCALE = (DK ** -0.5, 1.0)
LEVEL = {"cross128": len(HALVES), "cross256": len(HALVES) + 1, "cross512": len(HALVES) + 2}


ATTN_START, ATTN_EVERY, SOFT_AFTER = 6.0, 1.84, 4.3
UPS_START, UPS_EVERY, GATES_BEFORE, DOWN_AFTER = 1.99, 4.3, 8.08, 6.79
MIX_START, MIX_EVERY = 1.0, 5.0
STACK_BEFORE, PV_AFTER, MROW_AFTER, HEADS_AFTER = 6.0, 2.0, 1.0, 3.87
FINISH_AFTER, NORM0_AFTER, ROUTE0_AFTER, NORM1_AFTER, ROUTE1_AFTER = 2.0, 1.0, 2.0, 2.0, 2.0
LATER = {'dve': {'up': 1.0, 'level': -0.3, 'down': 0.5}, 'act': {'level': -3.9}, 'pool': {'lora': 3.6, 'level': 1.2}, 'pe': {'down': 0.1, 'soft': -0.2}, 'sp': {}}


def due_times():
    due = {(0, "keep"): 0.0, (1, "keep"): 0.1, (0, "load"): 0.2}
    mix = [(0, "mixin"), (0, "lora", MIX_W), (0, "lora", MIX_K), (0, "decay"), (0, "lora", MIX_R),
           (0, "proj", WK), (0, "lora", MIX_V), (0, "proj", WR), (0, "lora", MIX_G), (0, "value"),
           (0, "proj", WG), (0, "diag"), (0, "pair")]
    mix += [(0, "level", n) for n in range(len(HALVES))]
    mix += [(0, "cross128"), (0, "cross256"), (0, "cross512", 0), (0, "cross512", 1), (0, "wkv"), (0, "wkvT")]
    for i, s in enumerate(mix):
        due[s] = MIX_START + MIX_EVERY * i
    start = ATTN_START
    for i, s in enumerate([(1, "qk", AQ), (1, "qk", AK), (1, "attnv")]):
        due[s] = 0.3 + 0.1 * i
    for g in range(NG):
        for i in range(HG * NT):
            at = start + ATTN_EVERY * (HG * NT * g + i)
            soft_at = at + ATTN_EVERY * HG * NT + SOFT_AFTER
            due[1, "smax", HG * g + i // NT, i % NT] = at
            due[1, "soft", HG * g + i % HG, i // HG] = soft_at
            if i % HG == HG - 1:
                due[1, "pv", g, i // HG] = soft_at + PV_AFTER
        due[1, "stack", AQ, g] = max(start + ATTN_EVERY * HG * NT * g - STACK_BEFORE, 0.6)
        due[1, "stack", AK, g] = max(start + ATTN_EVERY * HG * NT * g - STACK_BEFORE / 2, 0.7)
        due[1, "mrow", g] = at + MROW_AFTER
        due[1, "headsT", g] = soft_at + PV_AFTER + HEADS_AFTER
    due[1, "outT"] = due[1, "headsT", NG - 1] + 1
    experts = [(1, e) for e in [E] + list(range(E))] + [(0, e) for e in range(E)]
    for i, (layer, e) in enumerate(experts):
        at = UPS_START + UPS_EVERY * FT * i
        for f in range(FT):
            due[layer, "up", e, f] = at + UPS_EVERY * f
        due[layer, "down", e] = at + UPS_EVERY * (FT - 1) + DOWN_AFTER
        if layer == 1 and e < E:
            due[layer, "gates", e] = max(at - GATES_BEFORE, 0.0)
    due[1, "mixed"] = due[1, "down", E - 1] + 1
    due[1, "finish"] = due[1, "outT"] + 1
    due[0, "finish"] = max(due[0, "wkvT"], due[0, "down", E - 1]) + FINISH_AFTER
    due[0, "norm"] = max(due[0, "wkvT"], due[0, "up", E - 1, FT - 1]) + NORM0_AFTER
    due[0, "route"] = max(due[0, "norm"], due[0, "down", E - 1]) + ROUTE0_AFTER
    due[1, "norm"] = due[0, "finish"] + NORM1_AFTER
    due[1, "route"] = due[1, "norm"] + ROUTE1_AFTER
    return due


DUE = due_times()
PLAN = sorted(DUE, key=lambda s: DUE[s])
MISC = ("mix", "attn")
HB, GB, YB, SB, TB, VB = "h", "g", "y", "s", "st", "pv"
BANKS = MISC + (HB, GB, YB, SB, TB, VB)


def fills(step):
    layer, kind = step[:2]
    if kind == "up":
        return [HB, GB]
    if kind == "down":
        return [YB] if layer == 0 or step[2] == E - 1 else []
    if kind == "smax":
        return [SB]
    if kind == "soft":
        return [TB]
    if kind == "pv":
        return [VB] if step[3] == 0 else []
    if kind in ("keep", "load", "mixed"):
        return []
    twice = ((1, "route"), (0, "mixin"), (0, "decay"))
    return [MISC[layer]] * (2 if step[:2] in twice else 1)


def part(step):
    layer, kind = step[:2]
    return ("ready" if kind in ("load", "norm", "route") else "layer") + str(layer)


class Turn:

    def __init__(self, number, parts):
        self.seq = (number, number - 1)
        self.steps = [s for s in PLAN if part(s) in parts]
        self.ups = [s for s in self.steps if s[1] == "up"]
        self.before, count = {}, {b: 0 for b in BANKS}
        for s in self.steps:
            self.before[s] = dict(count)
            for b in fills(s):
                count[b] += 1

    def order(self, engine):
        return sorted(self.steps, key=lambda s: DUE[s] + LATER[engine].get(s[1], 0.0))

    def fill(self, step, bank, n=0):
        return self.before[step][bank] + n + 1


def two_layer_kernel(nc, x, cols, mix1, square, mix2, dec1, dec2, up0, gate0, down0, up1, gate1, down1,
                     routers, ident, masks, select, iota, out):
    with ExitStack() as ctx:
        def sb(name, shape, dt=F32):
            return ctx.enter_context(nc.sbuf_tensor(name, shape, dt))

        def sem(name):
            return ctx.enter_context(nc.semaphore(name))

        def tiles(tensor):
            return tensor[:].rearrange("p (q c) -> p q c", q=NT)

        cols_sb = sb("cols_sb", [P, 11])
        mix1_sb = sb("mix1_sb", [P, 160])
        sq = sb("sq", [P, 9, C])
        mix2_sb = sb("mix2_sb", [P, C])
        mix2g_sb = sb("mix2g_sb", [32, C])
        dec1_sb = sb("dec1_sb", [P, 64])
        dec2_sb = sb("dec2_sb", [64, C])
        up_sb = [sb("up0_sb", [P, E, 256]), sb("up1_sb", [P, E1, 256])]
        gate_sb = [sb("gate0_sb", [P, E, 256]), sb("gate1_sb", [P, E1, 256])]
        down_sb = [sb("down0_sb", [P, E, FT, C]), sb("down1_sb", [P, E1, FT, C])]
        router_sb = sb("router_sb", [P, 2, E])
        ident_sb = sb("ident_sb", [P, P])
        masks_sb = sb("masks_sb", [P, 7, HS])
        select_sb = sb("select_sb", [P, 4, P], F32R)
        iota_sb = sb("iota_sb", [P, E])
        ones_sb = sb("ones_sb", [P, P])
        power_sb = sb("power_sb", [P, 8])

        stats = [sb(f"stats{i}", [P, NT, 6]) for i in range(2)]
        moments = [sb(f"moments{i}", [P, NT, 2]) for i in range(2)]
        vareps = [sb(f"vareps{i}", [P, NT]) for i in range(2)]
        rstd = [sb(f"rstd{i}", [P, NT]) for i in range(2)]
        xn = [sb(f"xn{i}", [P, NT, C]) for i in range(2)]
        xnT0 = sb("xnT0", [P, 1 + T])
        xnT1 = sb("xnT1", [P, T])
        xnT = (xnT0[:, 1:], xnT1[:])
        top = [sb(f"top{i}", [P, NT, 8]) for i in range(2)]
        scores_sb = [sb(f"scores{i}", [P, NT, E]) for i in range(2)]
        topi = [sb(f"topi{i}", [P, NT, 8], U32) for i in range(2)]
        wtmp = [sb(f"wtmp{i}", [P, 6, NT]) for i in range(2)]
        gatew = [sb(f"gatew{i}", [P, NT, E]) for i in range(2)]
        pick_sb = [sb(f"pick{i}", [P, 2, NT, E]) for i in range(2)]
        th = sb("th", [P, 2, T])
        hid = sb("hid", [P, 4, T])

        x_next = sb("x_next", [P, NT, C])
        x_sb = sb("x_sb", [P, NT, C])
        shiftT = sb("shiftT", [P, T])
        p128 = shiftT[0:HS, :].rearrange("p (q h c) -> p q h c", q=NT, h=NH0)
        xxxT = sb("xxxT", [P, T])
        elw, gth = xxxT, xxxT
        pdiag = xxxT[:].rearrange("p (q h c) -> p q h c", q=NT, h=NH0)
        mixa = sb("mixa", [P, T])
        zT = mixa
        gT = sb("gT", [P, T])
        mixb = gT[0:32, :]
        elwc = sb("elwc", [P, T])
        dec_h, ynT = elwc[0:64, :], elwc
        moved = sb("moved", [P, 2, T])
        diff = moved
        th_f0 = moved[:, 0, :].rearrange("p (q c) -> p q c", q=NT)
        xmixT = sb("xmixT", [P, 3, T])
        p512 = xmixT[:, 0:2, :].rearrange("p h (c n) -> p h c n", c=2)
        p256 = xmixT[:, 2, :].rearrange("p (m h c) -> p m h c", m=2, h=NH0)
        cum = sb("cum", [P, NT, P + 1])
        tot01 = sb("tot01", [P, 1])
        rT = sb("rT", [P, T])
        kT = sb("kT", [P, T])
        urT = sb("urT", [P, T])
        v0 = sb("v0", [P, NT, C])
        expd = sb("expd", [P, 2, T])
        q2_0 = expd[:, 0, :].rearrange("p (q c) -> p q c", q=NT)
        rk = sb("rk", [P, 2, T])
        gstats = sb("gstats", [P, NT * NH0, 6])
        gmom = sb("gmom", [P, NT * NH0, 2])
        gvar = sb("gvar", [P, NT * NH0])
        grstd = sb("grstd", [P, NT * NH0])
        yn = xn[0]
        acc0 = sb("acc0", [P, NT, C])
        ytmp = sb("ytmp", [P, 2, NT, C])
        x1 = sb("x1", [P, NT, C])

        x1b = sb("x1b", [P, NT, C])
        gw_hi = sb("gw_hi", [E, T], F32R)
        gw_lo = sb("gw_lo", [E, T], F32R)
        unit_sb = sb("unit_sb", [E, E], F32R)
        xg = sb("xg", [P, 2, T])
        qk_hi = sb("qk_hi", [P, 2, T], F32R)
        qk_lo = sb("qk_lo", [P, 2, T], F32R)
        qs = sb("qs", [P, RING, T], F32R)
        ks = sb("ks", [P, RING, T], F32R)
        v1 = sb("v1", [P, NT, NH, VCOLS])
        rowmax = sb("rowmax", [P, NG, NT, HG])
        m_hi = sb("m_hi", [HG, T], F32R)
        m_lo = sb("m_lo", [HG, T], F32R)
        probs = sb("probs", [P, 2, HG, T])
        oT = sb("oT", [P, T])
        headsT_sb = oT
        rden = sb("rden", [P, NT, HG])
        heads = sb("heads", [P, NT, C])
        out_sb = heads
        q1_1 = sb("q1_1", [P, NT, C])

        select_ld = probs[:, 0, 0, :].rearrange("p (n c) -> p n c", n=4)
        th_f = (th_f0, xg[:, 1, :].rearrange("p (q c) -> p q c", q=NT))
        q1 = (ytmp[:, 0], q1_1[:])
        q2 = (q2_0, xg[:, 0, :].rearrange("p (q c) -> p q c", q=NT))

        bank = {b: ctx.enter_context(nc.psum_tensor(f"bank_{b}", [P, T], F32)) for b in BANKS}
        s_load = sem("s_load")
        s_set = sem("s_set")
        s_select = sem("s_select")
        arrived = sem("arrived")
        clearing = sem("clearing")
        entered = sem("entered")
        left = sem("left")
        first_turn_sem = left.num + 1
        filled = {b: sem(f"filled_{b}") for b in BANKS}
        emptied = {b: sem(f"emptied_{b}") for b in BANKS}

        x_in = sem("x_in")
        out_done = sem("out_done")
        mrow_in = sem("mrow_in")
        L = (0, 1)
        st_done = [sem(f"stats_done{i}") for i in L]
        rstd_done = [sem(f"rstd_done{i}") for i in L]
        xn_done = [sem(f"xn_done{i}") for i in L]
        kept = [sem(f"kept{i}") for i in L]
        top_done = [sem(f"top_done{i}") for i in L]
        gate_pre = [sem(f"gate_pre{i}") for i in L]
        gate_exp = [sem(f"gate_exp{i}") for i in L]
        gate_math = [sem(f"gate_math{i}") for i in L]
        gatew_done = [sem(f"gatew_done{i}") for i in L]
        shift_done = sem("shift_done")
        xxx_done = sem("xxx_done")
        xmix_done = sem("xmix_done")
        elwc_done = sem("elwc_done")
        cum_done = sem("cum_done")
        tot_done = sem("tot_done")
        ur_done = sem("ur_done")
        gth_done = sem("gth_done")
        diff_done = sem("diff_done")
        expd_done = sem("expd_done")
        rows_done = sem("rows_done")
        rk_half = sem("rk_half")
        rk_done = sem("rk_done")
        gst_done = sem("gst_done")
        grstd_done = sem("grstd_done")
        yn_done = sem("yn_done")
        zT_done = sem("zT_done")
        acc_done = sem("acc_done")
        thf_done = [sem(f"thf_done{i}") for i in L]
        q1_done = sem("q1_done")
        x1_done = sem("x1_done")
        th_done = [sem(f"th_done{i}") for i in L]
        down_done = [sem(f"down_done{i}") for i in L]
        qkhi_done = sem("qkhi_done")
        gwhi_done = sem("gwhi_done")
        pv_done = sem("pv_done")
        mhi_done = sem("mhi_done")
        rden_done = sem("rden_done")
        out_ready = sem("out_ready")

        loads = [(cols_sb[:], cols), (mix1_sb[:], mix1), (sq[:], square), (mix2_sb[:], mix2[0:P, :]),
                 (mix2g_sb[:], mix2[P:160, :]), (dec1_sb[:], dec1), (dec2_sb[:], dec2),
                 (router_sb[:], routers), (ident_sb[:], ident), (masks_sb[:], masks), (select_ld, select),
                 (iota_sb[:], iota), (up_sb[0][:], up0), (gate_sb[0][:], gate0), (down_sb[0][:], down0),
                 (up_sb[1][:], up1), (gate_sb[1][:], gate1), (down_sb[1][:], down1)]
        NSET = 6
        ups = [s for s in PLAN if s[1] == "up"]
        downs = [[s for s in PLAN if s[:2] == (i, "down")] for i in L]
        loras = [s[2] for s in PLAN if s[1] == "lora"]

        def up_no(s):
            return [u for u in ups if u[0] == s[0]].index(s)

        def hid_slot(s):
            return ups.index(s) % 4

        def down_no(s):
            return downs[s[0]].index((s[0], "down", s[2]))

        def lora_no(m):
            return loras.index(m)

        fenced = [s for s in PLAN if s[1] in ("diag", "pair", "level", "cross128", "cross256", "wkv")]

        def level_step(n):
            names = [(0, "diag"), (0, "pair")] + [(0, "level", k) for k in range(len(HALVES))] + [(0, "cross128"), (0, "cross256")]
            return names[n + 2]

        last_turn_sem = out_ready.num

        def turns(eng, name, step):
            run(eng, name, step, Turn(-1, ("ready0",)), 0)
            run(eng, name, step, Turn(0, ("layer0", "ready0", "ready1")), 1)
            with eng.Fori(1, B - 1) as i:
                run(eng, name, step, Turn(i, ("layer0", "layer1", "ready0", "ready1")), i + 1)
            run(eng, name, step, Turn(B - 1, ("layer0", "layer1", "ready1")), B)
            run(eng, name, step, Turn(B, ("layer1",)), None)

        def run(eng, name, step, turn, number):
            for s in turn.order(name):
                step(turn, s)
            if number is not None:
                eng.drain().then_inc(arrived, 1)
                if eng is nc.sync:
                    eng.wait_ge(arrived, number * 5 + 5)
                    eng.sem_inc(clearing, 1)
                    eng.sem_clear(range(first_turn_sem, last_turn_sem + 1))
                    eng.sem_inc(left, 1)
                else:
                    eng.wait_ge(left, number + 1)
                    eng.sem_inc(entered, 1)

        block = ctx.enter_context(nc.Block())

        @block.sync
        def _(sp):
            for dst, src in loads:
                sp.dma_start(dst, src).then_inc(s_load, 16)

            def step(t, s):
                layer, kind = s[:2]
                misc = MISC[layer]
                if kind == "load":
                    if (0, "keep") in t.steps:
                        sp.wait_ge(kept[0], 1)
                    sp.dma_start(x_next[:], x[t.seq[0] + 1].rearrange("(q p) c -> p q c", p=P)).then_inc(x_in, 16)
                elif kind == "mrow":
                    g = s[2]
                    sp.wait_ge(mhi_done, g + 1)
                    sp.dma_start(qs[24::32, g % RING, :].bitcast(F32), m_hi[:].bitcast(F32)).then_inc(mrow_in, 16)
                    sp.wait_ge(emptied[misc], t.fill(s, misc))
                    sp.dma_start(qs[25::32, g % RING, :].bitcast(F32), m_lo[:].bitcast(F32)).then_inc(mrow_in, 16)
                elif (layer, kind) == (1, "finish"):
                    sp.wait_ge(out_ready, 1)
                    sp.dma_start(out[t.seq[1]].rearrange("(q p) c -> p q c", p=P), out_sb[:]).then_inc(out_done, 16)
                    sp.wait_ge(out_done, 16)

            turns(sp, "sp", step)

        @block.tensor
        def _(pe):
            mm = nc.tensor.matmul

            def room(t, s, b, n=0):
                if t.fill(s, b, n) > 1:
                    pe.wait_ge(emptied[b], t.fill(s, b, n) - 1)
                return bank[b]

            def fence(s, last):
                last.then_inc(rows_done, 1)
                pe.wait_ge(rows_done, fenced.index(s) + 1)

            def transposes(dst, src):
                for q in range(NT):
                    last = nc.tensor.transpose(dst[:, q * P:(q + 1) * P], src[:, q, :], ident_sb[:])
                return last

            def step(t, s):
                layer, kind = s[:2]
                misc = MISC[layer]
                if kind == "norm":
                    pe.wait_ge(xn_done[layer], NT)
                    transposes(room(t, s, misc), xn[layer]).then_inc(filled[misc], 1)
                elif kind == "route":
                    pe.wait_ge(emptied[misc], t.fill((layer, "norm"), misc))
                    ps = room(t, s, misc)
                    for q in range(NT):
                        last = mm(ps[:, q * E:(q + 1) * E], xnT[layer][:, q * P:(q + 1) * P], router_sb[:, layer, :],
                                  start=True, stop=True)
                    last.then_inc(filled[misc], 1)
                    if layer == 1:
                        pe.wait_ge(gatew_done[1], 1)
                        ps = room(t, s, misc, 1)
                        for q in range(NT):
                            last = nc.tensor.transpose(ps[0:E, q * P:(q + 1) * P], gatew[1][:, q, :], ident_sb[:])
                        last.then_inc(filled[misc], 1)
                elif kind == "gates":
                    ps, one = room(t, s, misc), unit_sb[:, s[2]:s[2] + 1].to_broadcast([E, P])
                    mm(ps[:], one, gw_hi[:], start=True, stop=False)
                    mm(ps[:], one, gw_lo[:], start=False, stop=True).then_inc(filled[misc], 1)
                elif kind == "up":
                    e, f = s[2:]
                    if layer == 1 and e < E:
                        pe.wait_ge(emptied[MISC[1]], t.fill((1, "gates", e), MISC[1]))
                    rhs = xnT[layer] if layer == 0 or e == E else xg[:, e % 2, :]
                    for b, w in zip(fills(s), (up_sb[layer], gate_sb[layer])):
                        mm(room(t, s, b)[:], w[:, e, f * P:(f + 1) * P], rhs, start=True, stop=True).then_inc(filled[b], 1)
                elif kind == "down":
                    e, n = s[2], down_no(s)
                    pe.wait_ge(emptied[GB], t.fill((layer, "up", e, FT - 1), GB))
                    if layer == 0 or n == 0:
                        room(t, s if layer == 0 else (1, "down", E - 1), YB)
                    for q in range(NT):
                        for f in range(FT):
                            start = f == 0 if layer == 0 else n == q == f == 0
                            last = mm(bank[YB][:, q * P:(q + 1) * P],
                                      hid[:, hid_slot((layer, "up", e, f)), q * P:(q + 1) * P], down_sb[layer][:, e, f, :],
                                      start=start, stop=f == FT - 1 and (layer == 0 or n == E), skip_group_check=True)
                    last.then_inc(down_done[layer], 1)
                elif kind == "mixin":
                    pe.wait_ge(xxx_done, 1)
                    mm(room(t, s, misc)[:], mix1_sb[:, 0:P], xxxT[:], start=True, stop=True).then_inc(filled[misc], 1)
                    mm(room(t, s, misc, 1)[0:32, :], mix1_sb[:, P:160], xxxT[:], start=True, stop=True).then_inc(filled[misc], 1)
                elif kind == "lora":
                    m = s[2]
                    pe.wait_ge(emptied[MISC[0]], t.fill((0, "mixin"), MISC[0], 1))
                    lhsT, rhs = (mix2g_sb[:], mixb) if m == 4 else (mix2_sb[32 * m:32 * m + 32, :], mixa[32 * m:32 * m + 32, :])
                    mm(room(t, s, misc)[:], lhsT, rhs, start=True, stop=True).then_inc(filled[misc], 1)
                elif kind == "decay":
                    pe.wait_ge(xmix_done, lora_no(MIX_W) + 1)
                    mm(room(t, s, misc)[0:64, :], dec1_sb[:], xmixT[:, lora_no(MIX_W) % 3, :], start=True, stop=True).then_inc(filled[misc], 1)
                    pe.wait_ge(emptied[misc], t.fill(s, misc, 0))
                    mm(room(t, s, misc, 1)[:], dec2_sb[:], dec_h, start=True, stop=True).then_inc(filled[misc], 1)
                elif kind == "proj":
                    m = {WR: MIX_R, WK: MIX_K, WG: MIX_G}[s[2]]
                    pe.wait_ge(xmix_done, lora_no(m) + 1)
                    mm(room(t, s, misc)[:], sq[:, s[2], :], xmixT[:, lora_no(m) % 3, :], start=True, stop=True).then_inc(filled[misc], 1)
                elif kind == "value":
                    pe.wait_ge(xmix_done, lora_no(MIX_V) + 1)
                    ps = room(t, s, misc)
                    for q in range(NT):
                        last = mm(ps[:, q * P:(q + 1) * P], xmixT[:, lora_no(MIX_V) % 3, q * P:(q + 1) * P], sq[:, WV, :], start=True, stop=True)
                    last.then_inc(filled[misc], 1)
                elif kind == "attnv":
                    ps = room(t, s, misc)
                    for q in range(NT):
                        last = mm(ps[:, q * P:(q + 1) * P], xnT[1][:, q * P:(q + 1) * P], sq[:, AV, :], start=True, stop=True)
                    last.then_inc(filled[misc], 1)
                elif kind in ("diag", "pair", "level"):
                    if kind == "level":
                        pe.wait_ge(rk_done, s[2] + 1)
                        a = b = rk[:, s[2] % 2, :]
                    else:
                        pe.wait_ge(emptied[MISC[0]], t.fill((0, "proj", WK), MISC[0]))
                        pe.wait_ge(emptied[MISC[0]], t.fill((0, "proj", WR), MISC[0]))
                        if kind == "diag":
                            pe.wait_ge(ur_done, 1)
                        a, b = kT[:], (urT if kind == "diag" else rT)[:]
                    ps = room(t, s, misc)
                    for h in range(NH0):
                        for q in range(NT):
                            ch, o = slice(HS * h, HS * h + HS), (q * NH0 + h) * HS
                            for half in range(2):
                                tok = slice(q * P + HS * half, q * P + HS * half + HS)
                                last = mm(ps[HS * half:HS * half + HS, o:o + HS], a[ch, tok], b[ch, tok], start=True, stop=True)
                        if h == 0:
                            fence(s, last)
                    last.then_inc(filled[misc], 1)
                elif kind in ("cross128", "cross256", "cross512"):
                    n = LEVEL[kind]
                    pe.wait_ge(rk_done, n + 1)
                    ps, a = room(t, s, misc), rk[:, n % 2, :]
                    for h in ([s[2]] if kind == "cross512" else range(NH0)):
                        ch = slice(HS * h, HS * h + HS)
                        if kind == "cross128":
                            for q in range(NT):
                                o = (q * NH0 + h) * HS
                                last = mm(ps[0:HS, o:o + HS], a[ch, q * P:q * P + HS], a[ch, q * P + HS:(q + 1) * P], start=True, stop=True)
                        elif kind == "cross256":
                            for p in range(2):
                                o = (p * NH0 + h) * P
                                last = mm(ps[:, o:o + P], a[ch, 2 * p * P:(2 * p + 1) * P], a[ch, (2 * p + 1) * P:(2 * p + 2) * P],
                                          start=True, stop=True)
                        else:
                            for c in range(2):
                                last = mm(ps[:, c * 2 * P:(c + 1) * 2 * P], a[ch, c * P:(c + 1) * P], a[ch, 2 * P:4 * P], start=True, stop=True)
                        if h == 0 and kind != "cross512":
                            fence(s, last)
                    last.then_inc(filled[misc], 1)
                elif kind == "wkv":
                    pe.wait_ge(emptied[MISC[0]], t.fill((0, "value"), MISC[0]))
                    pe.wait_ge(emptied[MISC[0]], t.fill((0, "level", len(HALVES) - 1), MISC[0]))
                    pe.wait_ge(emptied[MISC[0]], t.fill((0, "cross512", 1), MISC[0]))
                    ps = room(t, s, misc)
                    for q in range(NT):
                        for h in range(NH0):
                            o, clear = ps[:, q * P + HS * h:q * P + HS * h + HS], q == h == 0
                            vv = v0[:, :, HS * h:HS * h + HS]
                            far = [(p256[:, q // 2, h, :], vv[:, q - 1, :])] if q % 2 else []
                            if q >= 2:
                                far += [(p512[:, h, c, (q - 2) * P:(q - 1) * P], vv[:, c, :]) for c in range(2)]
                            for a, b in far:
                                mm(o, a, b, start=False, stop=False, skip_group_check=True)
                            mm(o[0:HS], pdiag[0:HS, q, h, :], vv[0:HS, q, :], start=clear, stop=True, skip_group_check=True)
                            last = mm(o[HS:P], p128[:, q, h, :], vv[0:HS, q, :], start=clear, stop=False, skip_group_check=True)
                    fence(s, last)
                    for q in range(NT):
                        for h in range(NH0):
                            last = mm(ps[HS:P, q * P + HS * h:q * P + HS * h + HS], pdiag[HS:P, q, h, :],
                                      v0[HS:P, q, HS * h:HS * h + HS], start=False, stop=True, skip_group_check=True)
                    last.then_inc(filled[misc], 1)
                elif kind == "wkvT":
                    pe.wait_ge(yn_done, 1)
                    transposes(room(t, s, misc), yn).then_inc(filled[misc], 1)
                elif kind == "finish":
                    if layer == 0:
                        pe.wait_ge(zT_done, 1)
                    else:
                        pe.wait_ge(emptied[MISC[1]], t.fill((1, "outT"), MISC[1]))
                    ps, src = room(t, s, misc), (zT, headsT_sb)[layer]
                    for q in range(NT):
                        last = mm(ps[:, q * P:(q + 1) * P], src[:, q * P:(q + 1) * P], sq[:, (WO, AO)[layer], :], start=True, stop=True)
                    last.then_inc(filled[misc], 1)
                elif kind == "qk":
                    mm(room(t, s, misc)[:], sq[:, s[2], :], xnT[1], start=True, stop=True).then_inc(filled[misc], 1)
                elif kind == "stack":
                    k = s[2] - AQ
                    pe.wait_ge(emptied[MISC[1]], t.fill((1, "qk", s[2]), MISC[1]))
                    ps = room(t, s, misc)
                    r = slice(32 * s[3], 32 * s[3] + 32)
                    mm(ps[:], select_sb[r, 2 * k, :], qk_hi[r, k, :], start=True, stop=False)
                    mm(ps[:], select_sb[r, 2 * k + 1, :], qk_lo[r, k, :], start=False, stop=True).then_inc(filled[misc], 1)
                elif kind == "smax":
                    h, q = s[2:]
                    g, r = h // HG, 32 * (h % HG)
                    if (h % HG, q) == (0, 0):
                        pe.wait_ge(emptied[MISC[1]], t.fill((1, "stack", AK, g), MISC[1]))
                    mm(room(t, s, SB)[:], qs[r:r + 32, g % RING, q * P:(q + 1) * P], ks[r:r + 32, g % RING, :],
                       start=True, stop=True).then_inc(filled[SB], 1)
                elif kind == "mrow":
                    g = s[2]
                    pe.wait_ge(emptied[SB], t.fill((1, "smax", HG * g + HG - 1, NT - 1), SB))
                    ps = room(t, s, misc)
                    for q in range(NT):
                        last = nc.tensor.transpose(ps[0:HG, q * P:(q + 1) * P], rowmax[:, g, q, :], ident_sb[:])
                    last.then_inc(filled[misc], 1)
                elif kind == "soft":
                    h, k = s[2:]
                    g, r = h // HG, 32 * (h % HG)
                    if (h % HG, k) == (0, 0):
                        pe.wait_ge(mrow_in, 32 * (g + 1))
                    mm(room(t, s, TB)[:], ks[r:r + 32, g % RING, k * P:(k + 1) * P], qs[r:r + 32, g % RING, :],
                       start=True, stop=True).then_inc(filled[TB], 1)
                elif kind == "pv":
                    g, k = s[2:]
                    pe.wait_ge(emptied[MISC[1]], t.fill((1, "attnv"), MISC[1]))
                    pe.wait_ge(emptied[TB], t.fill((1, "soft", HG * g + HG - 1, k), TB))
                    ps = room(t, s, VB) if k == 0 else bank[VB]
                    for j in range(HG):
                        last = mm(ps[32 * j:32 * j + 32, :], v1[:, k, HG * g + j, :], probs[:, k % 2, j, :],
                                  start=k == 0, stop=k == NT - 1, skip_group_check=True)
                    last.then_inc(pv_done, 1)
                elif kind == "headsT":
                    pe.wait_ge(emptied[VB], t.fill((1, "pv", s[2], 0), VB))
                    ps = room(t, s, misc)
                    for q in range(NT):
                        last = nc.tensor.transpose(ps[:, q * P:(q + 1) * P], oT[:, q * P:(q + 1) * P], ident_sb[:])
                    last.then_inc(filled[misc], 1)
                elif kind == "outT":
                    pe.wait_ge(emptied[MISC[1]], t.fill((1, "headsT", NG - 1), MISC[1]))
                    transposes(room(t, s, misc), heads).then_inc(filled[misc], 1)

            pe.wait_ge(s_load, 16 * len(loads))
            pe.wait_ge(s_set, NSET)
            pe.wait_ge(s_select, 2)
            turns(pe, "pe", step)

        @block.scalar
        def _(act):
            A = nc.scalar.activation

            def content(t, s, b, n=0):
                act.wait_ge(filled[b], t.fill(s, b, n))
                return bank[b]

            def step(t, s):
                layer, kind = s[:2]
                misc = MISC[layer]
                if kind == "keep":
                    src, dst = ((x_next, x_sb), (x1, x1b))[layer]
                    A(dst[:], src[:], ACT.Copy).then_inc(kept[layer], 1)
                elif kind == "norm":
                    if (layer, "up", E - 1, FT - 1) in t.steps:
                        act.wait_ge(filled[GB], t.fill((layer, "up", E - 1, FT - 1), GB))
                        if layer == 0:
                            act.wait_ge(xmix_done, 5)
                        else:
                            act.wait_ge(emptied[misc], t.fill((1, "gates", E - 1), misc))
                    A(xnT[layer], content(t, s, misc)[:], ACT.Copy).then_inc(emptied[misc], 1)
                elif kind == "route":
                    w, n = wtmp[layer], layer + 1
                    act.wait_ge(gate_pre[layer], 1)
                    A(w[:, 2:2 + n, :], w[:, 0:n, :], ACT.Exp).then_inc(gate_exp[layer], 1)
                    if layer == 1:
                        A(gw_hi[:], content(t, s, misc, 1)[0:E, :], ACT.Copy).then_inc(gwhi_done, 1)
                elif kind == "up":
                    ba, bb = fills(s)
                    if t.fill(s, bb) > FT:
                        act.wait_ge(emptied[bb], t.fill(s, bb) - FT)
                    A(th[:, s[3], :], content(t, s, ba)[:], ACT.Tanh, scale=0.5).then_inc(th_done[layer], 1)
                elif kind == "mixed":
                    act.wait_ge(down_done[1], E + 1)
                    A(th_f[1], tiles(bank[YB]), ACT.Tanh, scale=0.25).then_inc(thf_done[1], 1)
                elif kind == "mixin":
                    A(mixa[:], content(t, s, misc)[:], ACT.Tanh).then_inc(emptied[misc], 1)
                    A(mixb, content(t, s, misc, 1)[0:32, :], ACT.Tanh).then_inc(emptied[misc], 1)
                elif kind == "decay":
                    A(dec_h, content(t, s, misc)[0:64, :], ACT.Tanh).then_inc(emptied[misc], 1)
                    A(elw[:], content(t, s, misc, 1)[:], ACT.Exp, bias=cols_sb[:, COL_DECAY:COL_DECAY + 1]).then_inc(emptied[misc], 1)
                elif kind == "proj":
                    if s[2] == WG:
                        A(gth[:], content(t, s, misc)[:], ACT.Tanh, scale=0.5).then_inc(gth_done, 1)
                    else:
                        A((rT if s[2] == WR else kT)[:], content(t, s, misc)[:], ACT.Copy).then_inc(emptied[misc], 1)
                elif kind == "value":
                    A(v0[:], tiles(content(t, s, misc)), ACT.Copy).then_inc(emptied[misc], 1)
                elif kind == "attnv":
                    A(v1[:, :, :, 0:DK], content(t, s, misc)[:].rearrange("p (q h k) -> p q h k", q=NT, h=NH),
                      ACT.Copy).then_inc(emptied[misc], 1)
                elif kind == "level":
                    decays(t, s[2])
                elif kind == "cross128":
                    decays(t, LEVEL[kind])
                    A(p128, content(t, s, misc)[0:HS, :].rearrange("p (q h c) -> p q h c", q=NT, h=NH0),
                      ACT.Copy).then_inc(emptied[misc], 1)
                elif kind == "cross256":
                    e = expd[:, LEVEL[kind] % 2, :].rearrange("p (q c) -> p q c", q=NT)
                    act.wait_ge(cum_done, NT)
                    act.wait_ge(rk_done, LEVEL[kind] - 1)
                    A(e[:, 1::2, :], cum[:, 1::2, 0:P], ACT.Exp).then_inc(expd_done, 1)
                    for q in (0, 2):
                        A(e[:, q, :], cum[:, q, 1:P + 1], ACT.Exp, bias=cum[:, q, P:P + 1], scale=-1.0).then_inc(expd_done, 1)
                    A(p256, content(t, s, misc)[:].rearrange("p (q h c) -> p q h c", q=2, h=NH0), ACT.Copy).then_inc(emptied[misc], 1)
                elif kind == "cross512":
                    if s[2] == 0:
                        e = expd[:, LEVEL[kind] % 2, :].rearrange("p (q c) -> p q c", q=NT)
                        act.wait_ge(tot_done, 1)
                        act.wait_ge(rk_done, LEVEL[kind] - 1)
                        A(e[:, 2, :], cum[:, 2, 0:P], ACT.Exp).then_inc(expd_done, 1)
                        A(e[:, 3, :], cum[:, 3, 0:P], ACT.Exp, bias=cum[:, 2, P:P + 1]).then_inc(expd_done, 1)
                        A(e[:, 1, :], cum[:, 1, 1:P + 1], ACT.Exp, bias=cum[:, 1, P:P + 1], scale=-1.0).then_inc(expd_done, 1)
                        A(e[:, 0, :], cum[:, 0, 1:P + 1], ACT.Exp, bias=tot01[:], scale=-1.0).then_inc(expd_done, 1)
                    A(p512[:, s[2]], content(t, s, misc)[:].rearrange("p (c n) -> p c n", c=2), ACT.Copy).then_inc(emptied[misc], 1)
                elif (layer, kind) == (0, "finish"):
                    act.wait_ge(acc_done, E - 1)
                    A(th_f[0], acc0[:], ACT.Tanh, scale=0.5).then_inc(thf_done[0], 1)
                elif kind == "qk":
                    k = s[2] - AQ
                    A(qk_hi[:, k, :], content(t, s, misc)[:], ACT.Copy, scale=QSCALE[k]).then_inc(qkhi_done, 1)
                elif kind == "stack":
                    ps = content(t, s, misc)
                    if s[3] >= RING:
                        act.wait_ge(filled[TB], t.fill((1, "soft", HG * (s[3] - RING + 1) - 1, NT - 1), TB))
                    if s[2] == AQ:
                        A(qs[:, s[3] % RING, :], ps[:], ACT.Copy).then_inc(emptied[misc], 1)
                    else:
                        A(ks[:, s[3] % RING, :], ps[:], ACT.Identity, bias=cols_sb[:, COL_KONE:COL_KONE + 1]).then_inc(emptied[misc], 1)
                elif kind == "mrow":
                    ps = content(t, s, misc)
                    if s[2] > 0:
                        act.wait_ge(mrow_in, 32 * s[2])
                    A(m_hi[:], ps[0:HG, :], ACT.Copy, scale=-1.0).then_inc(mhi_done, 1)
                elif kind == "soft":
                    h, k = s[2:]
                    ps = content(t, s, TB)
                    if h % HG == 0 and h // HG * NT + k >= 2:
                        act.wait_ge(pv_done, h // HG * NT + k - 1)
                    A(probs[:, k % 2, h % HG, :], ps[:], ACT.Exp).then_inc(emptied[TB], 1)
                elif kind == "pv" and s[3] == NT - 1:
                    g = s[2]
                    if g > 0:
                        act.wait_ge(filled[misc], t.fill((1, "headsT", g - 1), misc))
                    act.wait_ge(pv_done, NT * (g + 1))
                    A(oT[:], bank[VB][:], ACT.Copy).then_inc(emptied[VB], 1)
                elif kind == "outT":
                    A(headsT_sb[:], content(t, s, misc)[:], ACT.Copy).then_inc(emptied[misc], 1)

            def decays(t, n):
                act.wait_ge(diff_done, 2 * n + 2)
                if n >= 2:
                    act.wait_ge(rk_done, n - 1)
                A(expd[:, n % 2, :], diff[:, n % 2, :], ACT.Exp).then_inc(expd_done, 1)

            act.wait_ge(s_load, 16 * len(loads))
            A(select_sb[:], select_ld, ACT.Copy).then_inc(s_select, 1)
            A(unit_sb[:], ident_sb[0:E, 0:E], ACT.Copy).then_inc(s_select, 1)
            act.wait_ge(s_set, NSET)
            turns(act, "act", step)

        @block.gpsimd
        def _(pool):
            tt = nc.gpsimd.tensor_tensor

            def step(t, s):
                layer, kind = s[:2]
                misc = MISC[layer]
                if kind == "norm":
                    pool.wait_ge(st_done[layer], 2 * NT + 1)
                    tt(rstd[layer][:], vareps[layer][:], power_sb[:, 0:NT], ALU.pow).then_inc(rstd_done[layer], 1)
                elif kind == "mixin":
                    tt(shiftT[:], xnT0[:, 0:T], xnT[0], ALU.subtract).then_inc(shift_done, 1)
                elif kind == "lora":
                    m = s[2]
                    pool.wait_ge(emptied[misc], t.fill(s, misc))
                    n = lora_no(m)
                    if n >= 3:
                        user = {MIX_W: (0, "decay"), MIX_K: (0, "proj", WK)}[loras[n - 3]]
                        pool.wait_ge(filled[MISC[0]], t.fill(user, MISC[0]))
                    tt(xmixT[:, n % 3, :], moved[:, n % 2, :], xnT[0], ALU.add).then_inc(xmix_done, 1)
                elif kind == "diag":
                    differences(t, 0)
                elif kind == "level":
                    differences(t, s[2] + 1)
                    decayed(t, s[2])
                elif kind == "cross128":
                    decayed(t, LEVEL[kind])
                elif kind == "cross256":
                    n = LEVEL[kind]
                    pool.wait_ge(expd_done, n + 3)
                    pool.wait_ge(filled[MISC[0]], t.fill(level_step(n - 2), MISC[0]))
                    for k, src in ((0, kT), (1, rT)):
                        a, b, c = (v.rearrange("p (m k c) -> p m k c", m=2, k=2)[:, :, k, :] for v in (rk[:, n % 2, :], src[:], expd[:, n % 2, :]))
                        last = tt(a, b, c, ALU.mult)
                        if k == 0:
                            last.then_inc(rk_half, 1)
                    last.then_inc(rk_done, 1)
                elif kind == "cross512" and s[2] == 0:
                    n = LEVEL[kind]
                    pool.wait_ge(expd_done, n + 6)
                    pool.wait_ge(filled[MISC[0]], t.fill(level_step(n - 2), MISC[0]))
                    tt(rk[:, n % 2, 0:2 * P], kT[:, 0:2 * P], expd[:, n % 2, 0:2 * P], ALU.mult).then_inc(rk_half, 1)
                    tt(rk[:, n % 2, 2 * P:T], rT[:, 2 * P:T], expd[:, n % 2, 2 * P:T], ALU.mult).then_inc(rk_done, 1)
                elif kind == "wkv":
                    pool.wait_ge(gst_done, 2 * NT * NH0 + 1)
                    tt(grstd[:], gvar[:], power_sb[:], ALU.pow).then_inc(grstd_done, 1)
                elif (layer, kind) == (0, "down"):
                    n = down_no(s)
                    if n > 0:
                        pool.wait_ge(emptied[YB], t.fill(s, YB))
                        if n > 1:
                            pool.wait_ge(acc_done, n - 1)
                        tt(acc0[:], acc0[:], ytmp[:, n % 2], ALU.add).then_inc(acc_done, 1)
                elif kind == "finish":
                    pool.wait_ge(emptied[misc], t.fill(s, misc))
                    pool.wait_ge(kept[layer], 1)
                    if layer == 0 and (1, "keep") in t.steps:
                        pool.wait_ge(kept[1], 1)
                    dst, src, done = ((x1, x_sb, x1_done), (out_sb, x1b, out_ready))[layer]
                    tt(dst[:], src[:], q2[layer], ALU.add).then_inc(done, 1)

            def differences(t, n):
                if n > len(HALVES):
                    return
                hs = (HALVES + (HS,))[n]
                if n == 0:
                    pool.wait_ge(cum_done, NT)
                    pool.wait_ge(xmix_done, 5)
                if n >= 2:
                    pool.wait_ge(expd_done, n - 1)
                shape = [P, NT, P // (2 * hs), hs]
                before, upto = (cum[:, :, o:o + P].rearrange("p q (n a s) -> p q n a s", a=2, s=hs) for o in (0, 1))
                d = diff[:, n % 2, :].rearrange("p (q n a s) -> p q n a s", q=NT, a=2, s=hs)
                middle = before[:, :, :, 1, 0:1].to_broadcast(shape)
                tt(d[:, :, :, 0, :], middle, upto[:, :, :, 0, :], ALU.subtract).then_inc(diff_done, 1)
                tt(d[:, :, :, 1, :], before[:, :, :, 1, :], middle, ALU.subtract).then_inc(diff_done, 1)

            def decayed(t, n):
                hs = (HALVES + (HS,))[n]
                pool.wait_ge(expd_done, n + 1)
                if n == 0:
                    pool.wait_ge(emptied[MISC[0]], t.fill((0, "proj", WR), MISC[0]))
                    pool.wait_ge(emptied[MISC[0]], t.fill((0, "proj", WK), MISC[0]))
                if n >= 2:
                    pool.wait_ge(filled[MISC[0]], t.fill(level_step(n - 2), MISC[0]))
                for k, src, done in ((0, kT, rk_half), (1, rT, rk_done)):
                    a, b, c = (v.rearrange("p (m a s) -> p m a s", a=2, s=hs)[:, :, k, :] for v in (rk[:, n % 2, :], src[:], expd[:, n % 2, :]))
                    tt(a, b, c, ALU.mult).then_inc(done, 1)

            pool.wait_ge(s_load, 16 * len(loads))
            pool.wait_ge(s_set, NSET)
            turns(pool, "pool", step)

        @block.vector
        def _(dve):
            v = nc.vector
            v.memset(ones_sb[:], 1.0).then_inc(s_set, 1)
            v.memset(power_sb[:], -0.5).then_inc(s_set, 1)
            v.memset(xnT0[:, 0:1], 0.0).then_inc(s_set, 1)
            v.memset(cum[:, :, 0:1], 0.0).then_inc(s_set, 1)
            v.memset(v1[:], 0.0).then_inc(s_set, 1)
            dve.wait_ge(s_set, 5)
            v.memset(v1[:, :, :, DK:DK + 1], 1.0).then_inc(s_set, 1)

            def content(t, s, b, n=0):
                dve.wait_ge(filled[b], t.fill(s, b, n))
                return bank[b]

            def col(n):
                return cols_sb[:, n:n + 1]

            def row_mean_var(t, src, layer):
                sig = st_done[layer]
                for q in range(NT):
                    v.bn_stats(stats[layer][:, q, :], src[:, q, :]).then_inc(sig, 1)
                for q in range(NT):
                    dve.wait_ge(sig, q + 1)
                    v.bn_aggr(moments[layer][:, q, :], stats[layer][:, q, :]).then_inc(sig, 1)
                dve.wait_ge(sig, 2 * NT)
                v.tensor_scalar(vareps[layer][:], moments[layer][:, :, 1], LN_EPS, None, ALU.add).then_inc(sig, 1)

            def step(t, s):
                layer, kind = s[:2]
                misc = MISC[layer]
                if kind == "norm":
                    dve.wait_ge(*((x_in, 16), (x1_done, 1))[layer])
                    src = (x_next, x1)[layer]
                    row_mean_var(t, src, layer)
                    dve.wait_ge(rstd_done[layer], 1)
                    if (0, "wkvT") in t.steps and layer == 0:
                        dve.wait_ge(filled[misc], t.fill((0, "wkvT"), misc))
                    for q in range(NT):
                        v.tensor_scalar(xn[layer][:, q, :], src[:, q, :], moments[layer][:, q, 0:1], rstd[layer][:, q:q + 1],
                                        ALU.subtract, ALU.mult).then_inc(xn_done[layer], 1)
                elif kind == "route":
                    route(t, s)
                elif kind == "gates":
                    e = s[2]
                    ps = content(t, s, misc)
                    if e >= 2:
                        dve.wait_ge(filled[GB], t.fill((1, "up", e - 2, 1), GB))
                    v.tensor_tensor(xg[:, e % 2, :], ps[:], xnT[1], ALU.mult).then_inc(emptied[misc], 1)
                elif kind == "up":
                    ba, bb = fills(s)
                    no = t.ups.index(s)
                    dve.wait_ge(th_done[layer], up_no(s) + 1)
                    v.scalar_tensor_tensor(out=th[:, s[3], :], in0=th[:, s[3], :], scalar=1.0, in1=bank[ba][:],
                                           op0=ALU.add, op1=ALU.mult).then_inc(emptied[ba], 1)
                    ps = content(t, s, bb)
                    if no >= 4:
                        old = t.ups[no - 4]
                        dve.wait_ge(down_done[old[0]], down_no(old) + 1)
                    dve.wait_ge(emptied[ba], t.fill(s, ba))
                    v.tensor_tensor(hid[:, hid_slot(s), :], th[:, s[3], :], ps[:], ALU.mult).then_inc(emptied[bb], 1)
                elif (layer, kind) == (0, "down"):
                    e, n = s[2], down_no(s)
                    dve.wait_ge(down_done[0], n + 1)
                    if n >= 3:
                        dve.wait_ge(acc_done, n - 2)
                    v.tensor_tensor(acc0[:] if n == 0 else ytmp[:, n % 2], bank[YB][:].rearrange("p (q c) -> p q c", q=NT),
                                    gatew[0][:, :, e:e + 1].to_broadcast([P, NT, C]), ALU.mult).then_inc(emptied[YB], 1)
                elif kind == "mixed":
                    dve.wait_ge(thf_done[1], 1)
                    v.scalar_tensor_tensor(out=q1[1], in0=th_f[1], scalar=1.0, in1=bank[YB][:].rearrange("p (q c) -> p q c", q=NT),
                                           op0=ALU.add, op1=ALU.mult).then_inc(emptied[YB], 1)
                elif kind == "mixin":
                    dve.wait_ge(shift_done, 1)
                    v.scalar_tensor_tensor(out=xxxT[:], in0=shiftT[:], scalar=col(COL_X), in1=xnT[0],
                                           op0=ALU.mult, op1=ALU.add).then_inc(xxx_done, 1)
                elif kind == "lora":
                    m = s[2]
                    n = lora_no(m)
                    ps = content(t, s, misc)
                    if n >= 2:
                        dve.wait_ge(xmix_done, n - 1)
                    v.scalar_tensor_tensor(out=moved[:, n % 2, :], in0=ps[:], scalar=col(COL_MIX + m), in1=shiftT[:],
                                           op0=ALU.add, op1=ALU.mult).then_inc(emptied[misc], 1)
                elif kind == "decay":
                    dve.wait_ge(emptied[misc], t.fill(s, misc, 1))
                    v.tensor_scalar(elwc[:], elw[:], DECAY_MAX, None, ALU.min).then_inc(elwc_done, 1)
                    dve.wait_ge(elwc_done, 1)
                    for q in range(NT):
                        v.tensor_tensor_scan(cum[:, q, 1:P + 1], ones_sb[:], elwc[:, q * P:(q + 1) * P], 0.0,
                                             ALU.mult, ALU.subtract).then_inc(cum_done, 1)
                    dve.wait_ge(cum_done, NT)
                    v.tensor_tensor(tot01[:], cum[:, 0, P:P + 1], cum[:, 1, P:P + 1], ALU.add).then_inc(tot_done, 1)
                elif kind == "proj":
                    if s[2] == WR:
                        dve.wait_ge(emptied[misc], t.fill(s, misc))
                        v.tensor_scalar(urT[:], rT[:], col(COL_U), None, ALU.mult).then_inc(ur_done, 1)
                    elif s[2] == WG:
                        dve.wait_ge(gth_done, 1)
                        v.scalar_tensor_tensor(out=gT[:], in0=gth[:], scalar=1.0, in1=bank[misc][:],
                                               op0=ALU.add, op1=ALU.mult).then_inc(emptied[misc], 1)
                elif kind in ("diag", "pair", "level"):
                    n = {"diag": 0, "pair": 1}.get(kind, 2 + s[2] if kind == "level" else 0)
                    ps = content(t, s, misc)[:].rearrange("p (m c) -> p m c", c=HS)
                    mask = masks_sb[:, n:n + 1, :].to_broadcast([P, NT * NH0, HS])
                    dst = pdiag.rearrange("p q h c -> p (q h) c")
                    if n == 0:
                        v.tensor_tensor(dst, ps, mask, ALU.mult).then_inc(emptied[misc], 1)
                    else:
                        dve.wait_ge(emptied[MISC[0]], t.fill(level_step(n - 3), MISC[0]))
                        v.copy_predicated(dst, mask.bitcast(I32), ps).then_inc(emptied[misc], 1)
                elif kind == "wkv":
                    ps = content(t, s, misc)[:].rearrange("p (m c) -> p m c", c=HS)
                    n = NT * NH0
                    for m in range(n):
                        v.bn_stats(gstats[:, m, :], ps[:, m, :]).then_inc(gst_done, 1)
                    for m in range(n):
                        dve.wait_ge(gst_done, m + 1)
                        v.bn_aggr(gmom[:, m, :], gstats[:, m, :]).then_inc(gst_done, 1)
                    dve.wait_ge(gst_done, 2 * n)
                    v.tensor_scalar(gvar[:], gmom[:, :, 1], GN_EPS, None, ALU.add).then_inc(gst_done, 1)
                    v.tensor_tensor(yn[:].rearrange("p q (h c) -> p (q h) c", c=HS), ps, gmom[:, :, 0:1].to_broadcast([P, n, HS]),
                                    ALU.subtract).then_inc(emptied[misc], 1)
                    dve.wait_ge(emptied[misc], t.fill(s, misc))
                    dve.wait_ge(grstd_done, 1)
                    v.tensor_tensor(yn[:].rearrange("p q (h c) -> p (q h) c", c=HS), yn[:].rearrange("p q (h c) -> p (q h) c", c=HS),
                                    grstd[:].unsqueeze(2).to_broadcast([P, n, HS]), ALU.mult).then_inc(yn_done, 1)
                elif kind == "wkvT":
                    v.tensor_scalar(ynT[:], content(t, s, misc)[:], col(COL_LNW), col(COL_LNB), ALU.mult, ALU.add).then_inc(emptied[misc], 1)
                    dve.wait_ge(emptied[misc], t.fill(s, misc))
                    v.scalar_tensor_tensor(out=zT[:], in0=gT[:], scalar=0.5, in1=ynT[:], op0=ALU.mult, op1=ALU.mult).then_inc(zT_done, 1)
                elif kind == "finish":
                    if layer == 0:
                        dve.wait_ge(thf_done[0], 1)
                        v.scalar_tensor_tensor(out=q1[0], in0=th_f[0], scalar=1.0, in1=acc0[:],
                                               op0=ALU.add, op1=ALU.mult).then_inc(q1_done, 1)
                        dve.wait_ge(q1_done, 1)
                    else:
                        dve.wait_ge(emptied[YB], t.fill((1, "down", E - 1), YB))
                    v.scalar_tensor_tensor(out=q2[layer], in0=q1[layer], scalar=(0.5, 0.25)[layer],
                                           in1=content(t, s, misc)[:].rearrange("p (q c) -> p q c", q=NT),
                                           op0=ALU.mult, op1=ALU.mult).then_inc(emptied[misc], 1)
                elif kind == "qk":
                    k = s[2] - AQ
                    dve.wait_ge(qkhi_done, k + 1)
                    v.scalar_tensor_tensor(out=qk_lo[:, k, :], in0=bank[misc][:], scalar=QSCALE[k], in1=qk_hi[:, k, :].bitcast(F32),
                                           op0=ALU.mult, op1=ALU.subtract).then_inc(emptied[misc], 1)
                elif kind == "smax":
                    h, q = s[2:]
                    v.reduce_max(rowmax[:, h // HG, q, h % HG:h % HG + 1], content(t, s, SB)[:], AX).then_inc(emptied[SB], 1)
                elif kind == "mrow":
                    dve.wait_ge(mhi_done, s[2] + 1)
                    v.scalar_tensor_tensor(out=m_lo[:], in0=bank[misc][0:HG, :], scalar=-1.0, in1=m_hi[:].bitcast(F32),
                                           op0=ALU.mult, op1=ALU.subtract).then_inc(emptied[misc], 1)
                elif kind == "headsT":
                    g = s[2]
                    ps = content(t, s, misc)[:].rearrange("p (q j c) -> p q j c", q=NT, j=HG)
                    v.reciprocal(rden[:], ps[:, :, :, DK]).then_inc(rden_done, 1)
                    dve.wait_ge(rden_done, g + 1)
                    v.tensor_tensor(heads[:, :, 32 * g:32 * g + 32].rearrange("p q (j c) -> p q j c", j=HG), ps[:, :, :, 0:DK],
                                    rden[:].unsqueeze(3).to_broadcast([P, NT, HG, DK]), ALU.mult).then_inc(emptied[misc], 1)

            def route(t, s):
                layer, misc = s[0], MISC[s[0]]
                sc, w, sig = scores_sb[layer], wtmp[layer], gate_math[layer]
                v.tensor_copy(sc[:], content(t, s, misc)[:, 0:NT * E].rearrange("p (q e) -> p q e", q=NT)).then_inc(emptied[misc], 1)
                dve.wait_ge(emptied[misc], t.fill(s, misc, 0))
                tops = top_done[layer]
                for q in range(NT):
                    v.max(top[layer][:, q, :], sc[:, q, :]).then_inc(tops, 1)
                for q in range(NT):
                    dve.wait_ge(tops, q + 1)
                    v.max_index(topi[layer][:, q, :], top[layer][:, q, :], sc[:, q, :]).then_inc(tops, 1)
                dve.wait_ge(tops, NT)
                if layer == 0:
                    v.tensor_tensor(w[:, 0, :], top[0][:, :, 1], top[0][:, :, 0], ALU.subtract).then_inc(gate_pre[0], 1)
                else:
                    v.tensor_scalar(w[:, 0:2, :], top[1][:, :, 0:2].rearrange("p q k -> p k q"), -1.0, None, ALU.mult).then_inc(gate_pre[1], 1)
                dve.wait_ge(gate_exp[layer], 1)
                if layer == 0:
                    v.tensor_scalar(w[:, 3, :], w[:, 2, :], 1.0, None, ALU.add).then_inc(sig, 1)
                    dve.wait_ge(sig, 1)
                    v.reciprocal(w[:, 4, :], w[:, 3, :]).then_inc(sig, 1)
                    dve.wait_ge(sig, 2)
                    v.tensor_scalar(w[:, 4, :], w[:, 4, :], 0.5, None, ALU.mult).then_inc(sig, 1)
                    dve.wait_ge(sig, 3)
                    v.tensor_tensor(w[:, 5, :], w[:, 2, :], w[:, 4, :], ALU.mult).then_inc(sig, 1)
                else:
                    v.tensor_scalar(w[:, 2:4, :], w[:, 2:4, :], 1.0, None, ALU.add).then_inc(sig, 1)
                    dve.wait_ge(sig, 1)
                    v.reciprocal(w[:, 4:6, :], w[:, 2:4, :]).then_inc(sig, 1)
                n = 4 if layer == 0 else 2
                dve.wait_ge(sig, n)
                dve.wait_ge(tops, 2 * NT)
                shape = [P, NT, E]
                experts = iota_sb[:].unsqueeze(1).to_broadcast(shape)
                for k in range(2):
                    pick = pick_sb[layer][:, k]
                    v.tensor_tensor(pick, experts, topi[layer][:, :, k:k + 1].to_broadcast(shape), ALU.is_equal).then_inc(sig, 1)
                    dve.wait_ge(sig, n + 2 * k + 1)
                    v.tensor_tensor(pick, pick, w[:, 4 + k, :].unsqueeze(2).to_broadcast(shape), ALU.mult).then_inc(sig, 1)
                dve.wait_ge(sig, n + 4)
                v.tensor_tensor(gatew[layer][:], pick_sb[layer][:, 0], pick_sb[layer][:, 1], ALU.add).then_inc(gatew_done[layer], 1)
                if layer == 1:
                    dve.wait_ge(gwhi_done, 1)
                    v.tensor_tensor(gw_lo[:], bank[misc][0:E, :], gw_hi[:].bitcast(F32), ALU.subtract).then_inc(emptied[misc], 1)

            turns(dve, "dve", step)


def _layout(a, np):
    f = lambda v: np.ascontiguousarray(v, dtype=np.float32)
    p = "L0_attn_"
    kone = np.zeros(P)
    for j in range(HG):
        kone[32 * j + 24:32 * j + 26] = 1.0
    cols = [a[p + f"time_maa_{n}"] for n in "xwkvrg"] + [a[p + "time_decay"], a[p + "time_faaaa"].reshape(C), a[p + "ln_w"], a[p + "ln_b"], kone]
    square = [a[p + n] for n in ("Wr", "Wk", "Wv", "Wg", "Wo")]
    square += [a[f"L1_attn_W_{n}"].transpose(1, 0, 2).reshape(C, C) for n in ("query", "key", "val")] + [a["L1_attn_W_out"].reshape(C, C)]
    w3 = a["L0_ffn_W3"].transpose(2, 0, 1).reshape(FT, P, E, C).transpose(1, 2, 0, 3)
    up1 = np.concatenate([a["L1_ffn_w_in_eDF"], a["L1_ffn_w_in_shared_FD"].T[None]]).transpose(1, 0, 2)
    gate1 = np.concatenate([a["L1_ffn_w_swiglu_eDF"], a["L1_ffn_w_swiglu_FD"].T[None]]).transpose(1, 0, 2)
    down1 = np.concatenate([a["L1_ffn_w_out_eFD"], a["L1_ffn_w_out_shared_DF"].T[None]]).reshape(E1, FT, P, C).transpose(2, 0, 1, 3)
    s, u = np.arange(HS)[:, None], np.arange(HS)[None, :]
    masks = [s == u]
    for hs in (1,) + HALVES:
        masks.append((s // (2 * hs) == u // (2 * hs)) & (s % (2 * hs) < hs) & (u % (2 * hs) >= hs))
    masks = np.tile(np.stack(masks, 1), (2, 1, 1))
    select = np.zeros((P, 4, P))
    for g in range(NG):
        for j in range(HG):
            for d in range(DK):
                row = (HG * g + j) * DK + d
                for n, parts in enumerate(((0, 2), (1,), (0, 1), (2,))):
                    for part in parts:
                        select[row, n, 32 * j + DK * part + d] = 1.0
    return {
        "x": f(a["L0_attn_x"]), "cols": f(np.stack(cols, 1)), "mix1": f(a[p + "time_maa_w1"]), "square": f(np.stack(square, 1)),
        "mix2": f(a[p + "time_maa_w2"].reshape(5 * 32, C)), "dec1": f(a[p + "time_decay_w1"]), "dec2": f(a[p + "time_decay_w2"]),
        "up0": f(a["L0_ffn_W1"].transpose(2, 0, 1)), "gate0": f(a["L0_ffn_W2"].transpose(2, 0, 1)), "down0": f(w3),
        "up1": f(up1), "gate1": f(gate1), "down1": f(down1),
        "routers": f(np.stack([a["L0_ffn_Wg"].T, a["L1_ffn_router_DE"]], 1)), "ident": f(np.eye(P)), "masks": f(masks),
        "select": f(select), "iota": f(np.tile(np.arange(E), (P, 1))),
    }


def kernel(**inputs):
    import numpy as np
    from concourse import bacc
    from concourse.bass_utils import run_bass_kernel_spmd

    nc = bacc.Bacc("TRN2", target_bir_lowering=False, num_devices=1)
    arrays = _layout({k: np.asarray(v) for k, v in inputs.items()}, np)
    args = [nc.dram_tensor(n, v.shape, F32, kind="ExternalInput").ap() for n, v in arrays.items()]
    out = nc.dram_tensor("out", (B, T, C), F32, kind="ExternalOutput").ap()
    two_layer_kernel(nc, *args, out)
    return run_bass_kernel_spmd(nc, [arrays], core_ids=[0]).results[0]["out"]
```

```python
from contextlib import ExitStack

import concourse.bass as bass
import numpy as np
from concourse import mybir

F32 = mybir.dt.float32
F32R = mybir.dt.float32r
I32 = mybir.dt.int32
U32 = mybir.dt.uint32
ALU = mybir.AluOpType
ACT = mybir.ActivationFunctionType
AX = mybir.AxisListType.X

P = 128
B, T, C = 16, 512, 128
NT = T // P
NH0, HS = 2, 64
E = 8
FT = 2
E1 = E + 1
NH, DK = 16, 8
HG = 4
NG = NH // HG
LN_EPS = 1e-5
GN_EPS = 64e-5
DECAY_MAX = 110.0
HALVES = (2, 4, 8, 16, 32)
VCOLS = 32
RING = 3

MIX_W, MIX_K, MIX_V, MIX_R, MIX_G = range(5)
COL_X, COL_MIX, COL_DECAY, COL_U, COL_LNW, COL_LNB, COL_KONE = 0, 1, 6, 7, 8, 9, 10
WR, WK, WV, WG, WO, AQ, AK, AV, AO = range(9)
QSCALE = (DK ** -0.5, 1.0)
LEVEL = {"cross128": len(HALVES), "cross256": len(HALVES) + 1, "cross512": len(HALVES) + 2}


ATTN_START, ATTN_EVERY, SOFT_AFTER = 6, 1.84, 7
UPS_START, UPS_EVERY, GATES_BEFORE, DOWN_AFTER = -0.63, 4.0, 5.44, 7.03
MIX_START, MIX_EVERY = 1.0, 5.79
STACK_BEFORE, PV_AFTER, MROW_AFTER, HEADS_AFTER = 5.05, 3.58, 4.72, 5.59
FIRST_START, GATE_AFTER, LAST_HEADS_AFTER = -3.5, 1.94, 4.6
QK_START, QK_EVERY, DECAYS_BEFORE, CROSS_BEFORE = -5.41, 2.61, 5.06, 5.51
FINISH_AFTER, NORM0_AFTER, NORM1_AFTER, NORMT_AFTER, ROUTE0_AFTER, ROUTE1_AFTER, GATET_AFTER = 3.83, -2.28, 7.2, 12.75, 1.38, 4.88, 6.33
NORMT0_AFTER = 3.71
LATER = {
    "dve": {"up": 1.0, "gate": 1.0, "level": -0.3, "down": 0.5, "decay": 1.3, "lora": -0.1},
    "act": {"soft": -0.4, "decays": -1.4, "keep": 3.0},
    "pool": {"lora": -0.7, "down": -1.3},
    "pe": {"down": 0.1, "soft": -0.2},
    "sp": {},
}


def due_times():
    due = {(1, "keep"): 0.0, (0, "keep"): 0.1, (0, "load"): 0.2}
    mix = [(0, "mixin"), (0, "lora", MIX_W), (0, "lora", MIX_K), (0, "decay"), (0, "lora", MIX_R),
           (0, "proj", WK), (0, "lora", MIX_V), (0, "proj", WR), (0, "lora", MIX_G), (0, "value"),
           (0, "proj", WG), (0, "diag"), (0, "pair")]
    mix += [(0, "level", n) for n in range(len(HALVES))]
    mix += [(0, "cross128"), (0, "cross256"), (0, "cross512", 0), (0, "cross512", 1), (0, "wkv"), (0, "wkvT")]
    for i, s in enumerate(mix):
        due[s] = MIX_START + MIX_EVERY * i
        if s[1] == "level":
            due[0, "decays", s[2]] = due[s] - DECAYS_BEFORE
        elif s[1] in LEVEL and s[2:] != (1,):
            due[0, "decays", LEVEL[s[1]]] = due[s] - CROSS_BEFORE
    start = ATTN_START
    for i, s in enumerate([(1, "qk", AQ), (1, "qk", AK), (1, "attnv")]):
        due[s] = QK_START + QK_EVERY * i
    for g in range(NG):
        for i in range(HG * NT):
            at = start + ATTN_EVERY * (HG * NT * g + i)
            soft_at = at + ATTN_EVERY * HG * NT + SOFT_AFTER
            due[1, "smax", HG * g + i // NT, i % NT] = at
            due[1, "soft", HG * g + i % HG, i // HG] = soft_at
            if i % HG == HG - 1:
                due[1, "pv", g, i // HG] = soft_at + PV_AFTER
        due[1, "stack", AQ, g] = max(start + ATTN_EVERY * HG * NT * g - STACK_BEFORE, due[1, "qk", AK])
        due[1, "stack", AK, g] = max(start + ATTN_EVERY * HG * NT * g - STACK_BEFORE / 2, due[1, "qk", AK])
        due[1, "mrow", g] = at + MROW_AFTER
        due[1, "headsT", g] = soft_at + PV_AFTER + (HEADS_AFTER if g < NG - 1 else LAST_HEADS_AFTER)
    due[1, "outT"] = due[1, "headsT", NG - 1] + 1
    experts = [(1, e) for e in [E] + list(range(E))] + [(0, e) for e in range(E)]
    for i, (layer, e) in enumerate(experts):
        at = UPS_START + UPS_EVERY * FT * i if i else FIRST_START
        for f in range(FT):
            due[layer, "up", e, f] = at + UPS_EVERY * f
            due[layer, "gate", e, f] = at + UPS_EVERY * f + GATE_AFTER
        due[layer, "down", e] = at + UPS_EVERY * (FT - 1) + DOWN_AFTER
        due[layer, "down0", e] = due[layer, "down", e] - UPS_EVERY / 2
        if layer == 1 and e < E:
            due[layer, "gates", e] = max(at - GATES_BEFORE, 0.0)
    due[1, "mixed"] = due[1, "down", E - 1] + 1
    due[1, "finish"] = due[1, "outT"] + 1
    due[0, "finish"] = max(due[0, "wkvT"], due[0, "down", E - 1]) + FINISH_AFTER
    due[0, "norm"] = due[0, "wkvT"] + NORM0_AFTER
    due[0, "normT"] = max(due[0, "norm"], due[0, "gate", E - 1, FT - 1]) + NORMT0_AFTER
    due[0, "route"] = max(due[0, "normT"], due[0, "down", E - 1]) + ROUTE0_AFTER
    due[1, "norm"] = due[0, "finish"] + NORM1_AFTER
    due[1, "normT"] = due[1, "norm"] + NORMT_AFTER
    due[1, "route"] = due[1, "normT"] + ROUTE1_AFTER
    due[1, "gateT"] = due[1, "route"] + GATET_AFTER
    return due


DUE = due_times()
PLAN = sorted(DUE, key=lambda s: DUE[s])
MISC = ("mix", "attn")
HB, GB, YB, SB, TB, VB = "h", "g", "y", "s", "st", "pv"
BANKS = MISC + (HB, GB, YB, SB, TB, VB)


def fills(step):
    layer, kind = step[:2]
    if kind in ("up", "gate"):
        return [HB if kind == "up" else GB]
    if kind == "down":
        return [YB] if layer == 0 or step[2] == E - 1 else []
    if kind in ("smax", "soft"):
        alone = step[2] // HG == (0 if kind == "smax" else NG - 1) and step[3 if kind == "smax" else 2] % 2
        return [SB if (kind == "smax") != bool(alone) else TB]
    if kind == "pv":
        return [VB] if step[3] == 0 else []
    if kind in ("keep", "load", "mixed", "norm", "decays", "down0"):
        return []
    twice = ((0, "mixin"), (0, "decay"))
    return [MISC[layer]] * (2 if step[:2] in twice else 1)


def part(step):
    layer, kind = step[:2]
    return ("ready" if kind in ("load", "norm", "normT", "route", "gateT") else "layer") + str(layer)


class Turn:

    def __init__(self, number, parts):
        self.seq = (number, number - 1)
        self.first = isinstance(number, int) and number == 0
        self.steps = [s for s in PLAN if part(s) in parts]
        self.ups = [s for s in self.steps if s[1] == "up"]
        self.before, count = {}, {b: 0 for b in BANKS}
        for s in self.steps:
            self.before[s] = dict(count)
            for b in fills(s):
                count[b] += 1

    def order(self, engine):
        return sorted(self.steps, key=lambda s: DUE[s] + LATER[engine].get(s[1], 0.0))

    def fill(self, step, bank, n=0):
        return self.before[step][bank] + n + 1


def two_layer_kernel(nc, x, cols, mix1, square, mix2, dec1, dec2, up0, gate0, down0, up1, gate1, down1,
                     routers, ident, masks, select, iota, out):
    with ExitStack() as ctx:
        def sb(name, shape, dt=F32):
            return ctx.enter_context(nc.sbuf_tensor(name, shape, dt))

        def sem(name):
            return ctx.enter_context(nc.semaphore(name))

        def tiles(tensor):
            return tensor[:].rearrange("p (q c) -> p q c", q=NT)

        cols_sb = sb("cols_sb", [P, 11])
        mix1_sb = sb("mix1_sb", [P, 160])
        sq = sb("sq", [P, 9, C])
        mix2_sb = sb("mix2_sb", [P, C])
        mix2g_sb = sb("mix2g_sb", [32, C])
        dec1_sb = sb("dec1_sb", [P, 64])
        dec2_sb = sb("dec2_sb", [64, C])
        up_hi, up_lo = (sb(f"up0_{part}", [P, E, 256], F32R) for part in ("hi", "lo"))
        gate_hi, gate_lo = (sb(f"gate0_{part}", [P, E, 256], F32R) for part in ("hi", "lo"))
        up1_sb = sb("up1_sb", [P, E1, 256])
        gate1_sb = sb("gate1_sb", [P, E1, 256])
        down_sb = [sb("down0_sb", [P, E, FT, C]), sb("down1_sb", [P, E1, FT, C])]
        router_sb = sb("router_sb", [P, 2, E])
        ident_sb = sb("ident_sb", [P, P])
        masks_sb = sb("masks_sb", [P, 7, HS])
        select_sb = sb("select_sb", [P, 4, P], F32R)
        iota_sb = sb("iota_sb", [P, E])
        ones_sb = sb("ones_sb", [P, 1])
        power_sb = sb("power_sb", [P, 8])

        stats = [sb(f"stats{i}", [P, NT, 6]) for i in range(2)]
        moments = [sb(f"moments{i}", [P, NT, 2]) for i in range(2)]
        vareps = [sb(f"vareps{i}", [P, NT]) for i in range(2)]
        rstd = [sb(f"rstd{i}", [P, NT]) for i in range(2)]
        xn = [sb(f"xn{i}", [P, NT, C]) for i in range(2)]
        xnT0 = sb("xnT0", [P, 1 + T])
        xnT1 = sb("xnT1", [P, T])
        xnT = (xnT0[:, 1:], xnT1[:])
        xnT_hi = sb("xnT_hi", [P, T], F32R)
        xnT_lo = sb("xnT_lo", [P, T], F32R)
        top = [sb(f"top{i}", [P, NT, 8]) for i in range(2)]
        scores_sb = [sb(f"scores{i}", [P, NT, E]) for i in range(2)]
        topi = [sb(f"topi{i}", [P, NT, 8], U32) for i in range(2)]
        wtmp = [sb(f"wtmp{i}", [P, 6, NT]) for i in range(2)]
        gatew = [sb(f"gatew{i}", [P, NT, E]) for i in range(2)]
        pick_sb = [sb(f"pick{i}", [P, 2, NT, E]) for i in range(2)]
        th = sb("th", [P, 2, T])
        hid = sb("hid", [P, 4, T])

        x_next = sb("x_next", [P, NT, C])
        shiftT = sb("shiftT", [P, T])
        p128 = shiftT[0:HS, :].rearrange("p (q h c) -> p q h c", q=NT, h=NH0)
        xxxT = sb("xxxT", [P, T])
        elw, gth = xxxT, xxxT
        pdiag = xxxT[:].rearrange("p (q h c) -> p q h c", q=NT, h=NH0)
        mixa = sb("mixa", [P, T])
        zT = mixa
        gT = sb("gT", [P, T])
        mixb = gT[0:32, :]
        elwc = sb("elwc", [P, T])
        dec_h, ynT = elwc[0:64, :], elwc
        moved = sb("moved", [P, 2, T])
        diff = moved
        th_f0 = moved[:, 0, :].rearrange("p (q c) -> p q c", q=NT)
        xmixT = sb("xmixT", [P, 3, T])
        p512 = xmixT[:, 0:2, :].rearrange("p h (c n) -> p h c n", c=2)
        p256 = xmixT[:, 2, :].rearrange("p (m h c) -> p m h c", m=2, h=NH0)
        cum = sb("cum", [P, NT, P + 1])
        tot01 = sb("tot01", [P, 1])
        rT = sb("rT", [P, T])
        kT = sb("kT", [P, T])
        v0 = sb("v0", [P, NT, C])
        expd = sb("expd", [P, 2, T])
        urT = expd[:, 1, :]
        q2_0 = expd[:, 0, :].rearrange("p (q c) -> p q c", q=NT)
        rk = sb("rk", [P, 2, T])
        gstats = sb("gstats", [P, NT * NH0, 6])
        gmom = sb("gmom", [P, NT * NH0, 2])
        gvar = sb("gvar", [P, NT * NH0])
        grstd = sb("grstd", [P, NT * NH0])
        yn = xn[0]
        acc0 = sb("acc0", [P, NT, C])
        ytmp = sb("ytmp", [P, 2, NT, C])
        x1 = sb("x1", [P, NT, C])

        x1b = sb("x1b", [P, NT, C])
        gw_hi = sb("gw_hi", [E, T], F32R)
        gw_lo = sb("gw_lo", [E, T], F32R)
        unit_sb = sb("unit_sb", [E, E], F32R)
        xg = sb("xg", [P, 2, T])
        qk_hi = sb("qk_hi", [P, 2, T], F32R)
        qk_lo = sb("qk_lo", [P, 2, T], F32R)
        qs = sb("qs", [P, RING, T], F32R)
        ks = sb("ks", [P, RING, T], F32R)
        v1_all = sb("v1", [P, NT, (DK + 1) * (NH - 1) + VCOLS])
        v1 = v1_all[:, :, 0:(DK + 1) * NH].rearrange("p q (h k) -> p q h k", k=DK + 1)
        rowmax = sb("rowmax", [P, NG, NT, HG])
        m_hi = sb("m_hi", [HG, T], F32R)
        m_lo = sb("m_lo", [HG, T], F32R)
        probs = sb("probs", [P, 2, HG, T])
        oT = sb("oT", [P, T])
        headsT_sb = oT
        rden = sb("rden", [P, NT, HG])
        heads = sb("heads", [P, NT, C])
        out_sb = heads

        select_ld = hid[:, 0, :].rearrange("p (n c) -> p n c", n=4)
        up_ld, gate_ld = (probs[:, n].rearrange("p j t -> p (j t)").rearrange("p (e u) -> p e u", e=E) for n in range(2))
        th_f = (th_f0, xg[:, 1, :].rearrange("p (q c) -> p q c", q=NT))
        q1 = (ytmp[:, 0], th_f[1])
        q2 = (q2_0, xg[:, 0, :].rearrange("p (q c) -> p q c", q=NT))

        bank = {b: ctx.enter_context(nc.psum_tensor(f"bank_{b}", [P, T], F32)) for b in BANKS}
        s_load = sem("s_load")
        s_set = sem("s_set")
        s_select = sem("s_select")
        s_mix = sem("s_mix")
        s_up = sem("s_up")
        s_expert = sem("s_expert")
        s_high = sem("s_high")
        s_split = sem("s_split")
        arrived = sem("arrived")
        clearing = sem("clearing")
        entered = sem("entered")
        out_done = sem("out_done")
        left = sem("left")
        first_turn_sem = left.num + 1
        filled = {b: sem(f"filled_{b}") for b in BANKS}
        emptied = {b: sem(f"emptied_{b}") for b in BANKS}

        x_in = sem("x_in")
        out_free = sem("out_free")
        mrow_in = sem("mrow_in")
        L = (0, 1)
        st_done = [sem(f"stats_done{i}") for i in L]
        rstd_done = [sem(f"rstd_done{i}") for i in L]
        xn_done = [sem(f"xn_done{i}") for i in L]
        kept = [sem(f"kept{i}") for i in L]
        top_done = [sem(f"top_done{i}") for i in L]
        gate_pre = [sem(f"gate_pre{i}") for i in L]
        gate_exp = [sem(f"gate_exp{i}") for i in L]
        gate_math = [sem(f"gate_math{i}") for i in L]
        picked = [sem(f"picked{i}") for i in L]
        gatew_done = [sem(f"gatew_done{i}") for i in L]
        shift_done = sem("shift_done")
        xxx_done = sem("xxx_done")
        xmix_done = sem("xmix_done")
        elwc_done = sem("elwc_done")
        cum_done = sem("cum_done")
        tot_done = sem("tot_done")
        ur_done = sem("ur_done")
        gth_done = sem("gth_done")
        diff_done = sem("diff_done")
        expd_done = sem("expd_done")
        rows_done = sem("rows_done")
        rk_half = sem("rk_half")
        rk_done = sem("rk_done")
        gst_done = sem("gst_done")
        grstd_done = sem("grstd_done")
        yn_done = sem("yn_done")
        zT_done = sem("zT_done")
        acc_done = sem("acc_done")
        thf_done = [sem(f"thf_done{i}") for i in L]
        q1_done = sem("q1_done")
        x1_done = sem("x1_done")
        th_done = [sem(f"th_done{i}") for i in L]
        down_done = [sem(f"down_done{i}") for i in L]
        xhi_done = sem("xhi_done")
        qkhi_done = sem("qkhi_done")
        gwhi_done = sem("gwhi_done")
        pv_done = sem("pv_done")
        mhi_done = sem("mhi_done")
        rden_done = sem("rden_done")
        out_ready = sem("out_ready")

        loads = [(ident_sb[:], ident), (router_sb[:], routers), (iota_sb[:], iota), (select_ld, select)]
        mix_loads = [(cols_sb[:], cols), (mix1_sb[:], mix1), (sq[:], square), (mix2_sb[:], mix2[0:P, :]),
                     (mix2g_sb[:], mix2[P:160, :]), (dec1_sb[:], dec1), (dec2_sb[:], dec2), (masks_sb[:], masks)]
        up_loads = [(up_ld, up0), (gate_ld, gate0)]
        expert_loads = [(down_sb[0][:], down0),
                        (up1_sb[:], up1), (gate1_sb[:], gate1), (down_sb[1][:], down1)]
        NSET = 6
        ups = [s for s in PLAN if s[1] == "up"]
        downs = [[s for s in PLAN if s[:2] == (i, "down")] for i in L]
        loras = [s[2] for s in PLAN if s[1] == "lora"]

        def up_no(s):
            return [u for u in ups if u[0] == s[0]].index(s)

        def hid_slot(s):
            return ups.index(s) % 4

        def down_no(s):
            return downs[s[0]].index((s[0], "down", s[2]))

        def lora_no(m):
            return loras.index(m)

        fenced = [s for s in PLAN if s[1] in ("diag", "pair", "level", "cross128", "cross256", "wkv")]

        def level_step(n):
            names = [(0, "diag"), (0, "pair")] + [(0, "level", k) for k in range(len(HALVES))] + [(0, "cross128"), (0, "cross256")]
            return names[n + 2]

        last_turn_sem = out_ready.num

        def turns(eng, name, step):
            run(eng, name, step, Turn(-1, ("ready0",)), 0)
            run(eng, name, step, Turn(0, ("layer0", "ready0", "ready1")), 1)
            with eng.Fori(1, B - 1) as i:
                run(eng, name, step, Turn(i, ("layer0", "layer1", "ready0", "ready1")), i + 1)
            run(eng, name, step, Turn(B - 1, ("layer0", "layer1", "ready1")), B)
            run(eng, name, step, Turn(B, ("layer1",)), None)

        def run(eng, name, step, turn, number):
            for s in turn.order(name):
                step(turn, s)
            if number is not None:
                eng.drain().then_inc(arrived, 1)
                if eng is nc.sync:
                    eng.wait_ge(arrived, number * 5 + 5)
                    eng.sem_inc(clearing, 1)
                    eng.sem_clear(range(first_turn_sem, last_turn_sem + 1))
                    eng.sem_inc(left, 1)
                else:
                    eng.wait_ge(left, number + 1)
                    eng.sem_inc(entered, 1)

        block = ctx.enter_context(nc.Block())

        @block.sync
        def _(sp):
            for dst, src in loads:
                sp.dma_start(dst, src).then_inc(s_load, 16)

            def step(t, s):
                layer, kind = s[:2]
                misc = MISC[layer]
                if kind == "load":
                    if (0, "keep") in t.steps:
                        sp.wait_ge(kept[0], 1)
                    sp.dma_start(x_next[:], x[t.seq[0] + 1].rearrange("(q p) c -> p q c", p=P)).then_inc(x_in, 16)
                    if (0, "keep") not in t.steps:
                        for signal, group in ((s_mix, mix_loads), (s_up, up_loads), (s_expert, expert_loads)):
                            for dst, src in group:
                                sp.dma_start(dst, src).then_inc(signal, 16)
                elif (layer, kind) == (1, "keep"):
                    sp.wait_ge(out_done, 16 * (t.seq[1] + 1))
                    sp.sem_inc(out_free, 1)
                elif kind == "mrow":
                    g = s[2]
                    sp.wait_ge(mhi_done, g + 1)
                    sp.dma_start(qs[24::32, g % RING, :].bitcast(F32), m_hi[:].bitcast(F32)).then_inc(mrow_in, 16)
                    sp.wait_ge(emptied[misc], t.fill(s, misc))
                    sp.dma_start(qs[25::32, g % RING, :].bitcast(F32), m_lo[:].bitcast(F32)).then_inc(mrow_in, 16)
                elif (layer, kind) == (1, "finish"):
                    sp.wait_ge(out_ready, 1)
                    sp.dma_start(out[t.seq[1]].rearrange("(q p) c -> p q c", p=P), out_sb[:]).then_inc(out_done, 16)

            sp.sem_inc(out_done, 16)
            turns(sp, "sp", step)
            sp.wait_ge(out_done, 16 * (B + 1))

        @block.tensor
        def _(pe):
            mm = nc.tensor.matmul

            def room(t, s, b, n=0):
                if t.fill(s, b, n) > 1:
                    pe.wait_ge(emptied[b], t.fill(s, b, n) - 1)
                return bank[b]

            def fence(s, last):
                last.then_inc(rows_done, 1)
                pe.wait_ge(rows_done, fenced.index(s) + 1)

            def transposes(dst, src):
                for q in range(NT):
                    last = nc.tensor.transpose(dst[:, q * P:(q + 1) * P], src[:, q, :], ident_sb[:])
                return last

            def step(t, s):
                layer, kind = s[:2]
                misc = MISC[layer]
                if t.first and kind == "mixin":
                    pe.wait_ge(s_mix, 16 * len(mix_loads))
                if t.first and s == t.ups[0]:
                    pe.wait_ge(s_split, 2)
                    pe.wait_ge(s_expert, 16 * len(expert_loads))
                if kind == "normT":
                    pe.wait_ge(xn_done[layer], NT)
                    transposes(room(t, s, misc), xn[layer]).then_inc(filled[misc], 1)
                elif kind == "route":
                    pe.wait_ge(emptied[misc], t.fill((layer, "normT"), misc))
                    ps = room(t, s, misc)
                    for q in range(NT):
                        last = mm(ps[:, q * E:(q + 1) * E], xnT[layer][:, q * P:(q + 1) * P], router_sb[:, layer, :],
                                  start=True, stop=True)
                    last.then_inc(filled[misc], 1)
                elif kind == "gateT":
                    pe.wait_ge(gatew_done[1], 1)
                    ps = room(t, s, misc)
                    for q in range(NT):
                        last = nc.tensor.transpose(ps[0:E, q * P:(q + 1) * P], gatew[1][:, q, :], ident_sb[:])
                    last.then_inc(filled[misc], 1)
                elif kind == "gates":
                    ps, one = room(t, s, misc), unit_sb[:, s[2]:s[2] + 1].to_broadcast([E, P])
                    mm(ps[:], one, gw_hi[:], start=True, stop=False)
                    mm(ps[:], one, gw_lo[:], start=False, stop=True).then_inc(filled[misc], 1)
                elif kind in ("up", "gate"):
                    e, f = s[2:]
                    if layer == 1 and e < E:
                        pe.wait_ge(emptied[MISC[1]], t.fill((1, "gates", e), MISC[1]))
                    b, units = HB if kind == "up" else GB, slice(f * P, (f + 1) * P)
                    ps = room(t, s, b)
                    if layer == 0:
                        hi, lo = (up_hi, up_lo) if kind == "up" else (gate_hi, gate_lo)
                        mm(ps[:], hi[:, e, units], xnT_hi[:], start=True, stop=False)
                        mm(ps[:], hi[:, e, units], xnT_lo[:], start=False, stop=False)
                        mm(ps[:], lo[:, e, units], xnT_hi[:], start=False, stop=True).then_inc(filled[b], 1)
                    else:
                        w = up1_sb if kind == "up" else gate1_sb
                        mm(ps[:], w[:, e, units], xnT[1] if e == E else xg[:, e % 2, :], start=True, stop=True).then_inc(filled[b], 1)
                elif kind in ("down0", "down"):
                    e, n = s[2], down_no(s)
                    pe.wait_ge(emptied[GB], t.fill((layer, "gate", e, FT - 1), GB))
                    if kind == "down0" and (layer == 0 or n == 0):
                        room(t, (0, "down", e) if layer == 0 else (1, "down", E - 1), YB)
                    for q in (range(2, NT) if kind == "down" else range(2)):
                        for f in range(FT):
                            start = f == 0 if layer == 0 else n == q == f == 0
                            last = mm(bank[YB][:, q * P:(q + 1) * P],
                                      hid[:, hid_slot((layer, "up", e, f)), q * P:(q + 1) * P], down_sb[layer][:, e, f, :],
                                      start=start, stop=f == FT - 1 and (layer == 0 or n == E), skip_group_check=True)
                    if kind == "down":
                        last.then_inc(down_done[layer], 1)
                elif kind == "mixin":
                    pe.wait_ge(xxx_done, 1)
                    mm(room(t, s, misc)[:], mix1_sb[:, 0:P], xxxT[:], start=True, stop=True).then_inc(filled[misc], 1)
                    mm(room(t, s, misc, 1)[0:32, :], mix1_sb[:, P:160], xxxT[:], start=True, stop=True).then_inc(filled[misc], 1)
                elif kind == "lora":
                    m = s[2]
                    pe.wait_ge(emptied[MISC[0]], t.fill((0, "mixin"), MISC[0], 1))
                    lhsT, rhs = (mix2g_sb[:], mixb) if m == 4 else (mix2_sb[32 * m:32 * m + 32, :], mixa[32 * m:32 * m + 32, :])
                    mm(room(t, s, misc)[:], lhsT, rhs, start=True, stop=True).then_inc(filled[misc], 1)
                elif kind == "decay":
                    pe.wait_ge(xmix_done, lora_no(MIX_W) + 1)
                    mm(room(t, s, misc)[0:64, :], dec1_sb[:], xmixT[:, lora_no(MIX_W) % 3, :], start=True, stop=True).then_inc(filled[misc], 1)
                    pe.wait_ge(emptied[misc], t.fill(s, misc, 0))
                    mm(room(t, s, misc, 1)[:], dec2_sb[:], dec_h, start=True, stop=True).then_inc(filled[misc], 1)
                elif kind == "proj":
                    m = {WR: MIX_R, WK: MIX_K, WG: MIX_G}[s[2]]
                    pe.wait_ge(xmix_done, lora_no(m) + 1)
                    mm(room(t, s, misc)[:], sq[:, s[2], :], xmixT[:, lora_no(m) % 3, :], start=True, stop=True).then_inc(filled[misc], 1)
                elif kind == "value":
                    pe.wait_ge(xmix_done, lora_no(MIX_V) + 1)
                    ps = room(t, s, misc)
                    for q in range(NT):
                        last = mm(ps[:, q * P:(q + 1) * P], xmixT[:, lora_no(MIX_V) % 3, q * P:(q + 1) * P], sq[:, WV, :], start=True, stop=True)
                    last.then_inc(filled[misc], 1)
                elif kind == "attnv":
                    ps = room(t, s, misc)
                    for q in range(NT):
                        last = mm(ps[:, q * P:(q + 1) * P], xnT[1][:, q * P:(q + 1) * P], sq[:, AV, :], start=True, stop=True)
                    last.then_inc(filled[misc], 1)
                elif kind in ("diag", "pair", "level"):
                    if kind == "level":
                        pe.wait_ge(rk_done, s[2] + 1)
                        a = b = rk[:, s[2] % 2, :]
                    else:
                        pe.wait_ge(emptied[MISC[0]], t.fill((0, "proj", WK), MISC[0]))
                        pe.wait_ge(emptied[MISC[0]], t.fill((0, "proj", WR), MISC[0]))
                        if kind == "diag":
                            pe.wait_ge(ur_done, 1)
                        a, b = kT[:], urT if kind == "diag" else rT[:]
                    ps = room(t, s, misc)
                    for h in range(NH0):
                        for q in range(NT):
                            ch, o = slice(HS * h, HS * h + HS), (q * NH0 + h) * HS
                            for half in range(2):
                                tok = slice(q * P + HS * half, q * P + HS * half + HS)
                                last = mm(ps[HS * half:HS * half + HS, o:o + HS], a[ch, tok], b[ch, tok], start=True, stop=True)
                        if h == 0:
                            fence(s, last)
                    last.then_inc(filled[misc], 1)
                elif kind in ("cross128", "cross256", "cross512"):
                    n = LEVEL[kind]
                    pe.wait_ge(rk_done, n + 1)
                    ps, a = room(t, s, misc), rk[:, n % 2, :]
                    for h in ([s[2]] if kind == "cross512" else range(NH0)):
                        ch = slice(HS * h, HS * h + HS)
                        if kind == "cross128":
                            for q in range(NT):
                                o = (q * NH0 + h) * HS
                                last = mm(ps[0:HS, o:o + HS], a[ch, q * P:q * P + HS], a[ch, q * P + HS:(q + 1) * P], start=True, stop=True)
                        elif kind == "cross256":
                            for p in range(2):
                                o = (p * NH0 + h) * P
                                last = mm(ps[:, o:o + P], a[ch, 2 * p * P:(2 * p + 1) * P], a[ch, (2 * p + 1) * P:(2 * p + 2) * P],
                                          start=True, stop=True)
                        else:
                            for c in range(2):
                                last = mm(ps[:, c * 2 * P:(c + 1) * 2 * P], a[ch, c * P:(c + 1) * P], a[ch, 2 * P:4 * P], start=True, stop=True)
                        if h == 0 and kind != "cross512":
                            fence(s, last)
                    last.then_inc(filled[misc], 1)
                elif kind == "wkv":
                    pe.wait_ge(emptied[MISC[0]], t.fill((0, "value"), MISC[0]))
                    pe.wait_ge(emptied[MISC[0]], t.fill((0, "level", len(HALVES) - 1), MISC[0]))
                    pe.wait_ge(emptied[MISC[0]], t.fill((0, "cross512", 1), MISC[0]))
                    ps = room(t, s, misc)
                    for q in range(NT):
                        for h in range(NH0):
                            o, clear = ps[:, q * P + HS * h:q * P + HS * h + HS], q == h == 0
                            vv = v0[:, :, HS * h:HS * h + HS]
                            far = [(p256[:, q // 2, h, :], vv[:, q - 1, :])] if q % 2 else []
                            if q >= 2:
                                far += [(p512[:, h, c, (q - 2) * P:(q - 1) * P], vv[:, c, :]) for c in range(2)]
                            for a, b in far:
                                mm(o, a, b, start=False, stop=False, skip_group_check=True)
                            mm(o[0:HS], pdiag[0:HS, q, h, :], vv[0:HS, q, :], start=clear, stop=True, skip_group_check=True)
                            last = mm(o[HS:P], p128[:, q, h, :], vv[0:HS, q, :], start=clear, stop=False, skip_group_check=True)
                    fence(s, last)
                    for q in range(NT):
                        for h in range(NH0):
                            last = mm(ps[HS:P, q * P + HS * h:q * P + HS * h + HS], pdiag[HS:P, q, h, :],
                                      v0[HS:P, q, HS * h:HS * h + HS], start=False, stop=True, skip_group_check=True)
                    last.then_inc(filled[misc], 1)
                elif kind == "wkvT":
                    pe.wait_ge(yn_done, 1)
                    transposes(room(t, s, misc), yn).then_inc(filled[misc], 1)
                elif kind == "finish":
                    if layer == 0:
                        pe.wait_ge(zT_done, 1)
                    else:
                        pe.wait_ge(emptied[MISC[1]], t.fill((1, "outT"), MISC[1]))
                    ps, src = room(t, s, misc), (zT, headsT_sb)[layer]
                    for q in range(NT):
                        last = mm(ps[:, q * P:(q + 1) * P], src[:, q * P:(q + 1) * P], sq[:, (WO, AO)[layer], :], start=True, stop=True)
                    last.then_inc(filled[misc], 1)
                elif kind == "qk":
                    mm(room(t, s, misc)[:], sq[:, s[2], :], xnT[1], start=True, stop=True).then_inc(filled[misc], 1)
                elif kind == "stack":
                    k = s[2] - AQ
                    pe.wait_ge(emptied[MISC[1]], t.fill((1, "qk", s[2]), MISC[1]))
                    ps = room(t, s, misc)
                    r = slice(32 * s[3], 32 * s[3] + 32)
                    mm(ps[:], select_sb[r, 2 * k, :], qk_hi[r, k, :], start=True, stop=False)
                    mm(ps[:], select_sb[r, 2 * k + 1, :], qk_lo[r, k, :], start=False, stop=True).then_inc(filled[misc], 1)
                elif kind == "smax":
                    h, q = s[2:]
                    g, r = h // HG, 32 * (h % HG)
                    if (h % HG, q) == (0, 0):
                        pe.wait_ge(emptied[MISC[1]], t.fill((1, "stack", AK, g), MISC[1]))
                    b = fills(s)[0]
                    mm(room(t, s, b)[:], qs[r:r + 32, g % RING, q * P:(q + 1) * P], ks[r:r + 32, g % RING, :],
                       start=True, stop=True).then_inc(filled[b], 1)
                elif kind == "mrow":
                    g = s[2]
                    last = (1, "smax", HG * g + HG - 1, NT - 1)
                    b = fills(last)[0]
                    pe.wait_ge(emptied[b], t.fill(last, b))
                    ps = room(t, s, misc)
                    for q in range(NT):
                        last = nc.tensor.transpose(ps[0:HG, q * P:(q + 1) * P], rowmax[:, g, q, :], ident_sb[:])
                    last.then_inc(filled[misc], 1)
                elif kind == "soft":
                    h, k = s[2:]
                    g, r = h // HG, 32 * (h % HG)
                    if (h % HG, k) == (0, 0):
                        pe.wait_ge(mrow_in, 32 * (g + 1))
                    b = fills(s)[0]
                    mm(room(t, s, b)[:], ks[r:r + 32, g % RING, k * P:(k + 1) * P], qs[r:r + 32, g % RING, :],
                       start=True, stop=True).then_inc(filled[b], 1)
                elif kind == "pv":
                    g, k = s[2:]
                    pe.wait_ge(emptied[MISC[1]], t.fill((1, "attnv"), MISC[1]))
                    last = (1, "soft", HG * g + HG - 1, k)
                    b = fills(last)[0]
                    pe.wait_ge(emptied[b], t.fill(last, b))
                    ps = room(t, s, VB) if k == 0 else bank[VB]
                    for j in range(HG):
                        last = mm(ps[32 * j:32 * j + 32, :], v1_all[:, k, (DK + 1) * (HG * g + j):(DK + 1) * (HG * g + j) + VCOLS], probs[:, k % 2, j, :],
                                  start=k == 0, stop=k == NT - 1, skip_group_check=True)
                    last.then_inc(pv_done, 1)
                elif kind == "headsT":
                    pe.wait_ge(emptied[VB], t.fill((1, "pv", s[2], 0), VB))
                    ps = room(t, s, misc)
                    for q in range(NT):
                        last = nc.tensor.transpose(ps[:, q * P:(q + 1) * P], oT[:, q * P:(q + 1) * P], ident_sb[:])
                    last.then_inc(filled[misc], 1)
                elif kind == "outT":
                    pe.wait_ge(emptied[MISC[1]], t.fill((1, "headsT", NG - 1), MISC[1]))
                    transposes(room(t, s, misc), heads).then_inc(filled[misc], 1)

            pe.wait_ge(s_load, 16 * len(loads))
            pe.wait_ge(s_set, NSET)
            pe.wait_ge(s_select, 2)
            turns(pe, "pe", step)

        @block.scalar
        def _(act):
            A = nc.scalar.activation

            def content(t, s, b, n=0):
                act.wait_ge(filled[b], t.fill(s, b, n))
                return bank[b]

            def step(t, s):
                layer, kind = s[:2]
                misc = MISC[layer]
                if t.first and kind == "mixin":
                    act.wait_ge(s_mix, 16 * len(mix_loads))
                if t.first and s == t.ups[0]:
                    act.wait_ge(s_up, 16 * len(up_loads))
                    for hi, whole in ((up_hi, up_ld), (gate_hi, gate_ld)):
                        A(hi[:], whole, ACT.Copy).then_inc(s_high, 1)
                if kind == "keep":
                    src, dst = ((x_next, x1), (x1, x1b))[layer]
                    if layer == 0 and (1, "keep") in t.steps:
                        act.wait_ge(kept[1], 1)
                    A(dst[:], src[:], ACT.Copy).then_inc(kept[layer], 1)
                elif kind == "normT":
                    if (layer, "up", E - 1, FT - 1) in t.steps:
                        act.wait_ge(filled[GB], t.fill((layer, "gate", E - 1, FT - 1), GB))
                        if layer == 0:
                            act.wait_ge(xmix_done, 5)
                        else:
                            act.wait_ge(emptied[misc], t.fill((1, "gates", E - 1), misc))
                    ps = content(t, s, misc)
                    if layer == 0:
                        A(xnT_hi[:], ps[:], ACT.Copy).then_inc(xhi_done, 1)
                        A(xnT[0], ps[:], ACT.Copy).then_inc(xhi_done, 1)
                    else:
                        A(xnT[1], ps[:], ACT.Copy).then_inc(emptied[misc], 1)
                elif kind == "route":
                    w, n = wtmp[layer], layer + 1
                    act.wait_ge(gate_pre[layer], 1)
                    A(w[:, 2:2 + n, :], w[:, 0:n, :], ACT.Exp).then_inc(gate_exp[layer], 1)
                elif kind == "gateT":
                    A(gw_hi[:], content(t, s, misc)[0:E, :], ACT.Copy).then_inc(gwhi_done, 1)
                elif kind == "up":
                    ba, gate = HB, (layer, "gate") + s[2:]
                    if t.fill(gate, GB) > FT:
                        act.wait_ge(emptied[GB], t.fill(gate, GB) - FT)
                    A(th[:, s[3], :], content(t, s, ba)[:], ACT.Tanh, scale=0.5).then_inc(th_done[layer], 1)
                elif kind == "mixed":
                    act.wait_ge(down_done[1], E + 1)
                    A(th_f[1], tiles(bank[YB]), ACT.Tanh, scale=0.25).then_inc(thf_done[1], 1)
                elif kind == "mixin":
                    A(mixa[:], content(t, s, misc)[:], ACT.Tanh).then_inc(emptied[misc], 1)
                    A(mixb, content(t, s, misc, 1)[0:32, :], ACT.Tanh).then_inc(emptied[misc], 1)
                elif kind == "decay":
                    A(dec_h, content(t, s, misc)[0:64, :], ACT.Tanh).then_inc(emptied[misc], 1)
                    A(elw[:], content(t, s, misc, 1)[:], ACT.Exp, bias=cols_sb[:, COL_DECAY:COL_DECAY + 1]).then_inc(emptied[misc], 1)
                elif kind == "proj":
                    if s[2] == WG:
                        A(gth[:], content(t, s, misc)[:], ACT.Tanh, scale=0.5).then_inc(gth_done, 1)
                    else:
                        A((rT if s[2] == WR else kT)[:], content(t, s, misc)[:], ACT.Copy).then_inc(emptied[misc], 1)
                elif kind == "value":
                    A(v0[:], tiles(content(t, s, misc)), ACT.Copy).then_inc(emptied[misc], 1)
                elif kind == "attnv":
                    A(v1[:, :, :, 0:DK], content(t, s, misc)[:].rearrange("p (q h k) -> p q h k", q=NT, h=NH),
                      ACT.Copy).then_inc(emptied[misc], 1)
                elif kind == "decays":
                    decays(t, s[2])
                elif kind == "cross128":
                    A(p128, content(t, s, misc)[0:HS, :].rearrange("p (q h c) -> p q h c", q=NT, h=NH0),
                      ACT.Copy).then_inc(emptied[misc], 1)
                elif kind == "cross256":
                    A(p256, content(t, s, misc)[:].rearrange("p (q h c) -> p q h c", q=2, h=NH0), ACT.Copy).then_inc(emptied[misc], 1)
                elif kind == "cross512":
                    A(p512[:, s[2]], content(t, s, misc)[:].rearrange("p (c n) -> p c n", c=2), ACT.Copy).then_inc(emptied[misc], 1)
                elif (layer, kind) == (0, "finish"):
                    act.wait_ge(acc_done, E - 1)
                    A(th_f[0], acc0[:], ACT.Tanh, scale=0.5).then_inc(thf_done[0], 1)
                elif kind == "qk":
                    k = s[2] - AQ
                    A(qk_hi[:, k, :], content(t, s, misc)[:], ACT.Copy, scale=QSCALE[k]).then_inc(qkhi_done, 1)
                elif kind == "stack":
                    ps = content(t, s, misc)
                    if s[3] >= RING:
                        old = (1, "soft", HG * (s[3] - RING + 1) - 1, NT - 1)
                        b = fills(old)[0]
                        act.wait_ge(filled[b], t.fill(old, b))
                    if s[2] == AQ:
                        A(qs[:, s[3] % RING, :], ps[:], ACT.Copy).then_inc(emptied[misc], 1)
                    else:
                        A(ks[:, s[3] % RING, :], ps[:], ACT.Identity, bias=cols_sb[:, COL_KONE:COL_KONE + 1]).then_inc(emptied[misc], 1)
                elif kind == "mrow":
                    ps = content(t, s, misc)
                    if s[2] > 0:
                        act.wait_ge(mrow_in, 32 * s[2])
                    A(m_hi[:], ps[0:HG, :], ACT.Copy, scale=-1.0).then_inc(mhi_done, 1)
                elif kind == "soft":
                    h, k = s[2:]
                    b = fills(s)[0]
                    ps = content(t, s, b)
                    if h % HG == 0 and h // HG * NT + k >= 2:
                        act.wait_ge(pv_done, h // HG * NT + k - 1)
                    A(probs[:, k % 2, h % HG, :], ps[:], ACT.Exp).then_inc(emptied[b], 1)
                elif kind == "pv" and s[3] == NT - 1:
                    g = s[2]
                    if g > 0:
                        act.wait_ge(filled[misc], t.fill((1, "headsT", g - 1), misc))
                    act.wait_ge(pv_done, NT * (g + 1))
                    A(oT[:], bank[VB][:], ACT.Copy).then_inc(emptied[VB], 1)
                elif kind == "outT":
                    A(headsT_sb[:], content(t, s, misc)[:], ACT.Copy).then_inc(emptied[misc], 1)

            def decays(t, n):
                if n == 1:
                    act.wait_ge(filled[MISC[0]], t.fill((0, "diag"), MISC[0]))
                if n >= 2:
                    act.wait_ge(rk_done, n - 1)
                e = expd[:, n % 2, :].rearrange("p (q c) -> p q c", q=NT)
                if n <= LEVEL["cross128"]:
                    act.wait_ge(diff_done, 2 * n + 2)
                    A(expd[:, n % 2, :], diff[:, n % 2, :], ACT.Exp).then_inc(expd_done, 1)
                elif n == LEVEL["cross256"]:
                    act.wait_ge(cum_done, NT)
                    A(e[:, 1::2, :], cum[:, 1::2, 0:P], ACT.Exp).then_inc(expd_done, 1)
                    for q in (0, 2):
                        A(e[:, q, :], cum[:, q, 1:P + 1], ACT.Exp, bias=cum[:, q, P:P + 1], scale=-1.0).then_inc(expd_done, 1)
                else:
                    act.wait_ge(tot_done, 1)
                    A(e[:, 2, :], cum[:, 2, 0:P], ACT.Exp).then_inc(expd_done, 1)
                    A(e[:, 3, :], cum[:, 3, 0:P], ACT.Exp, bias=cum[:, 2, P:P + 1]).then_inc(expd_done, 1)
                    A(e[:, 1, :], cum[:, 1, 1:P + 1], ACT.Exp, bias=cum[:, 1, P:P + 1], scale=-1.0).then_inc(expd_done, 1)
                    A(e[:, 0, :], cum[:, 0, 1:P + 1], ACT.Exp, bias=tot01[:], scale=-1.0).then_inc(expd_done, 1)

            act.wait_ge(s_load, 16 * len(loads))
            A(select_sb[:], select_ld, ACT.Copy).then_inc(s_select, 1)
            A(unit_sb[:], ident_sb[0:E, 0:E], ACT.Copy).then_inc(s_select, 1)
            act.wait_ge(s_set, NSET)
            turns(act, "act", step)

        @block.gpsimd
        def _(pool):
            tt = nc.gpsimd.tensor_tensor

            def step(t, s):
                layer, kind = s[:2]
                misc = MISC[layer]
                if kind == "norm":
                    pool.wait_ge(st_done[layer], 2 * NT + 1)
                    tt(rstd[layer][:], vareps[layer][:], power_sb[:, 0:NT], ALU.pow).then_inc(rstd_done[layer], 1)
                elif kind == "mixin":
                    tt(shiftT[:], xnT0[:, 0:T], xnT[0], ALU.subtract).then_inc(shift_done, 1)
                elif kind == "lora":
                    m = s[2]
                    pool.wait_ge(emptied[misc], t.fill(s, misc))
                    n = lora_no(m)
                    if n >= 3:
                        user = {MIX_W: (0, "decay"), MIX_K: (0, "proj", WK)}[loras[n - 3]]
                        pool.wait_ge(filled[MISC[0]], t.fill(user, MISC[0]))
                    tt(xmixT[:, n % 3, :], moved[:, n % 2, :], xnT[0], ALU.add).then_inc(xmix_done, 1)
                elif kind == "decays" and s[2] <= LEVEL["cross128"]:
                    if s[2] == 0:
                        differences(t, 0)
                    differences(t, s[2] + 1)
                    decayed(t, s[2])
                elif kind == "decays" and s[2] == LEVEL["cross256"]:
                    n = s[2]
                    pool.wait_ge(expd_done, n + 3)
                    pool.wait_ge(filled[MISC[0]], t.fill(level_step(n - 2), MISC[0]))
                    for k, src in ((0, kT), (1, rT)):
                        a, b, c = (v.rearrange("p (m k c) -> p m k c", m=2, k=2)[:, :, k, :] for v in (rk[:, n % 2, :], src[:], expd[:, n % 2, :]))
                        last = tt(a, b, c, ALU.mult)
                        if k == 0:
                            last.then_inc(rk_half, 1)
                    last.then_inc(rk_done, 1)
                elif kind == "decays":
                    n = s[2]
                    pool.wait_ge(expd_done, n + 6)
                    pool.wait_ge(filled[MISC[0]], t.fill(level_step(n - 2), MISC[0]))
                    tt(rk[:, n % 2, 0:2 * P], kT[:, 0:2 * P], expd[:, n % 2, 0:2 * P], ALU.mult).then_inc(rk_half, 1)
                    tt(rk[:, n % 2, 2 * P:T], rT[:, 2 * P:T], expd[:, n % 2, 2 * P:T], ALU.mult).then_inc(rk_done, 1)
                elif kind == "wkv":
                    pool.wait_ge(gst_done, 2 * NT * NH0 + 1)
                    tt(grstd[:], gvar[:], power_sb[:], ALU.pow).then_inc(grstd_done, 1)
                elif (layer, kind) == (0, "down"):
                    n = down_no(s)
                    if 0 < n < E - 1:
                        pool.wait_ge(emptied[YB], t.fill(s, YB))
                        if n > 1:
                            pool.wait_ge(acc_done, n - 1)
                        tt(acc0[:], acc0[:], ytmp[:, n % 2], ALU.add).then_inc(acc_done, 1)

            def differences(t, n):
                if n > len(HALVES):
                    return
                hs = (HALVES + (HS,))[n]
                if n == 0:
                    pool.wait_ge(cum_done, NT)
                    pool.wait_ge(xmix_done, 5)
                if n >= 2:
                    pool.wait_ge(expd_done, n - 1)
                shape = [P, NT, P // (2 * hs), hs]
                before, upto = (cum[:, :, o:o + P].rearrange("p q (n a s) -> p q n a s", a=2, s=hs) for o in (0, 1))
                d = diff[:, n % 2, :].rearrange("p (q n a s) -> p q n a s", q=NT, a=2, s=hs)
                middle = before[:, :, :, 1, 0:1].to_broadcast(shape)
                tt(d[:, :, :, 0, :], middle, upto[:, :, :, 0, :], ALU.subtract).then_inc(diff_done, 1)
                tt(d[:, :, :, 1, :], before[:, :, :, 1, :], middle, ALU.subtract).then_inc(diff_done, 1)

            def decayed(t, n):
                hs = (HALVES + (HS,))[n]
                pool.wait_ge(expd_done, n + 1)
                if n == 0:
                    pool.wait_ge(emptied[MISC[0]], t.fill((0, "proj", WR), MISC[0]))
                    pool.wait_ge(emptied[MISC[0]], t.fill((0, "proj", WK), MISC[0]))
                if n >= 2:
                    pool.wait_ge(filled[MISC[0]], t.fill(level_step(n - 2), MISC[0]))
                for k, src, done in ((0, kT, rk_half), (1, rT, rk_done)):
                    a, b, c = (v.rearrange("p (m a s) -> p m a s", a=2, s=hs)[:, :, k, :] for v in (rk[:, n % 2, :], src[:], expd[:, n % 2, :]))
                    tt(a, b, c, ALU.mult).then_inc(done, 1)

            pool.wait_ge(s_load, 16 * len(loads))
            pool.wait_ge(s_set, NSET)
            turns(pool, "pool", step)

        @block.vector
        def _(dve):
            v = nc.vector
            v.memset(ones_sb[:], 1.0).then_inc(s_set, 1)
            v.memset(power_sb[:], -0.5).then_inc(s_set, 1)
            v.memset(xnT0[:, 0:1], 0.0).then_inc(s_set, 1)
            v.memset(cum[:, :, 0:1], 0.0).then_inc(s_set, 1)
            v.memset(v1_all[:], 0.0).then_inc(s_set, 1)
            dve.wait_ge(s_set, 5)
            v.memset(v1[:, :, :, DK:DK + 1], 1.0).then_inc(s_set, 1)

            def content(t, s, b, n=0):
                dve.wait_ge(filled[b], t.fill(s, b, n))
                return bank[b]

            def col(n):
                return cols_sb[:, n:n + 1]

            def row_mean_var(t, src, layer):
                sig = st_done[layer]
                for q in range(NT):
                    v.bn_stats(stats[layer][:, q, :], src[:, q, :]).then_inc(sig, 1)
                for q in range(NT):
                    dve.wait_ge(sig, q + 1)
                    v.bn_aggr(moments[layer][:, q, :], stats[layer][:, q, :]).then_inc(sig, 1)
                dve.wait_ge(sig, 2 * NT)
                v.tensor_scalar(vareps[layer][:], moments[layer][:, :, 1], LN_EPS, None, ALU.add).then_inc(sig, 1)

            def step(t, s):
                layer, kind = s[:2]
                misc = MISC[layer]
                if t.first and kind == "mixin":
                    dve.wait_ge(s_mix, 16 * len(mix_loads))
                if t.first and s == t.ups[0]:
                    for n, (hi, lo, whole) in enumerate(((up_hi, up_lo, up_ld), (gate_hi, gate_lo, gate_ld))):
                        dve.wait_ge(s_high, n + 1)
                        v.tensor_tensor(lo[:], whole, hi[:].bitcast(F32), ALU.subtract).then_inc(s_split, 1)
                if kind == "norm":
                    dve.wait_ge(*((x_in, 16), (x1_done, 1))[layer])
                    src = (x_next, x1)[layer]
                    row_mean_var(t, src, layer)
                    dve.wait_ge(rstd_done[layer], 1)
                    if (0, "wkvT") in t.steps and layer == 0:
                        dve.wait_ge(filled[misc], t.fill((0, "wkvT"), misc))
                    for q in range(NT):
                        v.tensor_scalar(xn[layer][:, q, :], src[:, q, :], moments[layer][:, q, 0:1], rstd[layer][:, q:q + 1],
                                        ALU.subtract, ALU.mult).then_inc(xn_done[layer], 1)
                elif kind == "normT" and layer == 0:
                    dve.wait_ge(xhi_done, 2)
                    v.tensor_tensor(xnT_lo[:], bank[misc][:], xnT_hi[:].bitcast(F32), ALU.subtract).then_inc(emptied[misc], 1)
                elif kind == "route":
                    route(t, s)
                elif kind == "gateT":
                    dve.wait_ge(gwhi_done, 1)
                    v.tensor_tensor(gw_lo[:], bank[misc][0:E, :], gw_hi[:].bitcast(F32), ALU.subtract).then_inc(emptied[misc], 1)
                elif kind == "gates":
                    e = s[2]
                    ps = content(t, s, misc)
                    if e >= 2:
                        dve.wait_ge(filled[GB], t.fill((1, "gate", e - 2, FT - 1), GB))
                    v.tensor_tensor(xg[:, e % 2, :], ps[:], xnT[1], ALU.mult).then_inc(emptied[misc], 1)
                elif kind == "up":
                    dve.wait_ge(th_done[layer], up_no(s) + 1)
                    v.scalar_tensor_tensor(out=th[:, s[3], :], in0=th[:, s[3], :], scalar=1.0, in1=bank[HB][:],
                                           op0=ALU.add, op1=ALU.mult).then_inc(emptied[HB], 1)
                elif kind == "gate":
                    up = (layer, "up") + s[2:]
                    no = t.ups.index(up)
                    ps = content(t, s, GB)
                    if no >= 4:
                        old = t.ups[no - 4]
                        dve.wait_ge(down_done[old[0]], down_no(old) + 1)
                    dve.wait_ge(emptied[HB], t.fill(up, HB))
                    v.tensor_tensor(hid[:, hid_slot(up), :], th[:, s[3], :], ps[:], ALU.mult).then_inc(emptied[GB], 1)
                elif (layer, kind) == (0, "down"):
                    e, n = s[2], down_no(s)
                    dve.wait_ge(down_done[0], n + 1)
                    if n >= 3:
                        dve.wait_ge(acc_done, n - 2)
                    v.tensor_tensor(acc0[:] if n == 0 else ytmp[:, n % 2], bank[YB][:].rearrange("p (q c) -> p q c", q=NT),
                                    gatew[0][:, :, e:e + 1].to_broadcast([P, NT, C]), ALU.mult).then_inc(emptied[YB], 1)
                    if n == E - 1:
                        dve.wait_ge(emptied[YB], t.fill(s, YB))
                        dve.wait_ge(acc_done, n - 1)
                        v.tensor_tensor(acc0[:], acc0[:], ytmp[:, n % 2], ALU.add).then_inc(acc_done, 1)
                elif kind == "mixed":
                    dve.wait_ge(thf_done[1], 1)
                    v.scalar_tensor_tensor(out=q1[1], in0=th_f[1], scalar=1.0, in1=bank[YB][:].rearrange("p (q c) -> p q c", q=NT),
                                           op0=ALU.add, op1=ALU.mult).then_inc(emptied[YB], 1)
                elif kind == "mixin":
                    dve.wait_ge(shift_done, 1)
                    v.scalar_tensor_tensor(out=xxxT[:], in0=shiftT[:], scalar=col(COL_X), in1=xnT[0],
                                           op0=ALU.mult, op1=ALU.add).then_inc(xxx_done, 1)
                elif kind == "lora":
                    m = s[2]
                    n = lora_no(m)
                    ps = content(t, s, misc)
                    if n >= 2:
                        dve.wait_ge(xmix_done, n - 1)
                    v.scalar_tensor_tensor(out=moved[:, n % 2, :], in0=ps[:], scalar=col(COL_MIX + m), in1=shiftT[:],
                                           op0=ALU.add, op1=ALU.mult).then_inc(emptied[misc], 1)
                elif kind == "decay":
                    dve.wait_ge(emptied[misc], t.fill(s, misc, 1))
                    v.tensor_scalar(elwc[:], elw[:], DECAY_MAX, None, ALU.min).then_inc(elwc_done, 1)
                    dve.wait_ge(elwc_done, 1)
                    for q in range(NT):
                        v.tensor_tensor_scan(cum[:, q, 1:P + 1], ones_sb[:].to_broadcast([P, P]), elwc[:, q * P:(q + 1) * P], 0.0,
                                             ALU.mult, ALU.subtract).then_inc(cum_done, 1)
                    dve.wait_ge(cum_done, NT)
                    v.tensor_tensor(tot01[:], cum[:, 0, P:P + 1], cum[:, 1, P:P + 1], ALU.add).then_inc(tot_done, 1)
                elif kind == "proj":
                    if s[2] == WR:
                        dve.wait_ge(emptied[misc], t.fill(s, misc))
                        v.tensor_scalar(urT, rT[:], col(COL_U), None, ALU.mult).then_inc(ur_done, 1)
                    elif s[2] == WG:
                        dve.wait_ge(gth_done, 1)
                        v.scalar_tensor_tensor(out=gT[:], in0=gth[:], scalar=1.0, in1=bank[misc][:],
                                               op0=ALU.add, op1=ALU.mult).then_inc(emptied[misc], 1)
                elif kind in ("diag", "pair", "level"):
                    n = {"diag": 0, "pair": 1}.get(kind, 2 + s[2] if kind == "level" else 0)
                    ps = content(t, s, misc)[:].rearrange("p (m c) -> p m c", c=HS)
                    mask = masks_sb[:, n:n + 1, :].to_broadcast([P, NT * NH0, HS])
                    dst = pdiag.rearrange("p q h c -> p (q h) c")
                    if n == 0:
                        v.tensor_tensor(dst, ps, mask, ALU.mult).then_inc(emptied[misc], 1)
                    else:
                        dve.wait_ge(emptied[MISC[0]], t.fill(level_step(n - 3), MISC[0]))
                        v.copy_predicated(dst, mask.bitcast(I32), ps).then_inc(emptied[misc], 1)
                elif kind == "wkv":
                    ps = content(t, s, misc)[:].rearrange("p (m c) -> p m c", c=HS)
                    n = NT * NH0
                    for m in range(n):
                        v.bn_stats(gstats[:, m, :], ps[:, m, :]).then_inc(gst_done, 1)
                    for m in range(n):
                        dve.wait_ge(gst_done, m + 1)
                        v.bn_aggr(gmom[:, m, :], gstats[:, m, :]).then_inc(gst_done, 1)
                    dve.wait_ge(gst_done, 2 * n)
                    v.tensor_scalar(gvar[:], gmom[:, :, 1], GN_EPS, None, ALU.add).then_inc(gst_done, 1)
                    v.tensor_tensor(yn[:].rearrange("p q (h c) -> p (q h) c", c=HS), ps, gmom[:, :, 0:1].to_broadcast([P, n, HS]),
                                    ALU.subtract).then_inc(emptied[misc], 1)
                    dve.wait_ge(emptied[misc], t.fill(s, misc))
                    dve.wait_ge(grstd_done, 1)
                    v.tensor_tensor(yn[:].rearrange("p q (h c) -> p (q h) c", c=HS), yn[:].rearrange("p q (h c) -> p (q h) c", c=HS),
                                    grstd[:].unsqueeze(2).to_broadcast([P, n, HS]), ALU.mult).then_inc(yn_done, 1)
                elif kind == "wkvT":
                    v.tensor_scalar(ynT[:], content(t, s, misc)[:], col(COL_LNW), col(COL_LNB), ALU.mult, ALU.add).then_inc(emptied[misc], 1)
                    dve.wait_ge(emptied[misc], t.fill(s, misc))
                    v.scalar_tensor_tensor(out=zT[:], in0=gT[:], scalar=0.5, in1=ynT[:], op0=ALU.mult, op1=ALU.mult).then_inc(zT_done, 1)
                elif kind == "finish":
                    if layer == 0:
                        dve.wait_ge(thf_done[0], 1)
                        v.scalar_tensor_tensor(out=q1[0], in0=th_f[0], scalar=1.0, in1=acc0[:],
                                               op0=ALU.add, op1=ALU.mult).then_inc(q1_done, 1)
                        dve.wait_ge(q1_done, 1)
                    else:
                        dve.wait_ge(emptied[YB], t.fill((1, "down", E - 1), YB))
                    v.scalar_tensor_tensor(out=q2[layer], in0=q1[layer], scalar=(0.5, 0.25)[layer],
                                           in1=content(t, s, misc)[:].rearrange("p (q c) -> p q c", q=NT),
                                           op0=ALU.mult, op1=ALU.mult).then_inc(emptied[misc], 1)
                    dve.wait_ge(emptied[misc], t.fill(s, misc))
                    dve.wait_ge(kept[layer], 1)
                    dst, src, done = ((x1, x1, x1_done), (out_sb, x1b, out_ready))[layer]
                    v.tensor_tensor(dst[:], src[:], q2[layer], ALU.add).then_inc(done, 1)
                elif kind == "qk":
                    k = s[2] - AQ
                    dve.wait_ge(qkhi_done, k + 1)
                    v.scalar_tensor_tensor(out=qk_lo[:, k, :], in0=bank[misc][:], scalar=QSCALE[k], in1=qk_hi[:, k, :].bitcast(F32),
                                           op0=ALU.mult, op1=ALU.subtract).then_inc(emptied[misc], 1)
                elif kind == "smax":
                    h, q = s[2:]
                    b = fills(s)[0]
                    v.reduce_max(rowmax[:, h // HG, q, h % HG:h % HG + 1], content(t, s, b)[:], AX).then_inc(emptied[b], 1)
                elif kind == "mrow":
                    dve.wait_ge(mhi_done, s[2] + 1)
                    v.scalar_tensor_tensor(out=m_lo[:], in0=bank[misc][0:HG, :], scalar=-1.0, in1=m_hi[:].bitcast(F32),
                                           op0=ALU.mult, op1=ALU.subtract).then_inc(emptied[misc], 1)
                elif kind == "headsT":
                    g = s[2]
                    ps = content(t, s, misc)[:].rearrange("p (q j c) -> p q j c", q=NT, j=HG)
                    if g == 0:
                        dve.wait_ge(out_free, 1)
                    v.reciprocal(rden[:], ps[:, :, :, DK]).then_inc(rden_done, 1)
                    dve.wait_ge(rden_done, g + 1)
                    v.tensor_tensor(heads[:, :, 32 * g:32 * g + 32].rearrange("p q (j c) -> p q j c", j=HG), ps[:, :, :, 0:DK],
                                    rden[:].unsqueeze(3).to_broadcast([P, NT, HG, DK]), ALU.mult).then_inc(emptied[misc], 1)

            def route(t, s):
                layer, misc = s[0], MISC[s[0]]
                sc, w, sig = scores_sb[layer], wtmp[layer], gate_math[layer]
                v.tensor_copy(sc[:], content(t, s, misc)[:, 0:NT * E].rearrange("p (q e) -> p q e", q=NT)).then_inc(emptied[misc], 1)
                dve.wait_ge(emptied[misc], t.fill(s, misc, 0))
                tops = top_done[layer]
                for q in range(NT):
                    v.max(top[layer][:, q, :], sc[:, q, :]).then_inc(tops, 1)
                dve.wait_ge(tops, NT)
                if layer == 0:
                    v.tensor_tensor(w[:, 0, :], top[0][:, :, 1], top[0][:, :, 0], ALU.subtract).then_inc(gate_pre[0], 1)
                else:
                    v.tensor_scalar(w[:, 0:2, :], top[1][:, :, 0:2].rearrange("p q k -> p k q"), -1.0, None, ALU.mult).then_inc(gate_pre[1], 1)
                for q in range(NT):
                    v.max_index(topi[layer][:, q, :], top[layer][:, q, :], sc[:, q, :]).then_inc(tops, 1)
                dve.wait_ge(tops, 2 * NT)
                shape = [P, NT, E]
                experts = iota_sb[:].unsqueeze(1).to_broadcast(shape)
                for k in range(2):
                    v.tensor_tensor(pick_sb[layer][:, k], experts, topi[layer][:, :, k:k + 1].to_broadcast(shape),
                                    ALU.is_equal).then_inc(picked[layer], 1)
                dve.wait_ge(gate_exp[layer], 1)
                if layer == 0:
                    v.tensor_scalar(w[:, 3, :], w[:, 2, :], 1.0, None, ALU.add).then_inc(sig, 1)
                    dve.wait_ge(sig, 1)
                    v.reciprocal(w[:, 4, :], w[:, 3, :]).then_inc(sig, 1)
                    dve.wait_ge(sig, 2)
                    v.tensor_scalar(w[:, 4, :], w[:, 4, :], 0.5, None, ALU.mult).then_inc(sig, 1)
                    dve.wait_ge(sig, 3)
                    v.tensor_tensor(w[:, 5, :], w[:, 2, :], w[:, 4, :], ALU.mult).then_inc(sig, 1)
                else:
                    v.tensor_scalar(w[:, 2:4, :], w[:, 2:4, :], 1.0, None, ALU.add).then_inc(sig, 1)
                    dve.wait_ge(sig, 1)
                    v.reciprocal(w[:, 4:6, :], w[:, 2:4, :]).then_inc(sig, 1)
                n = 4 if layer == 0 else 2
                dve.wait_ge(sig, n)
                dve.wait_ge(picked[layer], 2)
                for k in range(2):
                    pick = pick_sb[layer][:, k]
                    v.tensor_tensor(pick, pick, w[:, 4 + k, :].unsqueeze(2).to_broadcast(shape), ALU.mult).then_inc(sig, 1)
                dve.wait_ge(sig, n + 2)
                v.tensor_tensor(gatew[layer][:], pick_sb[layer][:, 0], pick_sb[layer][:, 1], ALU.add).then_inc(gatew_done[layer], 1)

            turns(dve, "dve", step)


def _layout(a, np):
    f = lambda v: np.ascontiguousarray(v, dtype=np.float32)
    p = "L0_attn_"
    kone = np.zeros(P)
    for j in range(HG):
        kone[32 * j + 24:32 * j + 26] = 1.0
    cols = [a[p + f"time_maa_{n}"] for n in "xwkvrg"] + [a[p + "time_decay"], a[p + "time_faaaa"].reshape(C), a[p + "ln_w"], a[p + "ln_b"], kone]
    square = [a[p + n] for n in ("Wr", "Wk", "Wv", "Wg", "Wo")]
    square += [a[f"L1_attn_W_{n}"].transpose(1, 0, 2).reshape(C, C) for n in ("query", "key", "val")] + [a["L1_attn_W_out"].reshape(C, C)]
    w3 = a["L0_ffn_W3"].transpose(2, 0, 1).reshape(FT, P, E, C).transpose(1, 2, 0, 3)
    up1 = np.concatenate([a["L1_ffn_w_in_eDF"], a["L1_ffn_w_in_shared_FD"].T[None]]).transpose(1, 0, 2)
    gate1 = np.concatenate([a["L1_ffn_w_swiglu_eDF"], a["L1_ffn_w_swiglu_FD"].T[None]]).transpose(1, 0, 2)
    down1 = np.concatenate([a["L1_ffn_w_out_eFD"], a["L1_ffn_w_out_shared_DF"].T[None]]).reshape(E1, FT, P, C).transpose(2, 0, 1, 3)
    s, u = np.arange(HS)[:, None], np.arange(HS)[None, :]
    masks = [s == u]
    for hs in (1,) + HALVES:
        masks.append((s // (2 * hs) == u // (2 * hs)) & (s % (2 * hs) < hs) & (u % (2 * hs) >= hs))
    masks = np.tile(np.stack(masks, 1), (2, 1, 1))
    select = np.zeros((P, 4, P))
    for g in range(NG):
        for j in range(HG):
            for d in range(DK):
                row = (HG * g + j) * DK + d
                for n, parts in enumerate(((0, 2), (1,), (0, 1), (2,))):
                    for part in parts:
                        select[row, n, 32 * j + DK * part + d] = 1.0
    return {
        "x": f(a["L0_attn_x"]), "cols": f(np.stack(cols, 1)), "mix1": f(a[p + "time_maa_w1"]), "square": f(np.stack(square, 1)),
        "mix2": f(a[p + "time_maa_w2"].reshape(5 * 32, C)), "dec1": f(a[p + "time_decay_w1"]), "dec2": f(a[p + "time_decay_w2"]),
        "up0": f(a["L0_ffn_W1"].transpose(2, 0, 1)), "gate0": f(a["L0_ffn_W2"].transpose(2, 0, 1)), "down0": f(w3),
        "up1": f(up1), "gate1": f(gate1), "down1": f(down1),
        "routers": f(np.stack([a["L0_ffn_Wg"].T, a["L1_ffn_router_DE"]], 1)), "ident": f(np.eye(P)), "masks": f(masks),
        "select": f(select), "iota": f(np.tile(np.arange(E), (P, 1))),
    }


def kernel(**inputs):
    import numpy as np
    from concourse import bacc
    from concourse.bass_utils import run_bass_kernel_spmd

    nc = bacc.Bacc("TRN2", target_bir_lowering=False, num_devices=1)
    arrays = _layout({k: np.asarray(v) for k, v in inputs.items()}, np)
    args = [nc.dram_tensor(n, v.shape, F32, kind="ExternalInput").ap() for n, v in arrays.items()]
    out = nc.dram_tensor("out", (B, T, C), F32, kind="ExternalOutput").ap()
    two_layer_kernel(nc, *args, out)
    return run_bass_kernel_spmd(nc, [arrays], core_ids=[0]).results[0]["out"]
```
